# Optimizing a Trainium2 kernel written in Bass

```python
import numpy as np
import jax
import jax.numpy as jnp

def _softmax(x, axis=-1):
    return jax.nn.softmax(x, axis=axis)

def _gelu(x):
    return jax.nn.gelu(x, approximate=True)

def _silu(x):
    return jax.nn.silu(x)

def _sigmoid(x):
    return jax.nn.sigmoid(x)

def _layernorm(x, axis=-1, eps=1e-05):
    m = jnp.mean(x, axis=axis, keepdims=True)
    v = jnp.var(x, axis=axis, keepdims=True)
    return (x - m) / jnp.sqrt(v + eps)

def _scatter_add(tgt, idx, src, axis=0):
    return tgt.at[idx].add(src)

def _segment_sum(src, seg, n):
    return jax.ops.segment_sum(src, seg, n)
kernel_name = 'mk_flamingo_gated_d2_seqx_r8_4d34d0'

def setup_inputs(seed: int=0):
    np.random.seed(seed)
    _w = jnp.asarray

    def _rec_inputs():
        import jax
        import jax.numpy as jnp
        _rk = jax.random.key(seed)
        x = 7.22e-05 + 1 * jax.random.normal(jax.random.fold_in(_rk, 1), (32, 128, 128), jnp.float32)
        _lenS = 128 - jax.random.randint(jax.random.fold_in(_rk, 7), (32,), 0, max(1, 128 // 4) + 1, jnp.int32)
        _lenS2 = 77 - jax.random.randint(jax.random.fold_in(_rk, 8), (32,), 0, max(1, 77 // 4) + 1, jnp.int32)
        _ctx_1024P = jax.random.normal(jax.random.fold_in(_rk, 11), (32, 16, 128), jnp.float32)
        _ctx_1024c = jax.random.dirichlet(jax.random.fold_in(_rk, 511), 0.3 * jnp.ones((16,), jnp.float32), (32, 77))
        _ctx_1024t = jnp.einsum('bsk,bkd->bsd', _ctx_1024c, _ctx_1024P)
        _ctx_1024t = _ctx_1024t * jax.lax.rsqrt(jnp.mean(jnp.square(_ctx_1024t)) + 1e-12) * 0.953939
        ctx_1024 = 4.13588e-05 + 0.999923 * (_ctx_1024t + 0.3 * jax.random.normal(jax.random.fold_in(_rk, 611), (32, 77, 128), jnp.float32))
        _validS = jnp.arange(128)[None, :] < _lenS[:, None]
        _validS2 = jnp.arange(77)[None, :] < _lenS2[:, None]
        _causal = jnp.tril(jnp.ones((128, 128), dtype=bool))
        mask_BxS2_bf1 = jnp.ones((32, 77), dtype=bool)
        _g = jax.random.normal(jax.random.fold_in(_rk, 9001), (2, 2), jnp.float32)
        _g = jnp.sign(_g) * jnp.maximum(jnp.abs(_g), 1.0) + (_g == 0) * 1.0
        g_xattn = _g[0]
        g_ffn = _g[1]
        return (x, ctx_1024, mask_BxS2_bf1, g_xattn, g_ffn)
    x, ctx_1024, mask_BxS2_bf1, g_xattn, g_ffn = _rec_inputs()

    def _L0_xattn_setup():
        import jax, jax.numpy as jnp
        import numpy as np
        D_MODEL = 128
        H = 16
        D_K = D_MODEL // H
        key = jax.random.key(seed)
        ks = jax.random.split(key, 8)
        B, S = (4, 256)
        q = jax.random.normal(ks[0], (B, S, D_MODEL), dtype=jnp.float32)
        k = jax.random.normal(ks[1], (B, S, D_MODEL), dtype=jnp.float32)
        v = jax.random.normal(ks[2], (B, S, D_MODEL), dtype=jnp.float32)
        scale = 1.0 / np.sqrt(D_MODEL)
        W_q = jax.random.normal(ks[3], (H, D_MODEL, D_K), dtype=jnp.float32) * scale
        W_k = jax.random.normal(ks[4], (H, D_MODEL, D_K), dtype=jnp.float32) * scale
        W_v = jax.random.normal(ks[5], (H, D_MODEL, D_K), dtype=jnp.float32) * scale
        W_o = jax.random.normal(ks[6], (D_MODEL, H * D_K), dtype=jnp.float32) * scale
        b_o = jax.random.normal(ks[7], (D_MODEL,), dtype=jnp.float32) * 0.01
        return {'q': q, 'k': k, 'v': v, 'W_q': W_q, 'W_k': W_k, 'W_v': W_v, 'W_o': W_o, 'b_o': b_o}
    _L0_xattn_all = _L0_xattn_setup()
    _L0_xattn_in = {k: v for k, v in _L0_xattn_all.items() if k in ('W_q', 'W_k', 'W_v', 'W_o', 'b_o')}
    del _L0_xattn_all

    def _L0_ffn_setup():
        import jax, jax.numpy as jnp
        import numpy as np
        B, S, D_MODEL, D_HIDDEN = (4, 256, 128, 512)

        def act_quant(x):
            scale = 127.0 / jnp.clip(jnp.max(jnp.abs(x), axis=-1, keepdims=True), 1e-05)
            return jnp.clip(jnp.round(x * scale), -128, 127) / scale

        def weight_quant(w):
            scale = 1.0 / jnp.clip(jnp.mean(jnp.abs(w)), 1e-05)
            return jnp.clip(jnp.round(w * scale), -1, 1) / scale

        def bit_linear(x, w):
            xq = x + jax.lax.stop_gradient(act_quant(x) - x)
            wq = w + jax.lax.stop_gradient(weight_quant(w) - w)
            return jnp.einsum('bsd,hd->bsh', xq, wq)

        def depthwise_conv1d(x_bcl, w, b):
            y = jax.lax.conv_general_dilated(x_bcl, w, window_strides=(1,), padding=[(1, 1)], dimension_numbers=('NCH', 'OIH', 'NCH'), feature_group_count=x_bcl.shape[1])
            return y + b[None, :, None]
        key = jax.random.key(seed)
        ks = jax.random.split(key, 5)
        lim1 = 1.0 / np.sqrt(D_MODEL)
        lim2 = 1.0 / np.sqrt(D_HIDDEN)
        limc = 1.0 / np.sqrt(3.0)
        return {'x': jax.random.normal(ks[0], (B, S, D_MODEL), dtype=jnp.float32), 'w1': jax.random.uniform(ks[1], (D_HIDDEN, D_MODEL), jnp.float32, -lim1, lim1), 'conv_w': jax.random.uniform(ks[2], (D_HIDDEN, 1, 3), jnp.float32, -limc, limc), 'conv_b': jax.random.uniform(ks[3], (D_HIDDEN,), jnp.float32, -limc, limc), 'w2': jax.random.uniform(ks[4], (D_MODEL, D_HIDDEN), jnp.float32, -lim2, lim2)}
    _L0_ffn_all = _L0_ffn_setup()
    _L0_ffn_in = {k: v for k, v in _L0_ffn_all.items() if k in ('w1', 'conv_w', 'conv_b', 'w2')}
    del _L0_ffn_all

    def _L1_xattn_setup():
        import jax, jax.numpy as jnp
        import numpy as np
        DIM = 128
        HEADS = 16
        DIM_HEAD = 64
        INNER = HEADS * DIM_HEAD
        EPS = 1e-05

        def layer_norm(x, gamma, beta):
            mu = jnp.mean(x, axis=-1, keepdims=True)
            var = jnp.var(x, axis=-1, keepdims=True)
            return (x - mu) * jax.lax.rsqrt(var + EPS) * gamma + beta
        key = jax.random.key(seed)
        ks = jax.random.split(key, 8)
        b, n, m = (8, 512, 64)
        x = jax.random.normal(ks[0], (b, n, DIM), dtype=jnp.float32)
        latents = jax.random.normal(ks[1], (b, m, DIM), dtype=jnp.float32)
        mask = jnp.ones((b, n), dtype=bool)
        s = 0.02
        Wq = jax.random.normal(ks[2], (DIM, INNER), dtype=jnp.float32) * s
        Wkv = jax.random.normal(ks[3], (DIM, 2 * INNER), dtype=jnp.float32) * s
        Wout = jax.random.normal(ks[4], (INNER, DIM), dtype=jnp.float32) * s
        g_x = jnp.ones((DIM,), jnp.float32)
        b_x = jnp.zeros((DIM,), jnp.float32)
        g_l = jnp.ones((DIM,), jnp.float32)
        b_l = jnp.zeros((DIM,), jnp.float32)
        g_o = jnp.ones((DIM,), jnp.float32)
        b_o = jnp.zeros((DIM,), jnp.float32)
        return {'x': x, 'latents': latents, 'mask': mask, 'g_x': g_x, 'b_x': b_x, 'g_l': g_l, 'b_l': b_l, 'Wq': Wq, 'Wkv': Wkv, 'Wout': Wout, 'g_o': g_o, 'b_o': b_o}
    _L1_xattn_all = _L1_xattn_setup()
    _L1_xattn_in = {k: v for k, v in _L1_xattn_all.items() if k in ('g_x', 'b_x', 'g_l', 'b_l', 'Wq', 'Wkv', 'Wout', 'g_o', 'b_o')}
    del _L1_xattn_all

    def _L1_ffn_setup():
        import jax, jax.numpy as jnp
        import numpy as np
        B, S, D = (4, 128, 128)
        E, K = (8, 2)
        H = 2 * D
        key = jax.random.key(seed)
        ks = jax.random.split(key, 5)
        x = jax.random.normal(ks[0], (B, S, D), dtype=jnp.float32)
        Wg = jax.random.normal(ks[1], (E, D), dtype=jnp.float32) * 0.02
        W1 = jax.random.normal(ks[2], (E, H, D), dtype=jnp.float32) * 0.02
        W2 = jax.random.normal(ks[3], (E, H, D), dtype=jnp.float32) * 0.02
        W3 = jax.random.normal(ks[4], (E, D, H), dtype=jnp.float32) * 0.02
        return {'x': x, 'Wg': Wg, 'W1': W1, 'W2': W2, 'W3': W3}
    _L1_ffn_all = _L1_ffn_setup()
    _L1_ffn_in = {k: v for k, v in _L1_ffn_all.items() if k in ('Wg', 'W1', 'W2', 'W3')}
    del _L1_ffn_all
    return {'x': x, 'ctx_1024': ctx_1024, 'mask_BxS2_bf1': mask_BxS2_bf1, 'g_xattn': g_xattn, 'g_ffn': g_ffn, 'L0_xattn_W_q': _L0_xattn_in['W_q'], 'L0_xattn_W_k': _L0_xattn_in['W_k'], 'L0_xattn_W_v': _L0_xattn_in['W_v'], 'L0_xattn_W_o': _L0_xattn_in['W_o'], 'L0_xattn_b_o': _L0_xattn_in['b_o'], 'L0_ffn_w1': _L0_ffn_in['w1'], 'L0_ffn_conv_w': _L0_ffn_in['conv_w'], 'L0_ffn_conv_b': _L0_ffn_in['conv_b'], 'L0_ffn_w2': _L0_ffn_in['w2'], 'L1_xattn_g_x': _L1_xattn_in['g_x'], 'L1_xattn_b_x': _L1_xattn_in['b_x'], 'L1_xattn_g_l': _L1_xattn_in['g_l'], 'L1_xattn_b_l': _L1_xattn_in['b_l'], 'L1_xattn_Wq': _L1_xattn_in['Wq'], 'L1_xattn_Wkv': _L1_xattn_in['Wkv'], 'L1_xattn_Wout': _L1_xattn_in['Wout'], 'L1_xattn_g_o': _L1_xattn_in['g_o'], 'L1_xattn_b_o': _L1_xattn_in['b_o'], 'L1_ffn_Wg': _L1_ffn_in['Wg'], 'L1_ffn_W1': _L1_ffn_in['W1'], 'L1_ffn_W2': _L1_ffn_in['W2'], 'L1_ffn_W3': _L1_ffn_in['W3']}

def reference(x, ctx_1024, mask_BxS2_bf1, g_xattn, g_ffn, L0_xattn_W_q, L0_xattn_W_k, L0_xattn_W_v, L0_xattn_W_o, L0_xattn_b_o, L0_ffn_w1, L0_ffn_conv_w, L0_ffn_conv_b, L0_ffn_w2, L1_xattn_g_x, L1_xattn_b_x, L1_xattn_g_l, L1_xattn_b_l, L1_xattn_Wq, L1_xattn_Wkv, L1_xattn_Wout, L1_xattn_g_o, L1_xattn_b_o, L1_ffn_Wg, L1_ffn_W1, L1_ffn_W2, L1_ffn_W3):
    import jax
    import jax.numpy as jnp

    def _L0_xattn_ref(q, k, v, W_q, W_k, W_v, W_o, b_o):
        import jax, jax.numpy as jnp
        import numpy as np
        D_MODEL = 128
        H = 16
        D_K = D_MODEL // H
        qh = jnp.einsum('bsd,hdk->hbsk', q, W_q)
        kh = jnp.einsum('bsd,hdk->hbsk', k, W_k)
        vh = jnp.einsum('bsd,hdk->hbsk', v, W_v)
        scores = jnp.einsum('hbsk,hbtk->hbst', qh, kh) / jnp.sqrt(jnp.asarray(D_K, qh.dtype))
        attn = jax.nn.softmax(scores, axis=-1)
        out = jnp.einsum('hbst,hbtk->hbsk', attn, vh)
        out = jnp.transpose(out, (1, 2, 0, 3)).reshape(q.shape[0], q.shape[1], H * D_K)
        return out @ W_o.T + b_o

    def _L0_ffn_ref(x, w1, conv_w, conv_b, w2):
        import jax, jax.numpy as jnp
        import numpy as np
        B, S, D_MODEL, D_HIDDEN = (4, 256, 128, 512)

        def act_quant(x):
            scale = 127.0 / jnp.clip(jnp.max(jnp.abs(x), axis=-1, keepdims=True), 1e-05)
            return jnp.clip(jnp.round(x * scale), -128, 127) / scale

        def weight_quant(w):
            scale = 1.0 / jnp.clip(jnp.mean(jnp.abs(w)), 1e-05)
            return jnp.clip(jnp.round(w * scale), -1, 1) / scale

        def bit_linear(x, w):
            xq = x + jax.lax.stop_gradient(act_quant(x) - x)
            wq = w + jax.lax.stop_gradient(weight_quant(w) - w)
            return jnp.einsum('bsd,hd->bsh', xq, wq)

        def depthwise_conv1d(x_bcl, w, b):
            y = jax.lax.conv_general_dilated(x_bcl, w, window_strides=(1,), padding=[(1, 1)], dimension_numbers=('NCH', 'OIH', 'NCH'), feature_group_count=x_bcl.shape[1])
            return y + b[None, :, None]
        h = bit_linear(x, w1)
        h = depthwise_conv1d(h.transpose(0, 2, 1), conv_w, conv_b)
        h = h.transpose(0, 2, 1)
        h = jax.nn.silu(h)
        return bit_linear(h, w2)

    def _L1_xattn_ref(x, latents, mask, g_x, b_x, g_l, b_l, Wq, Wkv, Wout, g_o, b_o):
        import jax, jax.numpy as jnp
        import numpy as np
        DIM = 128
        HEADS = 16
        DIM_HEAD = 64
        INNER = HEADS * DIM_HEAD
        EPS = 1e-05

        def layer_norm(x, gamma, beta):
            mu = jnp.mean(x, axis=-1, keepdims=True)
            var = jnp.var(x, axis=-1, keepdims=True)
            return (x - mu) * jax.lax.rsqrt(var + EPS) * gamma + beta
        scale = DIM_HEAD ** (-0.5)
        xn = layer_norm(x, g_x, b_x)
        ln = layer_norm(latents, g_l, b_l)
        b, m = (ln.shape[0], ln.shape[1])
        q = jnp.einsum('bnd,de->bne', ln, Wq)
        kv_in = jnp.concatenate([xn, ln], axis=1)
        kv = jnp.einsum('bnd,de->bne', kv_in, Wkv)
        k, v = jnp.split(kv, 2, axis=-1)

        def split_heads(t):
            return t.reshape(t.shape[0], t.shape[1], HEADS, DIM_HEAD).transpose(0, 2, 1, 3)
        q, k, v = (split_heads(q), split_heads(k), split_heads(v))
        q = q * scale
        sim = jnp.einsum('bhid,bhjd->bhij', q, k)
        full_mask = jnp.concatenate([mask, jnp.ones((b, m), dtype=bool)], axis=1)
        max_neg = -jnp.finfo(sim.dtype).max
        sim = jnp.where(full_mask[:, None, None, :], sim, max_neg)
        attn = jax.nn.softmax(sim, axis=-1)
        out = jnp.einsum('bhij,bhjd->bhid', attn, v)
        out = out.transpose(0, 2, 1, 3).reshape(b, m, INNER)
        out = jnp.einsum('bne,ed->bnd', out, Wout)
        return layer_norm(out, g_o, b_o)

    def _L1_ffn_ref(x, Wg, W1, W2, W3):
        import jax, jax.numpy as jnp
        import numpy as np
        B, S, D = (4, 128, 128)
        E, K = (8, 2)
        H = 2 * D
        gate_out = jnp.einsum('bsd,ed->bse', x, Wg)
        top_v, top_i = jax.lax.top_k(gate_out, K)
        probs = jax.nn.softmax(top_v, axis=-1)
        out = jnp.zeros_like(x)
        for e in range(E):
            w_e = jnp.sum(probs * (top_i == e), axis=-1)
            h1 = jnp.einsum('bsd,hd->bsh', x, W1[e])
            h2 = jnp.einsum('bsd,hd->bsh', x, W2[e])
            g = h1 * jax.nn.sigmoid(h1) * h2
            y = jnp.einsum('bsh,dh->bsd', g, W3[e])
            out = out + y * w_e[..., None]
        return out
    x = x + jnp.tanh(g_xattn[0]) * _L0_xattn_ref(_layernorm(x, axis=-1), ctx_1024, ctx_1024, L0_xattn_W_q, L0_xattn_W_k, L0_xattn_W_v, L0_xattn_W_o, L0_xattn_b_o)
    x = x + jnp.tanh(g_ffn[0]) * _L0_ffn_ref(_layernorm(x, axis=-1), L0_ffn_w1, L0_ffn_conv_w, L0_ffn_conv_b, L0_ffn_w2)
    x = x + jnp.tanh(g_xattn[1]) * _L1_xattn_ref(ctx_1024, _layernorm(x, axis=-1), mask_BxS2_bf1, L1_xattn_g_x, L1_xattn_b_x, L1_xattn_g_l, L1_xattn_b_l, L1_xattn_Wq, L1_xattn_Wkv, L1_xattn_Wout, L1_xattn_g_o, L1_xattn_b_o)
    x = x + jnp.tanh(g_ffn[1]) * _L1_ffn_ref(_layernorm(x, axis=-1), L1_ffn_Wg, L1_ffn_W1, L1_ffn_W2, L1_ffn_W3)
    return x

_drawn_inputs = setup_inputs


def setup_inputs(seed=0):
    import zlib

    import numpy as np

    out = dict(_drawn_inputs(seed))
    spreads = {'g_ffn': (-1.0, 0.6),
     'L1_xattn_g_x': (1.0, 0.2),
     'L1_xattn_b_x': (0.0, 0.1),
     'L1_xattn_g_l': (1.0, 0.2),
     'L1_xattn_b_l': (0.0, 0.1),
     'L1_xattn_g_o': (1.0, 0.2),
     'L1_xattn_b_o': (0.0, 0.1)}
    factors = {'L0_xattn_b_o': 5.419,
     'L1_xattn_Wq': 3.126,
     'L1_ffn_Wg': 8.0,
     'L1_ffn_W1': 8.0,
     'L1_ffn_W2': 8.0,
     'L1_ffn_W3': 8.0}
    for name, (base, spread) in spreads.items():
        noise = np.random.default_rng([zlib.crc32(name.encode()), seed]).standard_normal(out[name].shape)
        drawn = base * np.exp(spread * noise) if base else spread * noise
        out[name] = jnp.asarray(drawn.astype(out[name].dtype))
    for name, factor in factors.items():
        out[name] = (out[name] * factor).astype(out[name].dtype)
    return out
```

```python
import concourse.bass as bass
from concourse import mybir
from contextlib import ExitStack

FP32 = mybir.dt.float32
FP16 = mybir.dt.float16
INT32 = mybir.dt.int32
UINT32 = mybir.dt.uint32
UINT8 = mybir.dt.uint8
ALU = mybir.AluOpType
ACT = mybir.ActivationFunctionType
AX = mybir.AxisListType

B, S, D = 32, 128, 128
C = 77
H = 16
DK0 = D // H
DK1 = 64
G = 4
HG = H // G
KV = S + C
HID = 512
M0 = HID // 128
E, MH = 8, 2
R0 = 3 * HG * DK0
CH = 4
NCH = B // CH
N = CH * S
EPS = 1e-5
ROUND = 1.5 * 2.0 ** 23
WS = 64.0
AS = 1024.0
MASKED = -30000.0


class Weights:
    pass


def late(x, least=1):
    return not isinstance(x, int) or x >= least


def rsqrt(dve, link, out, var, t1, t2, scale=1.0):
    link(dve.tensor_scalar(t1, var, scale, EPS, ALU.mult, ALU.add))
    link(dve.tensor_single_scalar(t2.bitcast(INT32), t1.bitcast(INT32), 1, ALU.arith_shift_right))
    link(dve.tensor_scalar(out.bitcast(INT32), t2.bitcast(INT32), -1.0, float(0x5F3759DF), ALU.mult, ALU.add))
    for _ in range(3):
        link(dve.scalar_tensor_tensor(t2, out, -0.5, out, ALU.mult, ALU.mult))
        link(dve.tensor_tensor(t2, t2, t1, ALU.mult))
        link(dve.scalar_tensor_tensor(out, t2, 1.5, out, ALU.add, ALU.mult))


RSQRT_LINKS = 12


def linker(eng, sem, base=0):
    n = [0]

    def link(ins):
        n[0] += 1
        ins.then_inc(sem, 1)
        eng.wait_ge(sem, base + n[0])
    return link


class Memory:

    def __init__(self, nc, tag):
        self.nc, self.tag, self.stack = nc, tag, ExitStack()

    def __enter__(self):
        return self

    def __exit__(self, *e):
        return self.stack.__exit__(*e)

    def sb(self, name, shape, dt=FP32):
        return self.stack.enter_context(self.nc.sbuf_tensor(f"{self.tag}_{name}", shape, dt))

    def sem(self, name):
        return self.stack.enter_context(self.nc.semaphore(f"{self.tag}_{name}"))

    def block(self):
        return self.stack.enter_context(self.nc.Block())


def setup(nc, a, w, bank):
    with Memory(nc, "setup") as m:
        nat_q0, nat_k0, nat_v0 = (m.sb(n, [128, D]) for n in ("nat_q0", "nat_k0", "nat_v0"))
        nat_o0 = m.sb("nat_o0", [128, 1, D])
        nat_f = m.sb("nat_f", [128, 2, HID])
        conv_w, conv_b = m.sb("conv_w", [128, M0, 3]), w.conv_b
        nat_q1, nat_k1, nat_v1 = (m.sb(n, [128, H * DK1]) for n in ("nat_q1", "nat_k1", "nat_v1"))
        nat_o1 = m.sb("nat_o1", [128, H // 2, D])
        nat_moe = m.sb("nat_moe", [128, 2, E * MH, D])
        nat_w3 = m.sb("nat_w3", [128, E * MH, D])
        nat_g = m.sb("nat_g", [E, 1, D])
        mask_u8, mask_f = m.sb("mask_u8", [B, C], UINT8), m.sb("mask_f", [B, 1, C])
        mask_rows = m.sb("mask_rows", [128, B * C], UINT8)
        gates, tanhs = m.sb("gates", [128, 4]), m.sb("tanhs", [128, 4])
        rows = m.sb("rows", [128, 3, D])
        bn = m.sb("bn", [128, B, 6])
        bn_c = m.sb("bn_c", [C, B, 6])
        absum, wmean, winv = m.sb("absum", [128, 2]), m.sb("wmean", [128, 2]), m.sb("winv", [128, 2])
        ones = m.sb("ones", [128, 128])
        cs = m.sb("cs", [128, M0, 3])
        tap_w = m.sb("tap_w", [128, 3, M0, D])
        q1t, k1t = m.sb("q1t", [128, H // 2, D]), m.sb("k1t", [128, H // 2, D])
        comp = m.sb("comp", [128, 4, D], FP16)
        t1, t2 = m.sb("t1", [128, B]), m.sb("t2", [128, B])
        iota_i = m.sb("iota_i", [128, E], INT32)

        x_in = [m.sem(f"x_in{i}") for i in range(4)]
        ctx_in, l0_in, ffn_in, l1_in, moe_in, small_in = (
            m.sem(n) for n in ("ctx_in", "l0_in", "ffn_in", "l1_in", "moe_in", "small_in"))
        made, tanh_done, summed, quant_done, chain, tiles_done, hi_done, lo_done, plain_hi, plain_lo, mask_done, pchain = (
            m.sem(n) for n in ("made", "tanh_done", "summed", "quant_done", "chain", "tiles_done", "hi_done",
                               "lo_done", "plain_hi", "plain_lo", "mask_done", "pchain"))
        block = m.block()

        LD_L1, LD_MOE, LD_SMALL, QUANT, TAPS = range(5)
        tiles = []
        for i in range(2):
            tiles.append((nat_q1[:, 512 * i:512 * i + 512].rearrange("p (t n) -> p t n", n=128), LD_L1,
                          q1t[:, 4 * i:4 * i + 4, :], None, 1.0))
            tiles.append((nat_k1[:, 512 * i:512 * i + 512].rearrange("p (t n) -> p t n", n=128), LD_L1,
                          k1t[:, 4 * i:4 * i + 4, :], None, 1.0))
        tiles.append((nat_o0[:], LD_L1, w.o0h[:], w.o0l[:], WS))
        tiles.append((nat_g[:], LD_SMALL, w.wgt[:, 0:1, :], w.wgt[:, 1:2, :], WS))
        tiles.append((mask_f[:], LD_SMALL, w.mask_bias[:], None, 1.0))
        for t in range(3):
            tiles.append((tap_w[:, t], TAPS, w.taph[:, t], w.tapl[:, t], WS))
        tiles.append((nat_f[:, 1].rearrange("p (t n) -> p t n", n=128), QUANT, w.w2t[:], None, 1.0))
        for s in range(2):
            for i in range(4):
                tiles.append((nat_moe[:, s, 4 * i:4 * i + 4], LD_MOE, w.moeh[:, s, 4 * i:4 * i + 4],
                              w.moel[:, s, 4 * i:4 * i + 4], WS))
        for i in range(4):
            tiles.append((nat_w3[:, 4 * i:4 * i + 4], LD_MOE, w.w3t[:, 4 * i:4 * i + 4], None, 1.0))
        NT = len(tiles)
        NB = 6

        def lows(k):
            return sum(lo is not None for _, _, _, lo, _ in tiles[:k])

        def tile_bank(k, src):
            p, t, n = src.shape
            return bank[k % NB][0:n, 0:t * p].rearrange("q (t p) -> q t p", p=p)

        def product_bank(g):
            return bank[(NT + g) % NB][:, :].rearrange("q (t p) -> q t p", p=128)

        def product_heads(g):
            first = 2 * HG * (g // 2) + g % 2
            return slice(first, first + 2 * HG - 1, 2)

        @block.sync
        def _(sp):
            xv = a["x"].rearrange("b s d -> s b d")
            for i in range(4):
                sp.dma_start(w.X[:, 8 * i:8 * i + 8, :], xv[:, 8 * i:8 * i + 8, :]).then_inc(x_in[i], 16)
            sp.dma_start(w.ctx[:], a["ctx"].rearrange("b s d -> s b d")).then_inc(ctx_in, 16)
            for i, src in enumerate((a["w1"], a["w2"])):
                sp.dma_start(nat_moe[:, i], src.rearrange("e (m p) d -> p (e m) d", p=128)).then_inc(moe_in, 16)
            sp.dma_start(nat_w3[:].rearrange("p (e m) d -> p e m d", m=MH),
                         a["w3"].rearrange("e d (m h) -> d e m h", h=128)).then_inc(moe_in, 16)
            for s in (*x_in, ctx_in):
                sp.wait_ge(s, 16)
            sp.wait_ge(moe_in, 48)

        @block.scalar
        def _(act):
            act.dma_start(gates[:, 0:2], a["gx"].rearrange("(o n) -> o n", o=1).broadcast_to([128, 2])).then_inc(small_in, 16)
            act.dma_start(gates[:, 2:4], a["gf"].rearrange("(o n) -> o n", o=1).broadcast_to([128, 2])).then_inc(small_in, 16)
            act.dma_start(nat_f[:, 0].rearrange("p (m d) -> p m d", d=D),
                          a["fw1"].rearrange("(m p) d -> p m d", p=128)).then_inc(ffn_in, 16)
            act.dma_start(nat_f[:, 1], a["fw2"]).then_inc(ffn_in, 16)
            act.dma_start(conv_w[:], a["cw"].rearrange("(m p) o t -> p m (o t)", p=128)).then_inc(ffn_in, 16)
            act.dma_start(conv_b[:], a["cb"].rearrange("(m p) -> p m", p=128),
                          allow_slow_non_contiguous=True).then_inc(ffn_in, 16)
            act.dma_start(nat_q1[:], a["q1"]).then_inc(l1_in, 16)
            act.dma_start(nat_k1[:], a["kv1"][:, 0:H * DK1]).then_inc(l1_in, 16)
            act.dma_start(nat_v1[:], a["kv1"][:, H * DK1:]).then_inc(l1_in, 16)
            act.dma_start(nat_o1[:], a["o1"].rearrange("(t p) d -> p t d", p=128)).then_inc(l1_in, 16)
            act.dma_start(nat_o0[:, 0], a["o0"]).then_inc(l1_in, 16)
            for dst, src in ((nat_q0, a["q0"]), (nat_k0, a["k0"]), (nat_v0, a["v0"])):
                act.dma_start(dst[:].rearrange("d (h k) -> d h k", k=DK0), src.rearrange("h d k -> d h k")).then_inc(l0_in, 16)
            act.dma_start(nat_g[:, 0], a["wg"]).then_inc(small_in, 16)
            act.dma_start(mask_u8[:], a["mask"]).then_inc(small_in, 16)
            act.dma_start(mask_rows[:], a["mask"].rearrange("(o b) c -> o (b c)", o=1).broadcast_to([128, B * C])).then_inc(small_in, 16)
            for i, src in enumerate((a["bo0"], a["go1"], a["bo1"])):
                act.dma_start(rows[:, i], src.rearrange("(o n) -> o n", o=1).broadcast_to([128, D])).then_inc(small_in, 16)
            for i, src in enumerate((a["gl1"], a["bl1"], a["gx1"], a["bx1"])):
                act.dma_start(w.gb[:, i:i + 1], src.rearrange("(n o) -> n o", o=1)).then_inc(small_in, 16)
            act.wait_ge(small_in, 12 * 16)
            act.activation(tanhs[:], gates[:], ACT.Tanh).then_inc(tanh_done, 1)
            act.wait_ge(l0_in, 48)
            act.activation(comp[:, 0], nat_q0[:], ACT.Copy, scale=WS).then_inc(plain_hi, 1)
            act.activation(comp[:, 2], nat_k0[:], ACT.Copy, scale=WS).then_inc(plain_hi, 1)
            act.activation(w.v0h[:], nat_v0[:], ACT.Copy, scale=WS).then_inc(plain_hi, 1)
            act.wait_ge(l1_in, 80)
            act.activation(w.v1h[:], nat_v1[:], ACT.Copy, scale=WS).then_inc(plain_hi, 1)
            act.activation(w.o1h[:], nat_o1[:], ACT.Copy, scale=WS).then_inc(plain_hi, 1)
            for k, (src, _, hi, _, scale) in enumerate(tiles):
                act.wait_ge(tiles_done, k + 1)
                act.activation(hi, tile_bank(k, src), ACT.Copy, scale=scale).then_inc(hi_done, 1)
            for g in range(G):
                act.wait_ge(tiles_done, NT + g + 1)
                act.activation(w.ah[:, product_heads(g)], product_bank(g), ACT.Copy,
                               scale=AS * DK1 ** -0.5).then_inc(hi_done, 1)

        @block.tensor
        def _(pe):
            pe.wait_ge(made, 2)
            pe.wait_ge(summed, 1)
            pe.matmul(bank[7][:, 0:2], ones[:], absum[:], start=True, stop=True).then_inc(summed, 1)
            for k, (src, stage, _, _, _) in enumerate(tiles):
                if stage == LD_L1:
                    pe.wait_ge(l1_in, 80)
                elif stage == LD_MOE:
                    pe.wait_ge(moe_in, 48)
                elif stage == LD_SMALL:
                    pe.wait_ge(small_in, 12 * 16)
                    pe.wait_ge(mask_done, 1)
                elif stage == TAPS:
                    pe.wait_ge(quant_done, 2)
                elif stage == QUANT:
                    pe.wait_ge(quant_done, 1)
                if k >= NB:
                    pe.wait_ge(hi_done, k - NB + 1)
                    if lows(k - NB + 1):
                        pe.wait_ge(lo_done, lows(k - NB + 1))
                p, t, n = src.shape
                dst = tile_bank(k, src)
                for i in range(t):
                    last = pe.transpose(dst[:, i, :], src[:, i, :], w.ident[0:p, 0:p])
                last.then_inc(tiles_done, 1)
            pe.wait_ge(hi_done, 4)
            for g in range(G):
                pe.wait_ge(hi_done, NT + g - NB + 1)
                pe.wait_ge(lo_done, lows(NT + g - NB + 1))
                for i in range(HG):
                    half, t = slice(DK1 * (g % 2), DK1 * (g % 2) + DK1), HG * (g // 2) + i
                    last = pe.matmul(product_bank(g)[:, i, :], q1t[half, t, :], k1t[half, t, :],
                                     start=True, stop=True)
                last.then_inc(tiles_done, 1)

        @block.gpsimd
        def _(pool):
            link = linker(pool, pchain)
            link(pool.memset(w.ident[:], 0.0))
            link(pool.memset(w.identh[:], 0.0))
            pool.affine_select(out=w.ident[:], in_=w.ident[:], compare_op=ALU.not_equal, fill=1.0, base=0,
                               pattern=[[-1, 128]], channel_multiplier=1).then_inc(made, 1)
            pool.memset(ones[:], 1.0).then_inc(made, 1)
            pool.affine_select(out=w.identh[:], in_=w.identh[:], compare_op=ALU.not_equal, fill=1.0, base=0,
                               pattern=[[-1, 128]], channel_multiplier=1).then_inc(made, 1)
            link(pool.memset(w.head_rows[:], 0.0))
            for r in range(3):
                blk = w.head_rows[32 * r:32 * r + 32, :]
                link(pool.memset(blk, 1.0))
                link(pool.affine_select(out=blk, in_=blk, compare_op=ALU.is_ge, fill=0.0, base=0,
                                        pattern=[[-DK0, HG]], channel_multiplier=1))
                link(pool.affine_select(out=blk, in_=blk, compare_op=ALU.is_ge, fill=0.0, base=DK0 - 1,
                                        pattern=[[DK0, HG]], channel_multiplier=-1))
            link(pool.iota(iota_i[:], pattern=[[1, E]], base=0, channel_multiplier=0))
            link(pool.tensor_copy(w.iota[:], iota_i[:]))
            pool.wait_ge(small_in, 12 * 16)
            link(pool.tensor_copy(mask_f[:, 0], mask_u8[:]))
            pool.tensor_scalar(mask_f[:, 0], mask_f[:, 0], -1.0, -MASKED, ALU.add, ALU.mult).then_inc(mask_done, 1)
            pool.tensor_copy(w.mask01[:].rearrange("p b c -> p (b c)"), mask_rows[:]).then_inc(mask_done, 1)

        @block.vector
        def _(dve):
            link = linker(dve, chain)
            dve.wait_ge(ffn_in, 64)
            link(dve.tensor_reduce(absum[:], nat_f[:], AX.X, ALU.add, apply_absolute_value=True))
            dve.sem_inc(summed, 1)
            dve.wait_ge(summed, 2)
            link(dve.tensor_scalar(wmean[:], bank[7][:, 0:2], 1.0 / (HID * D), 1e-5, ALU.mult, ALU.max))
            link(dve.reciprocal(winv[:], wmean[:]))
            for i in (1, 0):
                link(dve.tensor_scalar(nat_f[:, i], nat_f[:, i], winv[:, i:i + 1], ROUND, ALU.mult, ALU.add))
                link(dve.tensor_scalar(nat_f[:, i], nat_f[:, i], ROUND, 1.0, ALU.subtract, ALU.min))
                ins = dve.tensor_scalar(nat_f[:, i], nat_f[:, i], -1.0, None, ALU.max)
                if i == 1:
                    ins.then_inc(quant_done, 1)
                else:
                    link(ins)
            link(dve.tensor_scalar(cs[:], conv_w[:], wmean[:, 0:1], None, ALU.mult))
            for t in range(3):
                for i in range(M0):
                    last = dve.tensor_scalar(tap_w[:, t, i], nat_f[:, 0, D * i:D * i + D], cs[:, i, t:t + 1], None, ALU.mult)
            link(last)
            dve.sem_inc(quant_done, 1)
            dve.tensor_scalar(w.conv_b_half[:], conv_b[:], 0.5, None, ALU.mult)
            dve.wait_ge(tanh_done, 1)
            dve.tensor_scalar(w.tg0[:], tanhs[:, 0:1], 1.0 / WS, None, ALU.mult)
            dve.tensor_scalar(w.bias0[:], rows[:, 0], tanhs[:, 0:1], None, ALU.mult)
            dve.tensor_scalar(w.gain1[:], rows[:, 1], tanhs[:, 1:2], 1.0 / WS, ALU.mult, ALU.mult)
            dve.tensor_scalar(w.bias1[:], rows[:, 2], tanhs[:, 1:2], None, ALU.mult)
            link(dve.tensor_scalar(w.ffn_out[:], wmean[:, 1:2], 0.5, None, ALU.mult))
            link(dve.tensor_tensor(w.ffn_out[:], w.ffn_out[:], tanhs[:, 2:3], ALU.mult))
            dve.tensor_scalar(w.moe_out[:], tanhs[:, 3:4], 0.5 / (WS * WS), None, ALU.mult)
            dve.wait_ge(plain_hi, 5)
            dve.wait_ge(l0_in, 48)
            dve.wait_ge(l1_in, 80)
            link(dve.scalar_tensor_tensor(comp[:, 1], nat_q0[:], WS, comp[:, 0], ALU.mult, ALU.subtract))
            link(dve.scalar_tensor_tensor(comp[:, 3], nat_k0[:], WS, comp[:, 2], ALU.mult, ALU.subtract))
            dve.scalar_tensor_tensor(w.v0l[:], nat_v0[:], WS, w.v0h[:], ALU.mult, ALU.subtract)
            dve.scalar_tensor_tensor(w.v1l[:], nat_v1[:], WS, w.v1h[:], ALU.mult, ALU.subtract)
            dve.scalar_tensor_tensor(w.o1l[:].rearrange("p t d -> p (t d)"), nat_o1[:].rearrange("p t d -> p (t d)"), WS,
                                     w.o1h[:].rearrange("p t d -> p (t d)"), ALU.mult, ALU.subtract)
            for i, dst in enumerate((w.q0h, w.q0l, w.k0h, w.k0l)):
                dve.tensor_copy(dst[:], comp[:, i].rearrange("p (g r) -> p g r", g=G).unsqueeze(2).broadcast_to([128, G, 3, 32]))
            for k, (src, _, hi, lo, scale) in enumerate(tiles):
                if lo is not None:
                    dve.wait_ge(hi_done, k + 1)
                    dve.scalar_tensor_tensor(lo, tile_bank(k, src), scale, hi, ALU.mult, ALU.subtract).then_inc(lo_done, 1)
            for g in range(G):
                dve.wait_ge(hi_done, NT + g + 1)
                dve.scalar_tensor_tensor(w.al[:, product_heads(g)], product_bank(g), AS * DK1 ** -0.5,
                                         w.ah[:, product_heads(g)], ALU.mult, ALU.subtract).then_inc(lo_done, 1)
            for i in range(4):
                dve.wait_ge(x_in[i], 16)
            dve.wait_ge(ctx_in, 16)
            for b in range(B):
                dve.bn_stats(bn[:, b], w.X[:, b])
                last = dve.bn_stats(bn_c[:, b], w.ctx[:, b])
            link(last)
            for b in range(B):
                dve.bn_aggr(w.mv[:, b], bn[:, b])
                last = dve.bn_aggr(w.mv_c[:, b], bn_c[:, b])
            link(last)
            rsqrt(dve, link, w.rstd[:], w.mv[:, :, 1], t1[:], t2[:])
            rsqrt(dve, link, w.rstd_c[:], w.mv_c[:, :, 1], t1[0:C], t2[0:C])


def split_transposed(nc, w, bank, tag, rows, src, hi, lo, mean=None, rstd=None, gain=None, bias=None, before=None):
    with Memory(nc, tag) as m:
        normed = m.sb("normed", [rows, 2, CH, D])
        whole = m.sb("whole", [128, 2, CH, rows])
        ready, turned, high, split, chain = (
            m.sem(n) for n in ("ready", "turned", "high", "split", "chain"))
        pre = before(m) if before is not None else None
        block = m.block()
        banks = [bank[u][:, 0:CH * rows].rearrange("p (c r) -> p c r", r=rows) for u in range(2)]

        @block.vector
        def _(dve):
            if pre is not None:
                pre(dve, linker(dve, chain))
            with dve.Fori(0, NCH // 2) as i:
                for u in range(2):
                    dve.wait_ge(turned, i * 2 + (u + 1))
                    for c in range(CH):
                        one = bass.ds(i * (2 * CH) + (CH * u + c), 1)
                        if mean is None:
                            last = dve.tensor_copy(normed[:, u, c:c + 1], src[:, one, :])
                        else:
                            last = dve.tensor_scalar(normed[:, u, c:c + 1], src[:, one, :], mean[:, one, 0:1], rstd[:, one],
                                                     ALU.subtract, ALU.mult)
                    last.then_inc(ready, 1)

        @block.tensor
        def _(pe):
            pe.sem_inc(turned, 2)
            with pe.Fori(0, NCH // 2) as i:
                for u in range(2):
                    pe.wait_ge(ready, i * 2 + (u + 1))
                    pe.wait_ge(high, i * 2 + (u + 1))
                    for c in range(CH):
                        last = pe.transpose(banks[u][:, c, :], normed[:, u, c], w.ident[0:rows, 0:rows])
                    last.then_inc(turned, 1)

        @block.scalar
        def _(act):
            act.sem_inc(high, 2)
            with act.Fori(0, NCH // 2) as i:
                for u in range(2):
                    chunk = bass.ds(i * (2 * CH) + CH * u, CH)
                    act.wait_ge(turned, i * 2 + (u + 3))
                    act.wait_ge(split, i * 2 + (u + 1))
                    for dst in (whole[:, u], hi(chunk)):
                        if gain is None:
                            last = act.activation(dst, banks[u], ACT.Copy)
                        else:
                            last = act.activation(dst, banks[u], ACT.Identity, bias=bias, scale=gain)
                    last.then_inc(high, 1)

        @block.gpsimd
        def _(pool):
            pool.sem_inc(split, 2)
            with pool.Fori(0, NCH // 2) as i:
                for u in range(2):
                    chunk = bass.ds(i * (2 * CH) + CH * u, CH)
                    pool.wait_ge(high, i * 2 + (u + 3))
                    pool.tensor_tensor(lo(chunk), whole[:, u], hi(chunk), ALU.subtract).then_inc(split, 1)


def project0(nc, w, bank, xh, xl, ch, cl, qst, kst, vals):
    with Memory(nc, "project0") as m:
        q_done, q_hi, q_lo, k_done, k_hi, k_lo, v_done, v_out = (
            m.sem(n) for n in ("q_done", "q_hi", "q_lo", "k_done", "k_hi", "k_lo", "v_done", "v_out"))
        block = m.block()
        KC = CH * C
        q_bank = [bank[g][0:R0, :] for g in range(G)]
        k_bank = [bank[4 + g % 2][0:R0, 0:KC] for g in range(G)]
        v_bank = [bank[6 + u][0:C, :] for u in range(2)]
        SQ = DK0 ** -0.5 / WS

        @block.tensor
        def _(pe):
            pe.sem_inc(q_lo, G)
            pe.sem_inc(k_lo, 2)
            pe.sem_inc(v_out, 2)
            with pe.Fori(0, NCH // 2) as i:
                for u in range(2):
                    chunk = bass.ds(i * (2 * CH) + CH * u, CH)
                    for g in range(G):
                        n = G * u + g
                        pe.wait_ge(q_lo, i * (2 * G) + (n + 1))
                        for k, (wt, x) in enumerate(((w.q0h, xh), (w.q0l, xh), (w.q0h, xl))):
                            last = pe.matmul(q_bank[g], wt[:, g].rearrange("p a r -> p (a r)"), x[:, chunk, :],
                                             start=k == 0, stop=k == 2)
                        last.then_inc(q_done, 1)
                        pe.wait_ge(k_lo, i * (2 * G) + (n + 1))
                        for k, (wt, x) in enumerate(((w.k0h, ch), (w.k0l, ch), (w.k0h, cl))):
                            last = pe.matmul(k_bank[g], wt[:, g].rearrange("p a r -> p (a r)"), x[:, chunk, :],
                                             start=k == 0, stop=k == 2)
                        last.then_inc(k_done, 1)
                    pe.wait_ge(v_out, i * 2 + (u + 1))
                    for c in range(CH):
                        one = bass.ds(i * (2 * CH) + (CH * u + c), 1)
                        for k, (x, wt) in enumerate(((ch, w.v0h), (ch, w.v0l), (cl, w.v0h))):
                            last = pe.matmul(v_bank[u][:, D * c:D * c + D], x[:, one, :], wt[:], start=k == 0, stop=k == 2)
                    last.then_inc(v_done, 1)

        @block.scalar
        def _(act):
            with act.Fori(0, NCH // 2) as i:
                for u in range(2):
                    chunk = bass.ds(i * (2 * CH) + CH * u, CH)
                    for g in range(G):
                        n = G * u + g
                        act.wait_ge(q_done, i * (2 * G) + (n + 1))
                        act.activation(qst[:, g, chunk, :], q_bank[g].rearrange("p (c s) -> p c s", c=CH), ACT.Copy,
                                       scale=SQ).then_inc(q_hi, 1)
                        act.wait_ge(k_done, i * (2 * G) + (n + 1))
                        act.activation(kst[:, g, chunk, :], k_bank[g].rearrange("p (c s) -> p c s", c=CH), ACT.Copy,
                                       scale=1.0 / WS).then_inc(k_hi, 1)

        @block.vector
        def _(dve):
            dve.memset(vals[:, :, :, DK0:DK0 + 1], 1.0)
            with dve.Fori(0, NCH // 2) as i:
                for u in range(2):
                    chunk = bass.ds(i * (2 * CH) + CH * u, CH)
                    for g in range(G):
                        n = G * u + g
                        low = slice(64, 96)
                        dve.wait_ge(q_hi, i * (2 * G) + (n + 1))
                        dve.scalar_tensor_tensor(qst[low, g, chunk, :], q_bank[g][low].rearrange("p (c s) -> p c s", c=CH), SQ,
                                                 qst[low, g, chunk, :], ALU.mult, ALU.subtract).then_inc(q_lo, 1)
                        low = slice(32, 64)
                        dve.wait_ge(k_hi, i * (2 * G) + (n + 1))
                        dve.scalar_tensor_tensor(kst[low, g, chunk, :], k_bank[g][low].rearrange("p (c s) -> p c s", c=CH),
                                                 1.0 / WS, kst[low, g, chunk, :], ALU.mult, ALU.subtract).then_inc(k_lo, 1)
                    dve.wait_ge(v_done, i * 2 + (u + 1))
                    for c in range(CH):
                        one = bass.ds(i * (2 * CH) + (CH * u + c), 1)
                        last = dve.tensor_scalar(vals[:, one, :, 0:DK0], v_bank[u][:, D * c:D * c + D].rearrange("p (h k) -> p h k", k=DK0),
                                                 1.0 / WS, None, ALU.mult)
                    last.then_inc(v_out, 1)


def attention0(nc, w, bank, qst, kst, vals):
    with Memory(nc, "attention0") as m:
        keys = m.sb("keys", [R0, 2, G, HG, C], FP16)
        queries = m.sb("queries", [R0, 2, G, S], FP16)
        values = m.sb("values", [C, 2, H, DK0 + 1])
        negmax = m.sb("negmax", [S, G, HG], FP16)
        probs = m.sb("probs", [C, 2, HG, S])
        recip = m.sb("recip", [S, H])
        heads_out = m.sb("heads_out", [S, H, DK0])
        turned_h, turned_l = m.sb("turned_h", [D, S], FP16), m.sb("turned_l", [D, S], FP16)
        new, bn, mv = m.sb("new", [S, 1, D]), m.sb("bn", [S, 6]), m.sb("mv", [S, 1, 2])
        waited = m.sem("waited")
        staged, q_staged, v_staged, scored, maxed, shifted, exped, mixed, normed, turned, ot_hi, ot_lo, projected, added, biased, chain = (
            m.sem(n) for n in ("staged", "q_staged", "v_staged", "scored", "maxed", "shifted", "exped", "mixed", "normed", "turned",
                               "ot_hi", "ot_lo", "projected", "added", "biased", "chain"))
        block = m.block()
        score = [bank[u][:, 0:HG * C].rearrange("p (h c) -> p h c", c=C) for u in range(2)]
        score_t = [bank[2 + u][0:C, :].rearrange("p (h s) -> p h s", s=S) for u in range(2)]
        mix = [bank[4 + u][:, 0:H * (DK0 + 1)].rearrange("p (h k) -> p h k", k=DK0 + 1) for u in range(2)]
        out_t = bank[6][:, 0:S]
        out_p = bank[7][:, 0:D]

        def batches(eng, body):
            body(0, 0, True, False)
            with eng.Fori(0, (B - 2) // 2) as i:
                body(i * 2 + 1, 1, False, False)
                body(i * 2 + 2, 0, False, False)
            body(B - 1, (B - 1) % 2, False, True)

        @block.gpsimd
        def _(pool):
            def stage(b, u):
                one = bass.ds(b, 1)
                for g in range(G):
                    last = pool.tensor_tensor(keys[:, u, g], kst[:, g, one, :].broadcast_to([R0, HG, C]),
                                              w.head_rows[:].unsqueeze(2).broadcast_to([R0, HG, C]), ALU.mult)
                last.then_inc(staged, 1)

            def body(b, u, first, last):
                if not last:
                    if not first:
                        pool.wait_ge(shifted, b * G)
                    stage(b + 1, 1 - u)
                pool.tensor_tensor(w.X[:, bass.ds(b, 1), :], w.X[:, bass.ds(b, 1), :], w.bias0[:].unsqueeze(1), ALU.add).then_inc(biased, 1)

            stage(0, 0)
            batches(pool, body)

        @block.tensor
        def _(pe):
            def scores(n, u, g):
                pe.matmul(score[g % 2], queries[:, u, g], keys[:, u, g], start=True, stop=True).then_inc(scored, 1)

            def scores_by_key(n, u, g):
                for h in range(HG):
                    dst = score_t[g % 2][:, h, :]
                    pe.matmul(dst, keys[:, u, g, h], queries[:, u, g], start=True, stop=False)
                    last = pe.matmul(dst, negmax[:, g, h:h + 1].broadcast_to([S, C]), w.identh[:], start=False, stop=True)
                last.then_inc(shifted, 1)

            def mix_values(u, g):
                for h in range(HG):
                    last = pe.matmul(mix[u][:, HG * g + h, :], probs[:, g % 2, h], values[:, u, HG * g + h, :],
                                     start=True, stop=True)
                last.then_inc(mixed, 1)

            def turn(t):
                pe.wait_ge(normed, t + 1)
                pe.transpose(out_t, heads_out[:].rearrange("p h k -> p (h k)"), w.ident[:]).then_inc(turned, 1)

            def project(t):
                pe.wait_ge(ot_hi, t + 1)
                pe.wait_ge(ot_lo, t + 1)
                if not isinstance(t, int) or t > 0:
                    pe.wait_ge(added, t)
                for k, (x, wt) in enumerate(((turned_h, w.o0h), (turned_h, w.o0l), (turned_l, w.o0h))):
                    last_mm = pe.matmul(out_p, x[:], wt[:, 0, :], start=k == 0, stop=k == 2)
                last_mm.then_inc(projected, 1)

            def body(b, u, first, last):
                for g in range(G):
                    n = b * G + g
                    if not (last and g == G - 1):
                        if g == G - 1:
                            pe.wait_ge(staged, b + 2)
                            pe.wait_ge(q_staged, b + 2)
                            pe.wait_ge(v_staged, b + 2)
                        if not (first and g == 0):
                            pe.wait_ge(maxed, n)
                        scores(n + 1, u if g < G - 1 else 1 - u, (g + 1) % G)
                    pe.wait_ge(maxed, n + 1)
                    if not (first and g < 2):
                        pe.wait_ge(exped, n - 1)
                    scores_by_key(n, u, g)
                    if not (first and g == 0):
                        pe.wait_ge(exped, n)
                        mix_values(u if g > 0 else 1 - u, (g + G - 1) % G)
                    if g == 1 and not first:
                        turn(b - 1)
                    if g == 2 and not first:
                        project(b - 1)

            pe.wait_ge(staged, 1)
            pe.wait_ge(q_staged, 1)
            pe.wait_ge(v_staged, 1)
            scores(0, 0, 0)
            batches(pe, body)
            pe.wait_ge(exped, B * G)
            mix_values((B - 1) % 2, G - 1)
            turn(B - 1)
            project(B - 1)

        @block.scalar
        def _(act):
            def stage(b, u):
                act.activation(values[:, u], vals[:, bass.ds(b, 1), :, :].rearrange("p o h k -> p (o h) k"),
                               ACT.Copy).then_inc(v_staged, 1)

            def out_high(t):
                act.wait_ge(turned, t + 1)
                if not isinstance(t, int) or t > 0:
                    act.wait_ge(projected, t)
                act.activation(turned_h[:], out_t, ACT.Copy).then_inc(ot_hi, 1)

            def body(b, u, first, last):
                for g in range(G):
                    n = b * G + g
                    act.wait_ge(shifted, n + 1)
                    if not (first and g < 2):
                        act.wait_ge(mixed, n - 1)
                    act.activation(probs[:, g % 2], score_t[g % 2], ACT.Exp).then_inc(exped, 1)
                    if g == 1 and not first:
                        out_high(b - 1)
                    if g == 1 and not last:
                        if not first:
                            act.wait_ge(mixed, b * G)
                        stage(b + 1, 1 - u)

            stage(0, 0)
            batches(act, body)
            out_high(B - 1)

        @block.vector
        def _(dve):
            def stage(b, u):
                dve.tensor_copy(queries[:, u], qst[:, :, bass.ds(b, 1), :].rearrange("p g o s -> p g (o s)")).then_inc(q_staged, 1)

            def maximum(n, g):
                dve.wait_ge(scored, n + 1)
                dve.tensor_reduce(negmax[:, g], score[g % 2], AX.X, ALU.max, negate=True).then_inc(maxed, 1)

            LINKS = 4

            def normalise(t, u):
                dve.wait_ge(mixed, (t + 1) * G)
                dve.reciprocal(recip[:], mix[u][:, :, DK0]).then_inc(chain, 1)
                dve.wait_ge(chain, t * LINKS + 1)
                if not isinstance(t, int) or t > 0:
                    dve.wait_ge(turned, t)
                dve.tensor_tensor(heads_out[:], mix[u][:, :, 0:DK0], recip[:].unsqueeze(2).broadcast_to([S, H, DK0]),
                                  ALU.mult).then_inc(normed, 1)

            def out_low(t):
                dve.wait_ge(ot_hi, t + 1)
                dve.tensor_tensor(turned_l[:], out_t, turned_h[:], ALU.subtract).then_inc(ot_lo, 1)

            def residual(t):
                row = w.X[:, bass.ds(t, 1), :]
                dve.wait_ge(projected, t + 1)
                dve.wait_ge(biased, t + 1)
                dve.wait_ge(ot_lo, t + 1)
                dve.scalar_tensor_tensor(new[:], out_p.unsqueeze(1), w.tg0[:], row, ALU.mult, ALU.add).then_inc(added, 1)
                dve.wait_ge(added, t + 1)
                dve.bn_stats(bn[:], new[:, 0]).then_inc(chain, 1)
                dve.tensor_copy(row, new[:])
                dve.wait_ge(chain, t * LINKS + 2)
                dve.sem_inc(waited, 1)
                dve.bn_aggr(mv[:, 0], bn[:]).then_inc(chain, 1)
                dve.wait_ge(chain, t * LINKS + 3)
                dve.tensor_copy(w.mv[:, bass.ds(t, 1), :], mv[:]).then_inc(chain, 1)

            def body(b, u, first, last):
                for g in range(G):
                    maximum(b * G + g, g)
                    if g == 1:
                        if not first:
                            normalise(b - 1, 1 - u)
                        if not last:
                            if not first:
                                dve.wait_ge(shifted, b * G)
                            stage(b + 1, 1 - u)
                    if g == 2 and not first:
                        out_low(b - 1)
                    if g == 3 and not first:
                        residual(b - 1)

            stage(0, 0)
            batches(dve, body)
            normalise(B - 1, (B - 1) % 2)
            out_low(B - 1)
            residual(B - 1)


def feed_forward0(nc, w, bank):
    with Memory(nc, "feed_forward0") as m:
        normed, rounded = m.sb("normed", [S, 2, CH, D]), m.sb("rounded", [S, 2, CH, D])
        amax, scale, step_of = m.sb("amax", [S, 2, CH]), m.sb("scale", [S, 2, CH]), m.sb("step_of", [S, 2, CH])
        rows_h, rows_l = m.sb("rows_h", [D, 2, CH, S], FP16), m.sb("rows_l", [D, 2, CH, S], FP16)
        pre, tanh = m.sb("pre", [128, 2, N]), m.sb("tanh", [128, 2, N])
        silu = m.sb("silu", [128, 2, M0, N])
        biased = m.sb("biased", [S, 2, HID])
        ints = m.sb("ints", [128, 2, M0, S], FP16)
        amax2, scale2, out_of = m.sb("amax2", [S, 1]), m.sb("scale2", [S, 2]), m.sb("out_of", [S, 2])
        new, bn, mv = m.sb("new", [S, 1, D]), m.sb("bn", [S, 6]), m.sb("mv", [S, 1, 2])
        waited, pool_waited = m.sem("waited"), m.sem("pool_waited")
        t1, t2 = m.sb("t1", [S, B]), m.sb("t2", [S, B])
        (rsqrt_done, normed_in, scales, rounded_in, quant, turned, rows_hi, rows_lo, conved, activated, silued, returned,
         maxed, scale_in, biased_in, turned_back, ints_in, projected, added, chain, achain, chain_out) = (
            m.sem(n) for n in ("rsqrt_done", "normed_in", "scales", "rounded_in", "quant", "turned", "rows_hi", "rows_lo",
                               "conved", "activated", "silued", "returned", "maxed", "scale_in", "biased_in",
                               "turned_back", "ints_in", "projected", "added", "chain", "achain", "chain_out"))
        block = m.block()
        rows_t = bank[0][:, :].rearrange("p (c s) -> p c s", s=S)
        conv = [bank[1 + u][:, :].rearrange("p (c s) -> p c s", s=S) for u in range(2)]
        by_row = [bank[3 + u][:, :].rearrange("p (m c) -> p m c", c=128) for u in range(2)]
        by_channel = [bank[5 + u][:, :].rearrange("p (m s) -> p m s", s=S) for u in range(2)]
        out_p = bank[7][:, 0:D]
        LOOP = (1, 5)

        def chunks(eng, body):
            body(0, 0)
            with eng.Fori(0, (LOOP[1] - LOOP[0]) // 2) as i:
                body(i * 2 + 1, 1)
                body(i * 2 + 2, 0)
            for k in range(LOOP[1], NCH):
                body(k, k % 2)

        def within(k, ahead):
            return not isinstance(k, int) or k + ahead < NCH

        @block.gpsimd
        def _(pool):
            def quantise(k, u):
                pool.wait_ge(scales, k + 1)
                pool.sem_inc(pool_waited, 1)
                for c in range(CH):
                    last = pool.tensor_scalar(rounded[:, u, c], normed[:, u, c], scale[:, u, c:c + 1], ROUND, ALU.mult, ALU.add)
                last.then_inc(rounded_in, 1)
                pool.wait_ge(rounded_in, k + 1)
                if not isinstance(k, int) or k >= 2:
                    pool.wait_ge(turned, k - 1)
                pool.sem_inc(pool_waited, 1)
                for c in range(CH):
                    last = pool.tensor_scalar(normed[:, u, c], rounded[:, u, c], ROUND, step_of[:, u, c:c + 1],
                                              ALU.subtract, ALU.mult)
                last.then_inc(quant, 1)

            quantise(0, 0)
            quantise(1, 1)
            chunks(pool, lambda k, u: quantise(k + 2, u) if within(k, 2) else None)

        @block.tensor
        def _(pe):
            def turn(k, u):
                pe.wait_ge(quant, k + 1)
                if not isinstance(k, int) or k > 0:
                    pe.wait_ge(rows_lo, k)
                for c in range(CH):
                    last = pe.transpose(rows_t[:, c, :], normed[:, u, c], w.ident[:])
                last.then_inc(turned, 1)

            def convolve(k, u, t):
                n = k * M0 + t
                pe.wait_ge(rows_lo, k + 1)
                if not isinstance(k, int) or n >= 2:
                    pe.wait_ge(activated, n - 1)
                products = [(tap, wt, x) for tap in (1, 0, 2) for wt, x in ((w.taph, rows_h), (w.tapl, rows_h), (w.taph, rows_l))]
                for i, (tap, wt, x) in enumerate(products):
                    to = slice(max(0, 1 - tap), S - max(0, tap - 1))
                    of = slice(max(0, tap - 1), S - max(0, 1 - tap))
                    last = pe.matmul(conv[t % 2][:, :, to], wt[:, tap, t], x[:, u, :, of], start=i == 0, stop=i == len(products) - 1)
                last.then_inc(conved, 1)

            def to_rows(k, u, c):
                n = k * CH + c
                pe.wait_ge(silued, (k + 1) * M0)
                if not isinstance(k, int) or n >= 2:
                    pe.wait_ge(biased_in, n - 1)
                for t in range(M0):
                    last = pe.transpose(by_row[c % 2][:, t, :], silu[:, u, t, S * c:S * c + S], w.ident[:])
                last.then_inc(returned, 1)

            def to_channels(k, c):
                n = k * CH + c
                pe.wait_ge(biased_in, n + 1)
                if not isinstance(k, int) or n >= 2:
                    pe.wait_ge(ints_in, n - 1)
                for t in range(M0):
                    last = pe.transpose(by_channel[c % 2][:, t, :], biased[:, c % 2, 128 * t:128 * t + 128], w.ident[:])
                last.then_inc(turned_back, 1)

            def project(n, c):
                pe.wait_ge(ints_in, n + 1)
                if not isinstance(n, int) or n >= 1:
                    pe.wait_ge(added, n)
                for t in range(M0):
                    last = pe.matmul(out_p, ints[:, c % 2, t], w.w2t[:, t], start=t == 0, stop=t == M0 - 1)
                last.then_inc(projected, 1)

            def body(k, u):
                for c in range(CH):
                    to_rows(k, u, c)
                    if within(k, 1):
                        convolve(k + 1, 1 - u, c)
                    to_channels(k, c)
                    if not (isinstance(k, int) and k == 0 and c == 0):
                        project(k * CH + (c - 1), (c + CH - 1) % CH)
                    if c == CH - 1 and within(k, 2):
                        turn(k + 2, u)

            turn(0, 0)
            for t in range(M0):
                convolve(0, 0, t)
            turn(1, 1)
            chunks(pe, body)
            project(B - 1, CH - 1)

        @block.scalar
        def _(act):
            def rows_high(k, u):
                act.wait_ge(turned, k + 1)
                if not isinstance(k, int) or k >= 2:
                    act.wait_ge(conved, (k - 1) * M0)
                act.activation(rows_h[:, u], rows_t, ACT.Copy).then_inc(rows_hi, 1)

            def activate(k, t):
                n = k * M0 + t
                act.wait_ge(conved, n + 1)
                if not isinstance(k, int) or n >= 2:
                    act.wait_ge(silued, n - 1)
                src = bank[1 + t % 2][:, :]
                act.activation(tanh[:, t % 2], src, ACT.Tanh, bias=w.conv_b_half[:, t:t + 1], scale=0.5 / WS)
                act.activation(pre[:, t % 2], src, ACT.Identity, bias=w.conv_b[:, t:t + 1], scale=1.0 / WS).then_inc(activated, 1)

            def quantise(k, c):
                n = k * CH + c
                act.wait_ge(returned, n + 1)
                act.wait_ge(scale_in, n + 1)
                if not isinstance(k, int) or n >= 2:
                    act.wait_ge(turned_back, n - 1)
                act.activation(biased[:, c % 2], bank[3 + c % 2][:, :], ACT.Copy, bias=ROUND,
                               scale=scale2[:, c % 2:c % 2 + 1]).then_inc(biased_in, 1)

            def body(k, u):
                for c in range(CH):
                    quantise(k, c)
                    if within(k, 1):
                        activate(k + 1, c)
                    if c == CH - 1 and within(k, 2):
                        rows_high(k + 2, u)

            rows_high(0, 0)
            for t in range(M0):
                activate(0, t)
            rows_high(1, 1)
            chunks(act, body)

        @block.vector
        def _(dve):
            LINKS = 4
            OUT_LINKS = 4

            def normalise(k, u):
                if not isinstance(k, int) or k >= 2:
                    dve.wait_ge(turned, k - 1)
                for c in range(CH):
                    one = bass.ds(k * CH + c, 1)
                    last = dve.tensor_scalar(normed[:, u, c:c + 1], w.X[:, one, :], w.mv[:, one, 0:1], w.rstd[:, one],
                                             ALU.subtract, ALU.mult)
                last.then_inc(normed_in, 1)
                dve.wait_ge(normed_in, k + 1)
                dve.tensor_reduce(amax[:, u], normed[:, u], AX.X, ALU.max, apply_absolute_value=True).then_inc(chain, 1)
                dve.wait_ge(chain, k * LINKS + 1)
                dve.tensor_scalar(amax[:, u], amax[:, u], 1e-5, None, ALU.max).then_inc(chain, 1)
                dve.wait_ge(chain, k * LINKS + 2)
                dve.reciprocal(scale[:, u], amax[:, u]).then_inc(chain, 1)
                dve.wait_ge(chain, k * LINKS + 3)
                dve.tensor_scalar(scale[:, u], scale[:, u], 127.0, None, ALU.mult).then_inc(chain, 1)
                dve.tensor_scalar(step_of[:, u], amax[:, u], 1.0 / 127.0, None, ALU.mult).then_inc(scales, 1)
                dve.wait_ge(chain, k * LINKS + 4)

            def rows_low(k, u):
                dve.wait_ge(rows_hi, k + 1)
                dve.tensor_tensor(rows_l[:, u], rows_t, rows_h[:, u], ALU.subtract).then_inc(rows_lo, 1)

            def multiply(k, u, t):
                dve.wait_ge(activated, k * M0 + (t + 1))
                dve.scalar_tensor_tensor(silu[:, u, t], tanh[:, t % 2], 1.0, pre[:, t % 2], ALU.add, ALU.mult).then_inc(silued, 1)

            def scale_of(k, c):
                n = k * CH + c
                dve.wait_ge(returned, n + 1)
                if not isinstance(k, int) or n >= 2:
                    dve.wait_ge(biased_in, n - 1)
                dve.tensor_reduce(amax2[:], bank[3 + c % 2][:, :], AX.X, ALU.max, apply_absolute_value=True).then_inc(achain, 1)
                dve.wait_ge(achain, n * OUT_LINKS + 1)
                dve.tensor_scalar(amax2[:], amax2[:], 2e-5, None, ALU.max).then_inc(achain, 1)
                dve.wait_ge(achain, n * OUT_LINKS + 2)
                dve.reciprocal(scale2[:, c % 2:c % 2 + 1], amax2[:]).then_inc(achain, 1)
                dve.wait_ge(achain, n * OUT_LINKS + 3)
                dve.tensor_scalar(scale2[:, c % 2:c % 2 + 1], scale2[:, c % 2:c % 2 + 1], 127.0, None, ALU.mult).then_inc(scale_in, 1)
                dve.tensor_scalar(out_of[:, c % 2:c % 2 + 1], amax2[:], w.ffn_out[:], 1.0 / 127.0, ALU.mult, ALU.mult).then_inc(achain, 1)
                dve.wait_ge(achain, n * OUT_LINKS + 4)

            def integers(k, c):
                n = k * CH + c
                dve.wait_ge(turned_back, n + 1)
                if not isinstance(k, int) or n >= 2:
                    dve.wait_ge(projected, n - 1)
                dve.tensor_scalar(ints[:, c % 2], by_channel[c % 2], ROUND, None, ALU.subtract).then_inc(ints_in, 1)

            def residual(n, c):
                row = w.X[:, bass.ds(n, 1), :]
                dve.wait_ge(projected, n + 1)
                dve.scalar_tensor_tensor(new[:], out_p.unsqueeze(1), out_of[:, c % 2:c % 2 + 1], row, ALU.mult, ALU.add).then_inc(added, 1)
                dve.wait_ge(added, n + 1)
                dve.bn_stats(bn[:], new[:, 0]).then_inc(chain_out, 1)
                dve.tensor_copy(row, new[:])
                dve.wait_ge(chain_out, n * 3 + 1)
                dve.sem_inc(waited, 1)
                dve.bn_aggr(mv[:, 0], bn[:]).then_inc(chain_out, 1)
                dve.wait_ge(chain_out, n * 3 + 2)
                dve.tensor_copy(w.mv[:, bass.ds(n, 1), :], mv[:]).then_inc(chain_out, 1)

            def body(k, u):
                for c in range(CH):
                    scale_of(k, c)
                    if c == 0 and within(k, 2):
                        normalise(k + 2, u)
                    if within(k, 1):
                        multiply(k + 1, 1 - u, c)
                    integers(k, c)
                    if not (isinstance(k, int) and k == 0 and c == 0):
                        residual(k * CH + (c - 1), (c + CH - 1) % CH)
                    if c == CH - 1 and within(k, 2):
                        rows_low(k + 2, u)

            rsqrt(dve, linker(dve, rsqrt_done), w.rstd[:], w.mv[:, :, 1], t1[:], t2[:])
            normalise(0, 0)
            normalise(1, 1)
            rows_low(0, 0)
            for t in range(M0):
                multiply(0, 0, t)
            rows_low(1, 1)
            chunks(dve, body)
            residual(B - 1, CH - 1)


def mask_keys(nc, w, kv):
    with Memory(nc, "mask_keys") as m:
        diff = m.sb("diff", [D, CH, C], FP16)
        chain, copied = m.sem("chain"), m.sem("copied")
        block = m.block()

        @block.scalar
        def _(act):
            with act.Fori(0, NCH) as i:
                chunk = bass.ds(i * CH, CH)
                act.activation(kv[:, chunk, 2, 0:S], kv[:, chunk, 0, 0:S], ACT.Copy).then_inc(copied, 1)
            act.wait_ge(copied, NCH)

        @block.vector
        def _(dve):
            with dve.Fori(0, NCH) as i:
                chunk = bass.ds(i * CH, CH)
                latent0 = kv[:, chunk, 0, 0:1].broadcast_to([D, CH, C])
                dve.tensor_tensor(diff[:], kv[:, chunk, 0, S:KV], latent0, ALU.subtract).then_inc(chain, 1)
                dve.wait_ge(chain, i * 3 + 1)
                dve.tensor_tensor(diff[:], diff[:], w.mask01[:, chunk, :], ALU.mult).then_inc(chain, 1)
                dve.wait_ge(chain, i * 3 + 2)
                dve.tensor_tensor(kv[:, chunk, 2, S:KV], diff[:], latent0, ALU.add).then_inc(chain, 1)
                dve.wait_ge(chain, i * 3 + 3)


def latent_scale(w, B=B):
    def memory(m):
        t1, t2, r, v = (m.sb(n, [S, B]) for n in ("t1", "t2", "r", "v"))

        def work(dve, link):
            rsqrt(dve, link, r[:], w.mv[:, :, 1], t1[:], t2[:])
            link(dve.tensor_tensor(v[:], r[:], r[:], ALU.mult))
            link(dve.tensor_tensor(v[:], v[:], w.mv[:, :, 1], ALU.mult))
            rsqrt(dve, link, w.rstd[:], v[:], t1[:], t2[:])
            link(dve.tensor_tensor(w.rstd[:], w.rstd[:], r[:], ALU.mult))
        return work
    return memory


def row_scale(w):
    def memory(m):
        t1, t2 = m.sb("t1", [S, B]), m.sb("t2", [S, B])
        return lambda dve, link: rsqrt(dve, link, w.rstd[:], w.mv[:, :, 1], t1[:], t2[:])
    return memory


def attention1(nc, w, bank, kv):
    with Memory(nc, "attention1") as m:
        HI, LO, MAX = 0, 1, 2
        keys = m.sb("keys", [D, 2, 3, KV], FP16)
        th, tl = m.sb("th", [D, G, HG, S], FP16), m.sb("tl", [D, G, HG, S], FP16)
        negmax = m.sb("negmax", [S, G, HG], FP16)
        probs_l, probs_c = m.sb("probs_l", [S, 2, HG, S]), m.sb("probs_c", [C, 2, HG, S])
        vals_l, vals_c = m.sb("vals_l", [S, 2, H, DK1 + 1]), m.sb("vals_c", [C, 2, H, DK1 + 1])
        recip = m.sb("recip", [S, HG])
        heads_out = m.sb("heads_out", [S, 2, H, DK1])
        turned_h, turned_l = m.sb("turned_h", [D, H // 2, S], FP16), m.sb("turned_l", [D, H // 2, S], FP16)
        zn, new, bn, mv, rstd = (m.sb("zn", [S, D]), m.sb("new", [S, 1, D]), m.sb("bn", [S, 6]), m.sb("mv", [S, 1, 2]),
                                 m.sb("rstd", [S, 1]))
        t1, t2 = m.sb("t1", [S, 1]), m.sb("t2", [S, 1])
        (ones_in, staged, t_done, t_hi, t_lo, scored, maxed, shifted, exped, v_done, v_out, mixed, normed, turned, ot_hi,
         ot_lo, projected, out_normed, biased, nchain, chain, waited) = (
            m.sem(n) for n in ("ones_in", "staged", "t_done", "t_hi", "t_lo", "scored", "maxed", "shifted", "exped",
                               "v_done", "v_out", "mixed", "normed", "turned", "ot_hi", "ot_lo", "projected",
                               "out_normed", "biased", "nchain", "chain", "waited"))
        block = m.block()
        t_bank = bank[0][:, :].rearrange("p (h s) -> p h s", s=S)
        score = [bank[1 + i][:, 0:2 * KV].rearrange("p (h k) -> p h k", k=KV) for i in range(2)]
        by_key_l = bank[3][:, :].rearrange("p (h s) -> p h s", s=S)
        by_key_c = bank[4][0:C, :].rearrange("p (h s) -> p h s", s=S)
        mix = bank[5][:, 0:HG * (DK1 + 1)].rearrange("p (h k) -> p h k", k=DK1 + 1)
        VW = HG * DK1
        v_l, v_c = bank[6][:, 0:VW], bank[6][0:C, VW:2 * VW]
        out_t = bank[7][:, :].rearrange("p (t s) -> p t s", s=S)
        out_p = bank[7][:, 0:D]
        LAT, CTX = slice(0, S), slice(S, KV)

        def after(b, g, u, n):
            return (b, g + n, u) if g + n < G else (b + 1, g + n - G, 1 - u)

        def before(b, g, u):
            return (b, g - 1, u) if g > 0 else (b - 1, G - 1, 1 - u)

        def sequences(eng, body):
            body(0, 0, True, False)
            with eng.Fori(0, (B - 2) // 2) as i:
                body(i * 2 + 1, 1, False, False)
                body(i * 2 + 2, 0, False, False)
            body(B - 1, (B - 1) % 2, False, True)

        @block.gpsimd
        def _(pool):
            def stage(b, u):
                pool.tensor_copy(keys[:, u].rearrange("p v k -> p (v k)"),
                                 kv[:, bass.ds(b, 1), :, :].rearrange("p o v k -> p (o v k)")).then_inc(staged, 1)

            def body(b, u, first, last):
                if not last:
                    if not first:
                        pool.wait_ge(shifted, b * G)
                    stage(b + 1, 1 - u)
                row = w.X[:, bass.ds(b, 1), :]
                pool.tensor_tensor(row, row, w.bias1[:].unsqueeze(1), ALU.add).then_inc(biased, 1)

            stage(0, 0)
            sequences(pool, body)

        @block.tensor
        def _(pe):
            def three(dst, pairs):
                for i, (x, y) in enumerate(pairs):
                    last = pe.matmul(dst, x, y, start=i == 0, stop=i == 2)
                return last

            def make_t(b, g, u):
                pe.wait_ge(staged, b + 1)
                if late(b * G + g):
                    pe.wait_ge(t_lo, b * G + g)
                for h in range(HG):
                    ah, al = w.ah[:, HG * g + h], w.al[:, HG * g + h]
                    last = three(t_bank[:, h], ((ah, keys[:, u, HI, LAT]), (al, keys[:, u, HI, LAT]), (ah, keys[:, u, LO, LAT])))
                last.then_inc(t_done, 1)

            def scores(b, g, u):
                pe.wait_ge(t_hi, b * G + (g + 1))
                if late(b * G + g):
                    pe.wait_ge(maxed, b * G + g)
                for h in range(HG):
                    last = pe.matmul(score[h // 2][:, h % 2], th[:, g, h], keys[:, u, MAX], start=True, stop=True)
                last.then_inc(scored, 1)

            def scores_by_key(b, g, u):
                pe.wait_ge(t_lo, b * G + (g + 1))
                pe.wait_ge(maxed, b * G + (g + 1))
                if late(b * G + g):
                    pe.wait_ge(exped, b * G + g)
                for dst, part, width in ((by_key_l, LAT, S), (by_key_c, CTX, C)):
                    kh, kl = keys[:, u, HI, part], keys[:, u, LO, part]
                    for h in range(HG):
                        pe.matmul(dst[:, h], kh, th[:, g, h], start=True, stop=False)
                        pe.matmul(dst[:, h], kl, th[:, g, h], start=False, stop=False)
                        pe.matmul(dst[:, h], kh, tl[:, g, h], start=False, stop=False)
                        last = pe.matmul(dst[:, h], negmax[:, g, h:h + 1].broadcast_to([S, width]), w.identh[:],
                                         start=False, stop=True)
                last.then_inc(shifted, 1)

            def mix_values(b, g, u):
                pe.wait_ge(exped, b * G + (g + 1))
                pe.wait_ge(v_out, b * G + (g + 1))
                if late(b * G + g):
                    pe.wait_ge(normed, b * G + g)
                for h in range(HG):
                    pe.matmul(mix[:, h], probs_l[:, g % 2, h], vals_l[:, u, HG * g + h], start=True, stop=False)
                    last = pe.matmul(mix[:, h], probs_c[:, g % 2, h], vals_c[:, u, HG * g + h], start=False, stop=True)
                last.then_inc(mixed, 1)

            def values(b, g, u):
                pe.wait_ge(staged, b + 1)
                if late(b * G + g):
                    pe.wait_ge(v_out, b * G + g)
                cols = slice(VW * g, VW * g + VW)
                for dst, part in ((v_l, LAT), (v_c, CTX)):
                    kh, kl = keys[:, u, HI, part], keys[:, u, LO, part]
                    last = three(dst, ((kh, w.v1h[:, cols]), (kh, w.v1l[:, cols]), (kl, w.v1h[:, cols])))
                last.then_inc(v_done, 1)

            def turn(t, half, u):
                pe.wait_ge(normed, t * G + (2 + 2 * half))
                if half == 1:
                    pe.wait_ge(ot_lo, t * 2 + 1)
                elif late(t):
                    pe.wait_ge(out_normed, t)
                for i in range(4):
                    h = 2 * (4 * half + i)
                    last = pe.transpose(out_t[:, i], heads_out[:, u, h:h + 2].rearrange("p h k -> p (h k)"), w.ident[:])
                last.then_inc(turned, 1)

            def project(t):
                pe.wait_ge(ot_lo, t * 2 + 2)
                for i in range(H // 2):
                    for j, (x, wt) in enumerate(((turned_h, w.o1h), (turned_h, w.o1l), (turned_l, w.o1h))):
                        last = pe.matmul(out_p, x[:, i], wt[:, i], start=i == 0 and j == 0, stop=i == H // 2 - 1 and j == 2)
                last.then_inc(projected, 1)

            def body(b, u, first, last):
                for g in range(G):
                    scores_by_key(b, g, u)
                    if not (last and g + 2 >= G):
                        make_t(*after(b, g, u, 2))
                    if not (last and g + 1 >= G):
                        scores(*after(b, g, u, 1))
                    if not (first and g == 0):
                        mix_values(*before(b, g, u))
                    if not last:
                        values(b + 1, g, 1 - u)
                    if not first and g > 0:
                        if g < 3:
                            turn(b - 1, g - 1, 1 - u)
                        else:
                            project(b - 1)

            make_t(0, 0, 0)
            make_t(0, 1, 0)
            scores(0, 0, 0)
            pe.wait_ge(ones_in, 2)
            for g in range(G):
                values(0, g, 0)
            sequences(pe, body)
            end = (B - 1) % 2
            mix_values(B - 1, G - 1, end)
            turn(B - 1, 0, end)
            turn(B - 1, 1, end)
            project(B - 1)

        @block.scalar
        def _(act):
            def t_high(b, g, u):
                act.wait_ge(t_done, b * G + (g + 1))
                act.activation(th[:, g], t_bank, ACT.Copy, scale=1.0 / AS).then_inc(t_hi, 1)

            def exp(b, g, u):
                act.wait_ge(shifted, b * G + (g + 1))
                if late(b * G + g, 2):
                    act.wait_ge(mixed, b * G + (g - 1))
                act.activation(probs_l[:, g % 2], by_key_l, ACT.Exp)
                act.activation(probs_c[:, g % 2], by_key_c, ACT.Exp, bias=w.mask_bias[:, 0, bass.ds(b, 1)]).then_inc(exped, 1)

            def values_out(b, g, u):
                act.wait_ge(v_done, b * G + (g + 1))
                if late(b, 2) and g == 0:
                    act.wait_ge(mixed, (b - 1) * G)
                for dst, src in ((vals_l, v_l), (vals_c, v_c)):
                    last = act.activation(dst[:, u, HG * g:HG * g + HG, 0:DK1], src.rearrange("p (h k) -> p h k", k=DK1),
                                          ACT.Copy, scale=1.0 / WS)
                last.then_inc(v_out, 1)

            def out_high(t, half):
                act.wait_ge(turned, t * 2 + (half + 1))
                if late(t) and half == 0:
                    act.wait_ge(projected, t)
                act.activation(turned_h[:, 4 * half:4 * half + 4], out_t, ACT.Copy).then_inc(ot_hi, 1)

            def body(b, u, first, last):
                for g in range(G):
                    exp(b, g, u)
                    if not (last and g + 2 >= G):
                        t_high(*after(b, g, u, 2))
                    if not last:
                        values_out(b + 1, g, 1 - u)
                    if not first and g in (1, 2):
                        out_high(b - 1, g - 1)

            t_high(0, 0, 0)
            t_high(0, 1, 0)
            for g in range(G):
                values_out(0, g, 0)
            sequences(act, body)
            out_high(B - 1, 0)
            out_high(B - 1, 1)

        @block.vector
        def _(dve):
            def t_low(b, g, u):
                dve.wait_ge(t_hi, b * G + (g + 1))
                dve.scalar_tensor_tensor(tl[:, g].rearrange("p h s -> p (h s)"), bank[0][:, :], 1.0 / AS,
                                         th[:, g].rearrange("p h s -> p (h s)"), ALU.mult, ALU.subtract).then_inc(t_lo, 1)

            def maximum(b, g, u):
                dve.wait_ge(scored, b * G + (g + 1))
                for i in range(2):
                    last = dve.tensor_reduce(negmax[:, g, 2 * i:2 * i + 2], score[i], AX.X, ALU.max, negate=True)
                last.then_inc(maxed, 1)

            def normalise(b, g, u):
                dve.wait_ge(mixed, b * G + (g + 1))
                dve.reciprocal(recip[:], mix[:, :, DK1]).then_inc(nchain, 1)
                dve.wait_ge(nchain, b * G + (g + 1))
                if late(b, 2) and g == 0:
                    dve.wait_ge(turned, (b - 1) * 2)
                dve.tensor_tensor(heads_out[:, u, HG * g:HG * g + HG], mix[:, :, 0:DK1],
                                  recip[:].unsqueeze(2).broadcast_to([S, HG, DK1]), ALU.mult).then_inc(normed, 1)

            def out_low(t, half):
                dve.wait_ge(ot_hi, t * 2 + (half + 1))
                dve.tensor_tensor(turned_l[:, 4 * half:4 * half + 4], out_t, turned_h[:, 4 * half:4 * half + 4],
                                  ALU.subtract).then_inc(ot_lo, 1)

            LINKS = RSQRT_LINKS + 6

            def residual(t):
                row = w.X[:, bass.ds(t, 1), :]
                link = linker(dve, chain, t * LINKS)
                dve.wait_ge(projected, t + 1)
                link(dve.bn_stats(bn[:], out_p))
                dve.sem_inc(waited, 1)
                link(dve.bn_aggr(mv[:, 0], bn[:]))
                rsqrt(dve, link, rstd[:], mv[:, 0, 1:2], t1[:], t2[:], 1.0 / (WS * WS))
                dve.tensor_scalar(zn[:], out_p, mv[:, 0, 0:1], rstd[:], ALU.subtract, ALU.mult).then_inc(out_normed, 1)
                dve.wait_ge(out_normed, t + 1)
                link(dve.tensor_tensor(zn[:], zn[:], w.gain1[:], ALU.mult))
                dve.wait_ge(biased, t + 1)
                link(dve.tensor_tensor(new[:], zn[:].unsqueeze(1), row, ALU.add))
                link(dve.bn_stats(bn[:], new[:, 0]))
                dve.sem_inc(waited, 1)
                dve.tensor_copy(row, new[:])
                link(dve.bn_aggr(mv[:, 0], bn[:]))
                dve.sem_inc(waited, 1)
                dve.tensor_copy(w.mv[:, bass.ds(t, 1), :], mv[:])

            def body(b, u, first, last):
                for g in range(G):
                    if not (last and g + 2 >= G):
                        t_low(*after(b, g, u, 2))
                    if not (last and g + 1 >= G):
                        maximum(*after(b, g, u, 1))
                    if not (first and g == 0):
                        normalise(*before(b, g, u))
                    if not first and g in (1, 2):
                        out_low(b - 1, g - 1)
                    if not first and g == 3:
                        residual(b - 1)

            dve.memset(vals_l[:, :, :, DK1:DK1 + 1], 1.0).then_inc(ones_in, 1)
            dve.memset(vals_c[:, :, :, DK1:DK1 + 1], 1.0).then_inc(ones_in, 1)
            t_low(0, 0, 0)
            t_low(0, 1, 0)
            maximum(0, 0, 0)
            sequences(dve, body)
            end = (B - 1) % 2
            normalise(B - 1, G - 1, end)
            out_low(B - 1, 0)
            out_low(B - 1, 1)
            residual(B - 1)


def mixture(nc, a, w, bank, xh, xl):
    with Memory(nc, "mixture") as m:
        xs = m.sb("xs", [D, 2, 2, N], FP16)
        tanh, half = m.sb("tanh", [128, MH, N]), m.sb("half", [128, MH, N])
        hidden = m.sb("hidden", [128, 2, MH, N])
        part = m.sb("part", [S, 2, CH, D])
        gate2, gate = m.sb("gate2", [S, CH, 2, E]), m.sb("gate", [S, CH, E])
        top, index = m.sb("top", [S, CH, 8]), m.sb("index", [S, CH, 8], UINT32)
        chosen = m.sb("chosen", [S, CH, 2])
        diff, expd, p1, p2 = (m.sb(n, [S, CH]) for n in ("diff", "expd", "p1", "p2"))
        is1, is2 = m.sb("is1", [S, CH, E]), m.sb("is2", [S, CH, E])
        weight = m.sb("weight", [S, 2, CH, E])
        staged, gated, diffed, gexped, weighed, h_done, tanhed, halved, hid_in, y_done, combined, added, chain, stored, waited, pool_waited = (
            m.sem(n) for n in ("staged", "gated", "diffed", "gexped", "weighed", "h_done", "tanhed", "halved", "hid_in",
                               "y_done", "combined", "added", "chain", "stored", "waited", "pool_waited"))
        block = m.block()
        h1, h2 = [bank[i][:, :] for i in (0, 1)], [bank[i][:, :] for i in (2, 3)]
        y = [bank[4 + i][:, :].rearrange("p (c d) -> p c d", d=D) for i in range(2)]
        gates = bank[6][:, 0:CH * 2 * E]

        def chunks(eng, body):
            body(0, 0)
            with eng.Fori(0, (NCH - 2) // 2) as i:
                body(i * 2 + 1, 1)
                body(i * 2 + 2, 0)
            body(NCH - 1, (NCH - 1) % 2)

        def within(k):
            return not isinstance(k, int) or k + 1 < NCH

        @block.gpsimd
        def _(pool):
            def stage(k, u):
                chunk = bass.ds(k * CH, CH)
                for i, x in enumerate((xh, xl)):
                    last = pool.tensor_copy(xs[:, u, i].rearrange("p (c s) -> p c s", s=S), x[:, chunk, :])
                last.then_inc(staged, 1)

            def add(k, e):
                n = k * E + e
                rows = w.X[:, bass.ds(k * CH, CH), :]
                pool.wait_ge(combined, n + 1)
                if late(n):
                    pool.wait_ge(added, n)
                pool.sem_inc(pool_waited, 1)
                pool.tensor_tensor(rows, rows, part[:, e % 2], ALU.add).then_inc(added, 1)

            def body(k, u):
                for e in range(E):
                    if e > 0:
                        add(k, e - 1)
                    elif late(k):
                        add(k - 1, E - 1)
                    if e == 0 and within(k):
                        if late(k):
                            pool.wait_ge(h_done, k * (E * MH))
                        stage(k + 1, 1 - u)

            stage(0, 0)
            chunks(pool, body)
            add(NCH - 1, E - 1)

        @block.sync
        def _(sp):
            with sp.Fori(0, NCH) as i:
                chunk = bass.ds(i * CH, CH)
                sp.wait_ge(added, i * E + E)
                sp.dma_start(a["out"].rearrange("b s d -> s b d")[:, chunk, :], w.X[:, chunk, :]).then_inc(stored, 16)
            sp.wait_ge(stored, 16 * NCH)

        @block.tensor
        def _(pe):
            def choose(k, u):
                pe.wait_ge(staged, k + 1)
                for c in range(CH):
                    dst = gates[:, 2 * E * c:2 * E * c + 2 * E]
                    for i in range(2):
                        last = pe.matmul(dst, xs[:, u, i, S * c:S * c + S], w.wgt[:].rearrange("p i e -> p (i e)"),
                                         start=i == 0, stop=i == 1)
                last.then_inc(gated, 1)

            def rise(k, u, e, j):
                n = k * (E * MH) + (MH * e + j)
                if e == 0 and j == 0:
                    pe.wait_ge(staged, k + 1)
                if late(n, 2):
                    pe.wait_ge(hid_in, n - 1)
                for dst, i in ((h1[j], 0), (h2[j], 1)):
                    wh, wl = w.moeh[:, i, MH * e + j], w.moel[:, i, MH * e + j]
                    pe.matmul(dst, wh, xs[:, u, 0], start=True, stop=False)
                    pe.matmul(dst, wl, xs[:, u, 0], start=False, stop=False)
                    last = pe.matmul(dst, wh, xs[:, u, 1], start=False, stop=True)
                last.then_inc(h_done, 1)

            def fall(k, e):
                n = k * E + e
                pe.wait_ge(hid_in, n * MH + MH)
                if late(n, 2):
                    pe.wait_ge(combined, n - 1)
                for c in range(CH):
                    for j in range(MH):
                        last = pe.matmul(y[e % 2][:, c], hidden[:, e % 2, j, S * c:S * c + S], w.w3t[:, MH * e + j],
                                         start=j == 0, stop=j == MH - 1)
                last.then_inc(y_done, 1)

            def body(k, u):
                for e in range(E):
                    for j in range(MH):
                        rise(k, u, e, j)
                    if e > 0:
                        fall(k, e - 1)
                    elif late(k):
                        fall(k - 1, E - 1)
                    if e == 4 and within(k):
                        choose(k + 1, 1 - u)

            choose(0, 0)
            chunks(pe, body)
            fall(NCH - 1, E - 1)

        @block.scalar
        def _(act):
            def gate_exp(k):
                act.wait_ge(diffed, k + 1)
                act.activation(expd[:], diff[:], ACT.Exp).then_inc(gexped, 1)

            def body(k, u):
                for e in range(E):
                    for j in range(MH):
                        n = k * (E * MH) + (MH * e + j)
                        act.wait_ge(h_done, n + 1)
                        if late(n, 2):
                            act.wait_ge(halved, n - 1)
                        act.activation(tanh[:, j], h1[j], ACT.Tanh, scale=0.5 / WS).then_inc(tanhed, 1)
                    if e == 5 and within(k):
                        gate_exp(k + 1)

            gate_exp(0)
            chunks(act, body)

        @block.vector
        def _(dve):
            GATE_LINKS = 13

            def gates_in(k):
                link = linker(dve, chain, k * GATE_LINKS)
                dve.wait_ge(gated, k + 1)
                link(dve.tensor_scalar(gate2[:].rearrange("p c i e -> p (c i e)"), gates, 1.0 / WS, None, ALU.mult))
                link(dve.tensor_tensor(gate[:], gate2[:, :, 0], gate2[:, :, 1], ALU.add))
                dve.sem_inc(waited, 1)
                for c in range(CH):
                    last = dve.max(top[:, c], gate[:, c])
                link(last)
                dve.sem_inc(waited, 1)
                for c in range(CH):
                    last = dve.max_index(index[:, c], top[:, c], gate[:, c])
                link(last)
                link(dve.tensor_copy(chosen[:], index[:, :, 0:2]))
                dve.tensor_tensor(diff[:], top[:, :, 1], top[:, :, 0], ALU.subtract).then_inc(diffed, 1)

            def weigh(k, u):
                link = linker(dve, chain, k * GATE_LINKS + 5)
                dve.wait_ge(gexped, k + 1)
                link(dve.tensor_scalar(p1[:], expd[:], 1.0, None, ALU.add))
                link(dve.reciprocal(p1[:], p1[:]))
                link(dve.tensor_scalar(p1[:], p1[:], w.moe_out[:], None, ALU.mult))
                link(dve.tensor_scalar(p2[:], p1[:], -1.0, w.moe_out[:], ALU.mult, ALU.add))
                for dst, i in ((is1, 0), (is2, 1)):
                    link(dve.tensor_tensor(dst[:], w.iota[:].unsqueeze(1).broadcast_to([S, CH, E]),
                                           chosen[:, :, i:i + 1].broadcast_to([S, CH, E]), ALU.is_equal))
                    link(dve.tensor_tensor(dst[:], dst[:], (p1, p2)[i][:].unsqueeze(2).broadcast_to([S, CH, E]), ALU.mult))
                dve.tensor_tensor(weight[:, u], is1[:], is2[:], ALU.add).then_inc(weighed, 1)
                dve.wait_ge(weighed, k + 1)

            def hide(k, e, j):
                n = k * (E * MH) + (MH * e + j)
                dve.wait_ge(tanhed, n + 1)
                dve.scalar_tensor_tensor(half[:, j], tanh[:, j], 1.0, h1[j], ALU.add, ALU.mult).then_inc(halved, 1)
                dve.wait_ge(halved, n + 1)
                if j == 0 and late(k * E + e, 2):
                    dve.wait_ge(y_done, k * E + (e - 1))
                dve.tensor_tensor(hidden[:, e % 2, j], half[:, j], h2[j], ALU.mult).then_inc(hid_in, 1)

            def combine(k, u, e):
                n = k * E + e
                dve.wait_ge(y_done, n + 1)
                if late(n, 2):
                    dve.wait_ge(added, n - 1)
                dve.tensor_tensor(part[:, e % 2], y[e % 2], weight[:, u, :, e:e + 1].broadcast_to([S, CH, D]),
                                  ALU.mult).then_inc(combined, 1)

            def body(k, u):
                for e in range(E):
                    for j in range(MH):
                        hide(k, e, j)
                    if e > 0:
                        combine(k, u, e - 1)
                    elif late(k):
                        combine(k - 1, 1 - u, E - 1)
                    if e == 5 and within(k):
                        gates_in(k + 1)
                    if e == 6 and within(k):
                        weigh(k + 1, 1 - u)

            gates_in(0)
            weigh(0, 0)
            chunks(dve, body)
            combine(NCH - 1, (NCH - 1) % 2, E - 1)


def flamingo(nc, a):
    with ExitStack() as stack:
        def sb(name, shape, dt=FP32):
            return stack.enter_context(nc.sbuf_tensor(name, shape, dt))

        w = Weights()
        bank = [stack.enter_context(nc.psum_tensor(f"bank{i}", [128, 512], FP32)) for i in range(8)]
        w.X = sb("X", [S, B, D])
        w.mv, w.rstd = sb("mv", [S, B, 2]), sb("rstd", [S, B])
        w.mv_c, w.rstd_c = sb("mv_c", [C, B, 2]), sb("rstd_c", [C, B])
        w.ident, w.identh = sb("ident", [128, 128]), sb("identh", [128, 128], FP16)
        w.head_rows = sb("head_rows", [R0, HG], FP16)
        w.iota = sb("iota", [128, E])
        w.mask01, w.mask_bias = sb("mask01", [128, B, C], FP16), sb("mask_bias", [C, 1, B])
        w.q0h, w.q0l, w.k0h, w.k0l = (sb(n, [D, G, 3, 32], FP16) for n in ("q0h", "q0l", "k0h", "k0l"))
        w.v0h, w.v0l = sb("v0h", [D, D], FP16), sb("v0l", [D, D], FP16)
        w.o0h, w.o0l = sb("o0h", [D, 1, D], FP16), sb("o0l", [D, 1, D], FP16)
        w.bias0, w.tg0 = sb("bias0", [128, D]), sb("tg0", [128, 1])
        w.taph, w.tapl = sb("taph", [D, 3, M0, 128], FP16), sb("tapl", [D, 3, M0, 128], FP16)
        w.conv_b, w.conv_b_half = sb("conv_b", [128, M0]), sb("conv_b_half", [128, M0])
        w.w2t, w.ffn_out = sb("w2t", [128, M0, D], FP16), sb("ffn_out", [128, 1])
        w.gb = sb("gb", [D, 4])
        w.ah, w.al = sb("ah", [D, H, D], FP16), sb("al", [D, H, D], FP16)
        w.v1h, w.v1l = sb("v1h", [D, H * DK1], FP16), sb("v1l", [D, H * DK1], FP16)
        w.o1h, w.o1l = sb("o1h", [128, H // 2, D], FP16), sb("o1l", [128, H // 2, D], FP16)
        w.gain1, w.bias1 = sb("gain1", [128, D]), sb("bias1", [128, D])
        w.wgt = sb("wgt", [D, 2, E], FP16)
        w.moeh, w.moel = sb("moeh", [D, 2, E * MH, 128], FP16), sb("moel", [D, 2, E * MH, 128], FP16)
        w.w3t, w.moe_out = sb("w3t", [128, E * MH, D]), sb("moe_out", [128, 1])

        with ExitStack() as ctx_stack:
            w.ctx = ctx_stack.enter_context(nc.sbuf_tensor("ctx", [C, B, D], FP32))
            setup(nc, a, w, bank)
            with Memory(nc, "layer0") as m:
                xh, xl = m.sb("xh", [D, B, S], FP16), m.sb("xl", [D, B, S], FP16)
                ch, cl = m.sb("ch", [D, B, C], FP16), m.sb("cl", [D, B, C], FP16)
                qst, kst = m.sb("qst", [R0, G, B, S], FP16), m.sb("kst", [R0, G, B, C], FP16)
                vals = m.sb("vals", [C, B, H, DK0 + 1])
                split_transposed(nc, w, bank, "ctx0", C, w.ctx, lambda c: ch[:, c, :], lambda c: cl[:, c, :])
                split_transposed(nc, w, bank, "x0", S, w.X, lambda c: xh[:, c, :], lambda c: xl[:, c, :], w.mv, w.rstd)
                project0(nc, w, bank, xh, xl, ch, cl, qst, kst, vals)
                attention0(nc, w, bank, qst, kst, vals)
            feed_forward0(nc, w, bank)
            with Memory(nc, "layer1") as m:
                kv = m.sb("kv", [D, B, 3, KV], FP16)
                gain_l, bias_l, gain_x, bias_x = (w.gb[:, i:i + 1] for i in range(4))
                split_transposed(nc, w, bank, "ctx1", C, w.ctx, lambda c: kv[:, c, 0, S:KV], lambda c: kv[:, c, 1, S:KV],
                                 w.mv_c, w.rstd_c, gain_x, bias_x)
                split_transposed(nc, w, bank, "x1", S, w.X, lambda c: kv[:, c, 0, 0:S], lambda c: kv[:, c, 1, 0:S],
                                 w.mv, w.rstd, gain_l, bias_l, latent_scale(w))
                mask_keys(nc, w, kv)
                attention1(nc, w, bank, kv)
        with Memory(nc, "moe") as m:
            xh, xl = m.sb("xh", [D, B, S], FP16), m.sb("xl", [D, B, S], FP16)
            split_transposed(nc, w, bank, "x2", S, w.X, lambda c: xh[:, c, :], lambda c: xl[:, c, :], w.mv, w.rstd,
                             before=row_scale(w))
            mixture(nc, a, w, bank, xh, xl)


_INS = {'x': 'x', 'ctx': 'ctx_1024', 'mask': 'mask_BxS2_bf1', 'gx': 'g_xattn', 'gf': 'g_ffn',
        'q0': 'L0_xattn_W_q', 'k0': 'L0_xattn_W_k', 'v0': 'L0_xattn_W_v', 'o0': 'L0_xattn_W_o', 'bo0': 'L0_xattn_b_o',
        'fw1': 'L0_ffn_w1', 'cw': 'L0_ffn_conv_w', 'cb': 'L0_ffn_conv_b', 'fw2': 'L0_ffn_w2',
        'gx1': 'L1_xattn_g_x', 'bx1': 'L1_xattn_b_x', 'gl1': 'L1_xattn_g_l', 'bl1': 'L1_xattn_b_l',
        'q1': 'L1_xattn_Wq', 'kv1': 'L1_xattn_Wkv', 'o1': 'L1_xattn_Wout', 'go1': 'L1_xattn_g_o', 'bo1': 'L1_xattn_b_o',
        'wg': 'L1_ffn_Wg', 'w1': 'L1_ffn_W1', 'w2': 'L1_ffn_W2', 'w3': 'L1_ffn_W3'}


def kernel(**inputs):
    import numpy as _np
    import concourse.bacc as _bacc
    from concourse import mybir as _mybir
    from concourse.bass_utils import run_bass_kernel_spmd as _run

    nc = _bacc.Bacc("TRN2", target_bir_lowering=False, num_devices=1)
    arrays, aps = {}, {}
    for short, name in _INS.items():
        v = _np.ascontiguousarray(inputs[name])
        if v.dtype == _np.bool_:
            v = v.view(_np.uint8)
        arrays[f"in_{short}"] = v
        aps[short] = nc.dram_tensor(f"in_{short}", v.shape, _mybir.dt.from_np(v.dtype), kind="ExternalInput").ap()
    aps["out"] = nc.dram_tensor("out", (B, S, D), _mybir.dt.float32, kind="ExternalOutput").ap()
    flamingo(nc, aps)
    r = _run(nc, [arrays], core_ids=[0])
    return r.results[0]["out"]
```

```python
import concourse.bass as bass
from concourse import mybir
from contextlib import ExitStack

FP32 = mybir.dt.float32
FP16 = mybir.dt.float16
INT32 = mybir.dt.int32
UINT32 = mybir.dt.uint32
UINT8 = mybir.dt.uint8
ALU = mybir.AluOpType
ACT = mybir.ActivationFunctionType
AX = mybir.AxisListType

B, S, D = 32, 128, 128
C = 77
H = 16
DK0 = D // H
DK1 = 64
G = 4
HG = H // G
KV = S + C
HID = 512
M0 = HID // 128
E, MH = 8, 2
R0 = 3 * HG * DK0
CH = 4
NCH = B // CH
N = CH * S
EPS = 1e-5
ROUND = 1.5 * 2.0 ** 23
WS = 64.0
AS = 1024.0
MASKED = -30000.0


class Weights:
    pass


def late(x, least=1):
    return not isinstance(x, int) or x >= least


def rsqrt(dve, link, out, var, t1, t2, scale=1.0):
    link(dve.tensor_scalar(t1, var, scale, EPS, ALU.mult, ALU.add))
    link(dve.tensor_single_scalar(t2.bitcast(INT32), t1.bitcast(INT32), 1, ALU.arith_shift_right))
    link(dve.tensor_scalar(out.bitcast(INT32), t2.bitcast(INT32), -1.0, float(0x5F3759DF), ALU.mult, ALU.add))
    for _ in range(3):
        link(dve.scalar_tensor_tensor(t2, out, -0.5, out, ALU.mult, ALU.mult))
        link(dve.tensor_tensor(t2, t2, t1, ALU.mult))
        link(dve.scalar_tensor_tensor(out, t2, 1.5, out, ALU.add, ALU.mult))


def row_statistics(dve, link, w, bn):
    for b in range(B):
        last = dve.bn_stats(bn[:, b], w.X[:, b])
    link(last)
    for b in range(B):
        last = dve.bn_aggr(w.mv[:, b], bn[:, b])
    link(last)


def linker(eng, sem, base=0):
    n = [0]

    def link(ins):
        n[0] += 1
        ins.then_inc(sem, 1)
        eng.wait_ge(sem, base + n[0])
    return link


class Memory:

    def __init__(self, nc, tag):
        self.nc, self.tag, self.stack = nc, tag, ExitStack()

    def __enter__(self):
        return self

    def __exit__(self, *e):
        return self.stack.__exit__(*e)

    def sb(self, name, shape, dt=FP32):
        return self.stack.enter_context(self.nc.sbuf_tensor(f"{self.tag}_{name}", shape, dt))

    def sem(self, name):
        return self.stack.enter_context(self.nc.semaphore(f"{self.tag}_{name}"))

    def block(self):
        return self.stack.enter_context(self.nc.Block())


def setup(nc, a, w, bank):
    with Memory(nc, "setup") as m:
        nat_q0, nat_k0, nat_v0 = (m.sb(n, [128, D]) for n in ("nat_q0", "nat_k0", "nat_v0"))
        nat_o0 = m.sb("nat_o0", [128, 1, D])
        nat_f = m.sb("nat_f", [128, 2, HID])
        conv_w, conv_b = m.sb("conv_w", [128, M0, 3]), w.conv_b
        nat_q1, nat_k1, nat_v1 = (m.sb(n, [128, H * DK1]) for n in ("nat_q1", "nat_k1", "nat_v1"))
        nat_o1 = m.sb("nat_o1", [128, H // 2, D])
        nat_moe = m.sb("nat_moe", [128, 2, E * MH, D])
        nat_w3 = m.sb("nat_w3", [128, E * MH, D])
        nat_g = m.sb("nat_g", [E, 1, D])
        mask_u8, mask_f = m.sb("mask_u8", [B, C], UINT8), m.sb("mask_f", [B, 1, C])
        mask_rows = m.sb("mask_rows", [128, B * C], UINT8)
        gates, tanhs = m.sb("gates", [128, 4]), m.sb("tanhs", [128, 4])
        rows = m.sb("rows", [128, 3, D])
        bn = m.sb("bn", [128, B, 6])
        bn_c, mv_c = m.sb("bn_c", [C, B, 6]), m.sb("mv_c", [C, B, 2])
        absum, wmean, winv = m.sb("absum", [128, 2]), m.sb("wmean", [128, 2]), m.sb("winv", [128, 2])
        ones = m.sb("ones", [128, 128])
        cs = m.sb("cs", [128, M0, 3])
        tap_w = m.sb("tap_w", [128, 3, M0, D])
        q1t, k1t = m.sb("q1t", [128, H // 2, D]), m.sb("k1t", [128, H // 2, D])
        comp = m.sb("comp", [128, 4, D], FP16)
        t1, t2 = m.sb("t1", [128, B]), m.sb("t2", [128, B])
        iota_i = m.sb("iota_i", [128, E], INT32)

        x_in = [m.sem(f"x_in{i}") for i in range(4)]
        ctx_in, l0_in, ffn_in, l1_in, moe_in, small_in = (
            m.sem(n) for n in ("ctx_in", "l0_in", "ffn_in", "l1_in", "moe_in", "small_in"))
        made, tanh_done, summed, quant_done, chain, tiles_done, hi_done, lo_done, plain_hi, plain_lo, mask_done, pchain = (
            m.sem(n) for n in ("made", "tanh_done", "summed", "quant_done", "chain", "tiles_done", "hi_done",
                               "lo_done", "plain_hi", "plain_lo", "mask_done", "pchain"))
        block = m.block()

        LD_L1, LD_MOE, LD_SMALL, QUANT, TAPS = range(5)
        tiles = []
        for i in range(2):
            tiles.append((nat_q1[:, 512 * i:512 * i + 512].rearrange("p (t n) -> p t n", n=128), LD_L1,
                          q1t[:, 4 * i:4 * i + 4, :], None, 1.0))
            tiles.append((nat_k1[:, 512 * i:512 * i + 512].rearrange("p (t n) -> p t n", n=128), LD_L1,
                          k1t[:, 4 * i:4 * i + 4, :], None, 1.0))
        tiles.append((nat_o0[:], LD_L1, w.o0h[:], w.o0l[:], WS))
        tiles.append((nat_g[:], LD_SMALL, w.wgt[:, 0:1, :], w.wgt[:, 1:2, :], WS))
        tiles.append((mask_f[:], LD_SMALL, w.mask_bias[:], None, 1.0))
        for t in range(3):
            tiles.append((tap_w[:, t], TAPS, w.taph[:, t], w.tapl[:, t], WS))
        tiles.append((nat_f[:, 1].rearrange("p (t n) -> p t n", n=128), QUANT, w.w2t[:], None, 1.0))
        for s in range(2):
            for i in range(4):
                tiles.append((nat_moe[:, s, 4 * i:4 * i + 4], LD_MOE, w.moeh[:, s, 4 * i:4 * i + 4],
                              w.moel[:, s, 4 * i:4 * i + 4], WS))
        for i in range(4):
            tiles.append((nat_w3[:, 4 * i:4 * i + 4], LD_MOE, w.w3t[:, 4 * i:4 * i + 4], None, 1.0))
        NT = len(tiles)
        NB = 6

        def lows(k):
            return sum(lo is not None for _, _, _, lo, _ in tiles[:k])

        def tile_bank(k, src):
            p, t, n = src.shape
            return bank[k % NB][0:n, 0:t * p].rearrange("q (t p) -> q t p", p=p)

        def product_bank(g):
            return bank[(NT + g) % NB][:, :].rearrange("q (t p) -> q t p", p=128)

        def product_heads(g):
            first = 2 * HG * (g // 2) + g % 2
            return slice(first, first + 2 * HG - 1, 2)

        @block.sync
        def _(sp):
            xv = a["x"].rearrange("b s d -> s b d")
            for i in range(4):
                sp.dma_start(w.X[:, 8 * i:8 * i + 8, :], xv[:, 8 * i:8 * i + 8, :]).then_inc(x_in[i], 16)
            sp.dma_start(w.ctx[:], a["ctx"].rearrange("b s d -> s b d")).then_inc(ctx_in, 16)
            for i, src in enumerate((a["w1"], a["w2"])):
                sp.dma_start(nat_moe[:, i], src.rearrange("e (m p) d -> p (e m) d", p=128)).then_inc(moe_in, 16)
            sp.dma_start(nat_w3[:].rearrange("p (e m) d -> p e m d", m=MH),
                         a["w3"].rearrange("e d (m h) -> d e m h", h=128)).then_inc(moe_in, 16)
            for s in (*x_in, ctx_in):
                sp.wait_ge(s, 16)
            sp.wait_ge(moe_in, 48)

        @block.scalar
        def _(act):
            act.dma_start(gates[:, 0:2], a["gx"].rearrange("(o n) -> o n", o=1).broadcast_to([128, 2])).then_inc(small_in, 16)
            act.dma_start(gates[:, 2:4], a["gf"].rearrange("(o n) -> o n", o=1).broadcast_to([128, 2])).then_inc(small_in, 16)
            act.dma_start(nat_f[:, 0].rearrange("p (m d) -> p m d", d=D),
                          a["fw1"].rearrange("(m p) d -> p m d", p=128)).then_inc(ffn_in, 16)
            act.dma_start(nat_f[:, 1], a["fw2"]).then_inc(ffn_in, 16)
            act.dma_start(conv_w[:], a["cw"].rearrange("(m p) o t -> p m (o t)", p=128)).then_inc(ffn_in, 16)
            act.dma_start(conv_b[:], a["cb"].rearrange("(m p) -> p m", p=128),
                          allow_slow_non_contiguous=True).then_inc(ffn_in, 16)
            act.dma_start(nat_q1[:], a["q1"]).then_inc(l1_in, 16)
            act.dma_start(nat_k1[:], a["kv1"][:, 0:H * DK1]).then_inc(l1_in, 16)
            act.dma_start(nat_v1[:], a["kv1"][:, H * DK1:]).then_inc(l1_in, 16)
            act.dma_start(nat_o1[:], a["o1"].rearrange("(t p) d -> p t d", p=128)).then_inc(l1_in, 16)
            act.dma_start(nat_o0[:, 0], a["o0"]).then_inc(l1_in, 16)
            for dst, src in ((nat_q0, a["q0"]), (nat_k0, a["k0"]), (nat_v0, a["v0"])):
                act.dma_start(dst[:].rearrange("d (h k) -> d h k", k=DK0), src.rearrange("h d k -> d h k")).then_inc(l0_in, 16)
            act.dma_start(nat_g[:, 0], a["wg"]).then_inc(small_in, 16)
            act.dma_start(mask_u8[:], a["mask"]).then_inc(small_in, 16)
            act.dma_start(mask_rows[:], a["mask"].rearrange("(o b) c -> o (b c)", o=1).broadcast_to([128, B * C])).then_inc(small_in, 16)
            for i, src in enumerate((a["bo0"], a["go1"], a["bo1"])):
                act.dma_start(rows[:, i], src.rearrange("(o n) -> o n", o=1).broadcast_to([128, D])).then_inc(small_in, 16)
            for i, src in enumerate((a["gl1"], a["bl1"], a["gx1"], a["bx1"])):
                act.dma_start(w.gb[:, i:i + 1], src.rearrange("(n o) -> n o", o=1)).then_inc(small_in, 16)
            act.wait_ge(small_in, 12 * 16)
            act.activation(tanhs[:], gates[:], ACT.Tanh).then_inc(tanh_done, 1)
            act.wait_ge(l0_in, 48)
            act.activation(comp[:, 0], nat_q0[:], ACT.Copy, scale=WS).then_inc(plain_hi, 1)
            act.activation(comp[:, 2], nat_k0[:], ACT.Copy, scale=WS).then_inc(plain_hi, 1)
            act.activation(w.v0h[:], nat_v0[:], ACT.Copy, scale=WS).then_inc(plain_hi, 1)
            act.wait_ge(l1_in, 80)
            act.activation(w.v1h[:], nat_v1[:], ACT.Copy, scale=WS).then_inc(plain_hi, 1)
            act.activation(w.o1h[:], nat_o1[:], ACT.Copy, scale=WS).then_inc(plain_hi, 1)
            for k, (src, _, hi, _, scale) in enumerate(tiles):
                act.wait_ge(tiles_done, k + 1)
                act.activation(hi, tile_bank(k, src), ACT.Copy, scale=scale).then_inc(hi_done, 1)
            for g in range(G):
                act.wait_ge(tiles_done, NT + g + 1)
                act.activation(w.ah[:, product_heads(g)], product_bank(g), ACT.Copy,
                               scale=AS * DK1 ** -0.5).then_inc(hi_done, 1)

        @block.tensor
        def _(pe):
            pe.wait_ge(made, 2)
            pe.wait_ge(summed, 1)
            pe.matmul(bank[7][:, 0:2], ones[:], absum[:], start=True, stop=True).then_inc(summed, 1)
            for k, (src, stage, _, _, _) in enumerate(tiles):
                if stage == LD_L1:
                    pe.wait_ge(l1_in, 80)
                elif stage == LD_MOE:
                    pe.wait_ge(moe_in, 48)
                elif stage == LD_SMALL:
                    pe.wait_ge(small_in, 12 * 16)
                    pe.wait_ge(mask_done, 1)
                elif stage == TAPS:
                    pe.wait_ge(quant_done, 2)
                elif stage == QUANT:
                    pe.wait_ge(quant_done, 1)
                if k >= NB:
                    pe.wait_ge(hi_done, k - NB + 1)
                    if lows(k - NB + 1):
                        pe.wait_ge(lo_done, lows(k - NB + 1))
                p, t, n = src.shape
                dst = tile_bank(k, src)
                for i in range(t):
                    last = pe.transpose(dst[:, i, :], src[:, i, :], w.ident[0:p, 0:p])
                last.then_inc(tiles_done, 1)
            pe.wait_ge(hi_done, 4)
            for g in range(G):
                pe.wait_ge(hi_done, NT + g - NB + 1)
                pe.wait_ge(lo_done, lows(NT + g - NB + 1))
                for i in range(HG):
                    half, t = slice(DK1 * (g % 2), DK1 * (g % 2) + DK1), HG * (g // 2) + i
                    last = pe.matmul(product_bank(g)[:, i, :], q1t[half, t, :], k1t[half, t, :],
                                     start=True, stop=True)
                last.then_inc(tiles_done, 1)

        @block.gpsimd
        def _(pool):
            link = linker(pool, pchain)
            link(pool.memset(w.ident[:], 0.0))
            link(pool.memset(w.identh[:], 0.0))
            pool.affine_select(out=w.ident[:], in_=w.ident[:], compare_op=ALU.not_equal, fill=1.0, base=0,
                               pattern=[[-1, 128]], channel_multiplier=1).then_inc(made, 1)
            pool.memset(ones[:], 1.0).then_inc(made, 1)
            pool.affine_select(out=w.identh[:], in_=w.identh[:], compare_op=ALU.not_equal, fill=1.0, base=0,
                               pattern=[[-1, 128]], channel_multiplier=1).then_inc(made, 1)
            link(pool.memset(w.head_rows[:], 0.0))
            for r in range(3):
                blk = w.head_rows[32 * r:32 * r + 32, :]
                link(pool.memset(blk, 1.0))
                link(pool.affine_select(out=blk, in_=blk, compare_op=ALU.is_ge, fill=0.0, base=0,
                                        pattern=[[-DK0, HG]], channel_multiplier=1))
                link(pool.affine_select(out=blk, in_=blk, compare_op=ALU.is_ge, fill=0.0, base=DK0 - 1,
                                        pattern=[[DK0, HG]], channel_multiplier=-1))
            link(pool.iota(iota_i[:], pattern=[[1, E]], base=0, channel_multiplier=0))
            link(pool.tensor_copy(w.iota[:], iota_i[:]))
            pool.wait_ge(small_in, 12 * 16)
            link(pool.tensor_copy(mask_f[:, 0], mask_u8[:]))
            pool.tensor_scalar(mask_f[:, 0], mask_f[:, 0], -1.0, -MASKED, ALU.add, ALU.mult).then_inc(mask_done, 1)
            pool.tensor_copy(w.mask01[:].rearrange("p b c -> p (b c)"), mask_rows[:]).then_inc(mask_done, 1)

        @block.vector
        def _(dve):
            link = linker(dve, chain)
            for b in range(B):
                if b % 8 == 0:
                    dve.wait_ge(x_in[b // 8], 16)
                last = dve.bn_stats(bn[:, b], w.X[:, b])
            link(last)
            for b in range(B):
                last = dve.bn_aggr(w.mv[:, b], bn[:, b])
            link(last)
            dve.wait_ge(ffn_in, 64)
            link(dve.tensor_reduce(absum[:], nat_f[:], AX.X, ALU.add, apply_absolute_value=True))
            dve.sem_inc(summed, 1)
            dve.wait_ge(summed, 2)
            link(dve.tensor_scalar(wmean[:], bank[7][:, 0:2], 1.0 / (HID * D), 1e-5, ALU.mult, ALU.max))
            link(dve.reciprocal(winv[:], wmean[:]))
            for i in (1, 0):
                link(dve.tensor_scalar(nat_f[:, i], nat_f[:, i], winv[:, i:i + 1], ROUND, ALU.mult, ALU.add))
                link(dve.tensor_scalar(nat_f[:, i], nat_f[:, i], ROUND, 1.0, ALU.subtract, ALU.min))
                ins = dve.tensor_scalar(nat_f[:, i], nat_f[:, i], -1.0, None, ALU.max)
                if i == 1:
                    ins.then_inc(quant_done, 1)
                else:
                    link(ins)
            link(dve.tensor_scalar(cs[:], conv_w[:], wmean[:, 0:1], None, ALU.mult))
            for t in range(3):
                for i in range(M0):
                    last = dve.tensor_scalar(tap_w[:, t, i], nat_f[:, 0, D * i:D * i + D], cs[:, i, t:t + 1], None, ALU.mult)
            link(last)
            dve.sem_inc(quant_done, 1)
            dve.tensor_scalar(w.conv_b_half[:], conv_b[:], 0.5, None, ALU.mult)
            dve.wait_ge(ctx_in, 16)
            for b in range(B):
                last = dve.bn_stats(bn_c[:, b], w.ctx[:, b])
            link(last)
            for b in range(B):
                last = dve.bn_aggr(mv_c[:, b], bn_c[:, b])
            link(last)
            rsqrt(dve, link, w.rstd[:], w.mv[:, :, 1], t1[:], t2[:])
            rsqrt(dve, link, w.rstd_c[:], mv_c[:, :, 1], t1[0:C], t2[0:C])
            dve.scalar_tensor_tensor(w.shift_c[:], mv_c[:, :, 0], -1.0, w.rstd_c[:], ALU.mult, ALU.mult)
            dve.wait_ge(tanh_done, 1)
            dve.tensor_scalar(w.tg0[:], tanhs[:, 0:1], 1.0 / WS, None, ALU.mult)
            dve.tensor_scalar(w.bias0[:], rows[:, 0], tanhs[:, 0:1], None, ALU.mult)
            dve.tensor_scalar(w.gain1[:], rows[:, 1], tanhs[:, 1:2], 1.0 / WS, ALU.mult, ALU.mult)
            dve.tensor_scalar(w.bias1[:], rows[:, 2], tanhs[:, 1:2], None, ALU.mult)
            link(dve.tensor_scalar(w.ffn_out[:], wmean[:, 1:2], 0.5, None, ALU.mult))
            link(dve.tensor_tensor(w.ffn_out[:], w.ffn_out[:], tanhs[:, 2:3], ALU.mult))
            dve.tensor_scalar(w.moe_out[:], tanhs[:, 3:4], 0.5 / (WS * WS), None, ALU.mult)
            dve.wait_ge(plain_hi, 5)
            dve.wait_ge(l0_in, 48)
            dve.wait_ge(l1_in, 80)
            link(dve.scalar_tensor_tensor(comp[:, 1], nat_q0[:], WS, comp[:, 0], ALU.mult, ALU.subtract))
            link(dve.scalar_tensor_tensor(comp[:, 3], nat_k0[:], WS, comp[:, 2], ALU.mult, ALU.subtract))
            dve.scalar_tensor_tensor(w.v0l[:], nat_v0[:], WS, w.v0h[:], ALU.mult, ALU.subtract)
            dve.scalar_tensor_tensor(w.v1l[:], nat_v1[:], WS, w.v1h[:], ALU.mult, ALU.subtract)
            dve.scalar_tensor_tensor(w.o1l[:].rearrange("p t d -> p (t d)"), nat_o1[:].rearrange("p t d -> p (t d)"), WS,
                                     w.o1h[:].rearrange("p t d -> p (t d)"), ALU.mult, ALU.subtract)
            for i, dst in enumerate((w.q0h, w.q0l, w.k0h, w.k0l)):
                dve.tensor_copy(dst[:], comp[:, i].rearrange("p (g r) -> p g r", g=G).unsqueeze(2).broadcast_to([128, G, 3, 32]))
            for k, (src, _, hi, lo, scale) in enumerate(tiles):
                if lo is not None:
                    dve.wait_ge(hi_done, k + 1)
                    dve.scalar_tensor_tensor(lo, tile_bank(k, src), scale, hi, ALU.mult, ALU.subtract).then_inc(lo_done, 1)
            for g in range(G):
                dve.wait_ge(hi_done, NT + g + 1)
                dve.scalar_tensor_tensor(w.al[:, product_heads(g)], product_bank(g), AS * DK1 ** -0.5,
                                         w.ah[:, product_heads(g)], ALU.mult, ALU.subtract).then_inc(lo_done, 1)


class Split:

    def __init__(self, name, rows, src, hi, lo, by=None, mean=None, rstd=None, shift=None, gain=None, bias=None):
        self.name, self.rows, self.src, self.hi, self.lo = name, rows, src, hi, lo
        self.by, self.mean, self.rstd, self.shift, self.gain, self.bias = by, mean, rstd, shift, gain, bias


def split_transposed(nc, w, bank, tag, jobs, before=None):
    with Memory(nc, tag) as m:
        for at, job in enumerate(jobs):
            n, rows = job.name, job.rows
            job.normed = m.sb(f"normed_{n}", [rows, 2, CH, D]) if job.by else None
            job.whole = m.sb(f"whole_{n}", [128, 2, CH, rows])
            job.ready, job.turned, job.high, job.split = (m.sem(f"{x}_{n}") for x in ("ready", "turned", "high", "split"))
            job.banks = [bank[2 * at + u][:, 0:CH * rows].rearrange("p (c r) -> p c r", r=rows) for u in range(2)]
        chain = m.sem("chain")
        pre = before(m) if before is not None else None
        block = m.block()

        def chunks(eng, job, body):
            if job.by == "vector":
                with eng.Fori(0, NCH // 2) as i:
                    body(i * 2, 0)
                    body(i * 2 + 1, 1)
            else:
                for k in range(NCH):
                    body(k, k % 2)

        def normalise(eng, job, k, u):
            eng.wait_ge(job.turned, k + 1)
            for c in range(CH):
                one = slice(k * CH + c, k * CH + c + 1) if isinstance(k, int) else bass.ds(k * CH + c, 1)
                if job.by == "gpsimd":
                    how = (job.rstd[:, one], job.shift[:, one], ALU.mult, ALU.add)
                else:
                    how = (job.mean[:, one, 0:1], job.rstd[:, one], ALU.subtract, ALU.mult)
                last = eng.tensor_scalar(job.normed[:, u, c:c + 1], job.src[:, one, :], *how)
            last.then_inc(job.ready, 1)

        @block.vector
        def _(dve):
            if pre is not None:
                pre(dve, linker(dve, chain))
            for job in jobs:
                if job.by == "vector":
                    chunks(dve, job, lambda k, u: normalise(dve, job, k, u))

        @block.tensor
        def _(pe):
            for job in jobs:
                def turn(k, u):
                    if job.by:
                        pe.wait_ge(job.ready, k + 1)
                    pe.wait_ge(job.high, k + 1)
                    for c in range(CH):
                        rows = job.normed[:, u, c] if job.by else job.src[:, k * CH + c]
                        last = pe.transpose(job.banks[u][:, c, :], rows, w.ident[0:job.rows, 0:job.rows])
                    last.then_inc(job.turned, 1)

                pe.sem_inc(job.turned, 2)
                chunks(pe, job, turn)

        @block.scalar
        def _(act):
            for job in jobs:
                def copy(k, u):
                    chunk = bass.ds(k * CH, CH)
                    act.wait_ge(job.turned, k + 3)
                    act.wait_ge(job.split, k + 1)
                    for dst in (job.whole[:, u], job.hi(chunk)):
                        if job.gain is None:
                            last = act.activation(dst, job.banks[u], ACT.Copy)
                        else:
                            last = act.activation(dst, job.banks[u], ACT.Identity, bias=job.bias, scale=job.gain)
                    last.then_inc(job.high, 1)

                act.sem_inc(job.high, 2)
                chunks(act, job, copy)

        @block.gpsimd
        def _(pool):
            for job in jobs:
                def low(k, u):
                    chunk = bass.ds(k * CH, CH)
                    pool.wait_ge(job.high, k + 3)
                    pool.tensor_tensor(job.lo(chunk), job.whole[:, u], job.hi(chunk), ALU.subtract).then_inc(job.split, 1)
                    if job.by == "gpsimd" and k + 2 < NCH:
                        normalise(pool, job, k + 2, u)

                pool.sem_inc(job.split, 2)
                if job.by == "gpsimd":
                    normalise(pool, job, 0, 0)
                    normalise(pool, job, 1, 1)
                chunks(pool, job, low)


def project0(nc, w, bank, xh, xl, ch, cl, qst, kst, vals):
    with Memory(nc, "project0") as m:
        q_done, q_hi, q_lo, k_done, k_hi, k_lo, v_done, v_hi, v_out = (
            m.sem(n) for n in ("q_done", "q_hi", "q_lo", "k_done", "k_hi", "k_lo", "v_done", "v_hi", "v_out"))
        block = m.block()
        KC = CH * C
        q_bank = [bank[g][0:R0, :] for g in range(G)]
        k_bank = [bank[4 + g % 2][0:R0, 0:KC] for g in range(G)]
        v_bank = [bank[6 + u][0:C, :] for u in range(2)]
        SQ = DK0 ** -0.5 / WS

        @block.tensor
        def _(pe):
            pe.sem_inc(q_lo, G)
            pe.sem_inc(k_lo, 2)
            pe.sem_inc(v_out, 2)
            with pe.Fori(0, NCH // 2) as i:
                for u in range(2):
                    chunk = bass.ds(i * (2 * CH) + CH * u, CH)
                    for g in range(G):
                        n = G * u + g
                        pe.wait_ge(q_lo, i * (2 * G) + (n + 1))
                        for k, (wt, x) in enumerate(((w.q0h, xh), (w.q0l, xh), (w.q0h, xl))):
                            last = pe.matmul(q_bank[g], wt[:, g].rearrange("p a r -> p (a r)"), x[:, chunk, :],
                                             start=k == 0, stop=k == 2)
                        last.then_inc(q_done, 1)
                        pe.wait_ge(k_lo, i * (2 * G) + (n + 1))
                        for k, (wt, x) in enumerate(((w.k0h, ch), (w.k0l, ch), (w.k0h, cl))):
                            last = pe.matmul(k_bank[g], wt[:, g].rearrange("p a r -> p (a r)"), x[:, chunk, :],
                                             start=k == 0, stop=k == 2)
                        last.then_inc(k_done, 1)
                    pe.wait_ge(v_out, i * 2 + (u + 1))
                    for c in range(CH):
                        one = bass.ds(i * (2 * CH) + (CH * u + c), 1)
                        for k, (x, wt) in enumerate(((ch, w.v0h), (ch, w.v0l), (cl, w.v0h))):
                            last = pe.matmul(v_bank[u][:, D * c:D * c + D], x[:, one, :], wt[:], start=k == 0, stop=k == 2)
                    last.then_inc(v_done, 1)

        @block.scalar
        def _(act):
            with act.Fori(0, NCH // 2) as i:
                for u in range(2):
                    chunk = bass.ds(i * (2 * CH) + CH * u, CH)
                    for g in range(G):
                        n = G * u + g
                        act.wait_ge(q_done, i * (2 * G) + (n + 1))
                        act.activation(qst[:, g, chunk, :], q_bank[g].rearrange("p (c s) -> p c s", c=CH), ACT.Copy,
                                       scale=SQ).then_inc(q_hi, 1)
                        act.wait_ge(k_done, i * (2 * G) + (n + 1))
                        act.activation(kst[:, g, chunk, :], k_bank[g].rearrange("p (c s) -> p c s", c=CH), ACT.Copy,
                                       scale=1.0 / WS).then_inc(k_hi, 1)
                    act.wait_ge(v_done, i * 2 + (u + 1))
                    for c in range(CH):
                        one = bass.ds(i * (2 * CH) + (CH * u + c), 1)
                        head = v_bank[u][:, D * c:D * c + D].rearrange("p (o h k) -> p o h k", o=1, k=DK0)
                        last = act.activation(vals[:, one, 0, :, 0:DK0], head, ACT.Copy, scale=1.0 / WS)
                    last.then_inc(v_hi, 1)

        @block.vector
        def _(dve):
            for i, value in enumerate((1.0, 0.0)):
                dve.memset(vals[:, :, i, :, DK0:DK0 + 1], value)
            with dve.Fori(0, NCH // 2) as i:
                for u in range(2):
                    chunk = bass.ds(i * (2 * CH) + CH * u, CH)
                    for g in range(G):
                        n = G * u + g
                        low = slice(64, 96)
                        dve.wait_ge(q_hi, i * (2 * G) + (n + 1))
                        dve.scalar_tensor_tensor(qst[low, g, chunk, :], q_bank[g][low].rearrange("p (c s) -> p c s", c=CH), SQ,
                                                 qst[low, g, chunk, :], ALU.mult, ALU.subtract).then_inc(q_lo, 1)
                        low = slice(32, 64)
                        dve.wait_ge(k_hi, i * (2 * G) + (n + 1))
                        dve.scalar_tensor_tensor(kst[low, g, chunk, :], k_bank[g][low].rearrange("p (c s) -> p c s", c=CH),
                                                 1.0 / WS, kst[low, g, chunk, :], ALU.mult, ALU.subtract).then_inc(k_lo, 1)
                    dve.wait_ge(v_hi, i * 2 + (u + 1))
                    for c in range(CH):
                        one = bass.ds(i * (2 * CH) + (CH * u + c), 1)
                        head = v_bank[u][:, D * c:D * c + D].rearrange("p (o h k) -> p o h k", o=1, k=DK0)
                        last = dve.scalar_tensor_tensor(vals[:, one, 1, :, 0:DK0], head, 1.0 / WS, vals[:, one, 0, :, 0:DK0],
                                                        ALU.mult, ALU.subtract)
                    last.then_inc(v_out, 1)


def attention0(nc, w, bank, qst, kst, vals):
    with Memory(nc, "attention0") as m:
        LAG = 2
        keys = m.sb("keys", [R0, 2, G, HG, C], FP16)
        queries = m.sb("queries", [R0, 2, G, S], FP16)
        values = m.sb("values", [C, 2, 2, H, DK0 + 1], FP16)
        negmax = m.sb("negmax", [S, G, HG], FP16)
        probs, probs_h, probs_l = m.sb("probs", [C, 2, HG, S]), m.sb("probs_h", [C, G, HG, S], FP16), m.sb("probs_l", [C, G, HG, S], FP16)
        recip = m.sb("recip", [S, H])
        heads_out = m.sb("heads_out", [S, H, DK0])
        turned_h, turned_l = m.sb("turned_h", [D, S], FP16), m.sb("turned_l", [D, S], FP16)
        (k_staged, q_staged, v_staged, scored, maxed, shifted, exped, p_split, mixed, inverted, normed, turned, ot_hi, ot_lo,
         projected, added, biased, waited) = (
            m.sem(n) for n in ("k_staged", "q_staged", "v_staged", "scored", "maxed", "shifted", "exped", "p_split", "mixed",
                               "inverted", "normed", "turned", "ot_hi", "ot_lo", "projected", "added", "biased", "waited"))
        block = m.block()
        score = [bank[u][:, 0:HG * C].rearrange("p (h c) -> p h c", c=C) for u in range(2)]
        score_t = [bank[2 + u][0:C, :].rearrange("p (h s) -> p h s", s=S) for u in range(2)]
        mix = [bank[4 + u][:, 0:H * (DK0 + 1)].rearrange("p (h k) -> p h k", k=DK0 + 1) for u in range(2)]
        out_t = bank[6][:, 0:S]
        out_p = bank[7][:, 0:D]

        def sequences(eng, body):
            body(0, 0)
            body(1, 1)
            with eng.Fori(0, (B - 4) // 2) as i:
                body(i * 2 + 2, 0)
                body(i * 2 + 3, 1)
            body(B - 2, 0)
            body(B - 1, 1)

        def within(b):
            return not isinstance(b, int) or b < B

        @block.gpsimd
        def _(pool):
            def probs_low(b, g):
                n = b * G + g
                pool.wait_ge(exped, n + 1)
                if late(n, G):
                    pool.wait_ge(mixed, n - (G - 1))
                pool.tensor_tensor(probs_l[:, g], probs[:, g % 2], probs_h[:, g], ALU.subtract).then_inc(p_split, 1)

            def add_bias(b):
                row = w.X[:, bass.ds(b, 1), :]
                pool.tensor_tensor(row, row, w.bias0[:].unsqueeze(1), ALU.add).then_inc(biased, 1)

            def body(b, u):
                for g in range(G):
                    probs_low(b, g)
                add_bias(b)

            sequences(pool, body)

        @block.tensor
        def _(pe):
            def scores(b, g, u):
                n = b * G + g
                if g == 0:
                    pe.wait_ge(k_staged, b + 1)
                    pe.wait_ge(q_staged, b + 1)
                if late(n, 2):
                    pe.wait_ge(maxed, n - 1)
                pe.matmul(score[g % 2], queries[:, u, g], keys[:, u, g], start=True, stop=True).then_inc(scored, 1)

            def scores_by_key(b, g, u):
                n = b * G + g
                pe.wait_ge(maxed, n + 1)
                if late(n, 2):
                    pe.wait_ge(exped, n - 1)
                for h in range(HG):
                    dst = score_t[g % 2][:, h, :]
                    pe.matmul(dst, keys[:, u, g, h], queries[:, u, g], start=True, stop=False)
                    last = pe.matmul(dst, negmax[:, g, h:h + 1].broadcast_to([S, C]), w.identh[:], start=False, stop=True)
                last.then_inc(shifted, 1)

            def mix_values(b, g, u):
                pe.wait_ge(p_split, b * G + (g + 1))
                if g == 0:
                    pe.wait_ge(v_staged, b + 1)
                    if late(b, 2):
                        pe.wait_ge(normed, b - 1)
                for h in range(HG):
                    v = HG * g + h
                    for k, (x, part) in enumerate(((probs_h, 0), (probs_h, 1), (probs_l, 0))):
                        last = pe.matmul(mix[u][:, v, :], x[:, g, h], values[:, u, part, v, :], start=k == 0, stop=k == 2)
                last.then_inc(mixed, 1)

            def turn(b):
                pe.wait_ge(normed, b + 1)
                if late(b):
                    pe.wait_ge(ot_lo, b)
                pe.transpose(out_t, heads_out[:].rearrange("p h k -> p (h k)"), w.ident[:]).then_inc(turned, 1)

            def project(b):
                pe.wait_ge(ot_lo, b + 1)
                if late(b):
                    pe.wait_ge(added, b)
                for k, (x, wt) in enumerate(((turned_h, w.o0h), (turned_h, w.o0l), (turned_l, w.o0h))):
                    last = pe.matmul(out_p, x[:], wt[:, 0, :], start=k == 0, stop=k == 2)
                last.then_inc(projected, 1)

            def body(b, u):
                for g in range(G):
                    if g + 1 < G:
                        scores(b, g + 1, u)
                    elif within(b + 1):
                        scores(b + 1, 0, 1 - u)
                    scores_by_key(b, g, u)
                    if g >= LAG:
                        mix_values(b, g - LAG, u)
                    elif late(b):
                        mix_values(b - 1, G + g - LAG, 1 - u)
                    if g == 3 and late(b):
                        turn(b - 1)
                    if g == 0 and late(b, 2):
                        project(b - 2)

            scores(0, 0, 0)
            sequences(pe, body)
            for g in range(G - LAG, G):
                mix_values(B - 1, g, (B - 1) % 2)
            project(B - 2)
            turn(B - 1)
            project(B - 1)

        @block.scalar
        def _(act):
            def exp(b, g):
                n = b * G + g
                act.wait_ge(shifted, n + 1)
                if late(n, 2):
                    act.wait_ge(p_split, n - 1)
                if late(n, G):
                    act.wait_ge(mixed, n - (G - 1))
                act.activation(probs[:, g % 2], score_t[g % 2], ACT.Exp)
                act.activation(probs_h[:, g], score_t[g % 2], ACT.Exp).then_inc(exped, 1)

            def stage_values(b, u):
                if late(b, 2):
                    act.wait_ge(mixed, (b - 1) * G)
                act.activation(values[:, u].rearrange("p i h k -> p (i h k)"),
                               vals[:, bass.ds(b, 1)].rearrange("p o i h k -> p (o i h k)"), ACT.Copy).then_inc(v_staged, 1)

            def out_high(b):
                act.wait_ge(turned, b + 1)
                if late(b):
                    act.wait_ge(projected, b)
                act.activation(turned_h[:], out_t, ACT.Copy).then_inc(ot_hi, 1)

            def body(b, u):
                for g in range(G):
                    exp(b, g)
                    if g == 2 and within(b + 1):
                        stage_values(b + 1, 1 - u)
                    if g == 3 and late(b):
                        out_high(b - 1)

            stage_values(0, 0)
            sequences(act, body)
            out_high(B - 1)

        @block.vector
        def _(dve):
            def stage(b, u):
                one = bass.ds(b, 1)
                if late(b, 2):
                    dve.wait_ge(shifted, (b - 1) * G)
                dve.sem_inc(waited, 1)
                dve.tensor_copy(queries[:, u], qst[:, :, one, :].rearrange("p g o s -> p g (o s)")).then_inc(q_staged, 1)
                for g in range(G):
                    last = dve.tensor_tensor(keys[:, u, g], kst[:, g, one, :].broadcast_to([R0, HG, C]),
                                             w.head_rows[:].unsqueeze(2).broadcast_to([R0, HG, C]), ALU.mult)
                last.then_inc(k_staged, 1)

            def maximum(b, g):
                dve.wait_ge(scored, b * G + (g + 1))
                dve.tensor_reduce(negmax[:, g], score[g % 2], AX.X, ALU.max, negate=True).then_inc(maxed, 1)

            def normalise(b, u):
                dve.wait_ge(mixed, (b + 1) * G)
                dve.reciprocal(recip[:], mix[u][:, :, DK0]).then_inc(inverted, 1)
                dve.wait_ge(inverted, b + 1)
                if late(b):
                    dve.wait_ge(turned, b)
                dve.tensor_tensor(heads_out[:], mix[u][:, :, 0:DK0], recip[:].unsqueeze(2).broadcast_to([S, H, DK0]),
                                  ALU.mult).then_inc(normed, 1)

            def out_low(b):
                dve.wait_ge(ot_hi, b + 1)
                dve.tensor_tensor(turned_l[:], out_t, turned_h[:], ALU.subtract).then_inc(ot_lo, 1)

            def residual(b):
                row = w.X[:, bass.ds(b, 1), :]
                dve.wait_ge(projected, b + 1)
                dve.wait_ge(biased, b + 1)
                dve.sem_inc(waited, 1)
                dve.scalar_tensor_tensor(row, out_p.unsqueeze(1), w.tg0[:], row, ALU.mult, ALU.add).then_inc(added, 1)

            def body(b, u):
                for g in range(G):
                    if g + 1 < G:
                        maximum(b, g + 1)
                    elif within(b + 1):
                        maximum(b + 1, 0)
                    if g == 0 and late(b, 2):
                        out_low(b - 2)
                    if g == 0 and within(b + 1):
                        stage(b + 1, 1 - u)
                    if g == 1 and late(b, 2):
                        residual(b - 2)
                    if g == 2 and late(b):
                        normalise(b - 1, 1 - u)

            stage(0, 0)
            maximum(0, 0)
            sequences(dve, body)
            out_low(B - 2)
            residual(B - 2)
            normalise(B - 1, (B - 1) % 2)
            out_low(B - 1)
            residual(B - 1)


def feed_forward0(nc, w, bank):
    with Memory(nc, "feed_forward0") as m:
        normed, rounded = m.sb("normed", [S, 2, CH, D]), m.sb("rounded", [S, 2, CH, D])
        amax, scale, step_of = m.sb("amax", [S, 2, CH]), m.sb("scale", [S, 2, CH]), m.sb("step_of", [S, 2, CH])
        rows_h, rows_l = m.sb("rows_h", [D, 2, CH, S], FP16), m.sb("rows_l", [D, 2, CH, S], FP16)
        pre, tanh = m.sb("pre", [128, 2, N]), m.sb("tanh", [128, 2, N])
        silu = m.sb("silu", [128, 2, M0, N])
        biased = m.sb("biased", [S, 2, HID])
        ints = m.sb("ints", [128, 2, M0, S], FP16)
        amax2, step2, scale2, out_of = m.sb("amax2", [S, 1]), m.sb("step2", [S, 1]), m.sb("scale2", [S, 2]), m.sb("out_of", [S, CH])
        bn = m.sb("bn", [S, B, 6])
        waited, pool_waited = m.sem("waited"), m.sem("pool_waited")
        t1, t2 = m.sb("t1", [S, B]), m.sb("t2", [S, B])
        (rsqrt_done, normed_in, scales, rounded_in, quant, turned, rows_hi, rows_lo, conved, activated, silued, returned,
         maxed, scale_in, biased_in, turned_back, ints_in, projected, added, chain, achain, out_scale_in) = (
            m.sem(n) for n in ("rsqrt_done", "normed_in", "scales", "rounded_in", "quant", "turned", "rows_hi", "rows_lo",
                               "conved", "activated", "silued", "returned", "maxed", "scale_in", "biased_in",
                               "turned_back", "ints_in", "projected", "added", "chain", "achain", "out_scale_in"))
        block = m.block()
        rows_t = bank[0][:, :].rearrange("p (c s) -> p c s", s=S)
        conv = [bank[1 + u][:, :].rearrange("p (c s) -> p c s", s=S) for u in range(2)]
        by_row = [bank[3 + u][:, :].rearrange("p (m c) -> p m c", c=128) for u in range(2)]
        by_channel = [bank[5 + u][:, :].rearrange("p (m s) -> p m s", s=S) for u in range(2)]
        out_p = bank[7][:, 0:D]
        LOOP = (1, 5)

        def chunks(eng, body):
            body(0, 0)
            with eng.Fori(0, (LOOP[1] - LOOP[0]) // 2) as i:
                body(i * 2 + 1, 1)
                body(i * 2 + 2, 0)
            for k in range(LOOP[1], NCH):
                body(k, k % 2)

        def within(k, ahead):
            return not isinstance(k, int) or k + ahead < NCH

        def next_tile(k, u, c):
            return (within(k, 1), k + 1, 1 - u, c + 1) if c < CH - 1 else (within(k, 2), k + 2, u, 0)

        @block.gpsimd
        def _(pool):
            def quantise(k, u):
                pool.wait_ge(scales, k + 1)
                pool.sem_inc(pool_waited, 1)
                for c in range(CH):
                    last = pool.tensor_scalar(rounded[:, u, c], normed[:, u, c], scale[:, u, c:c + 1], ROUND, ALU.mult, ALU.add)
                last.then_inc(rounded_in, 1)
                pool.wait_ge(rounded_in, k + 1)
                if not isinstance(k, int) or k >= 2:
                    pool.wait_ge(turned, k - 1)
                pool.sem_inc(pool_waited, 1)
                for c in range(CH):
                    last = pool.tensor_scalar(normed[:, u, c], rounded[:, u, c], -ROUND, step_of[:, u, c:c + 1],
                                              ALU.add, ALU.mult)
                last.then_inc(quant, 1)

            quantise(0, 0)
            quantise(1, 1)
            quantise(2, 0)
            chunks(pool, lambda k, u: quantise(k + 3, 1 - u) if within(k, 3) else None)

        @block.tensor
        def _(pe):
            def turn(k, u):
                pe.wait_ge(quant, k + 1)
                if not isinstance(k, int) or k > 0:
                    pe.wait_ge(rows_lo, k)
                for c in range(CH):
                    last = pe.transpose(rows_t[:, c, :], normed[:, u, c], w.ident[:])
                last.then_inc(turned, 1)

            def convolve(k, u, t):
                n = k * M0 + t
                pe.wait_ge(rows_lo, k + 1)
                if not isinstance(k, int) or n >= 2:
                    pe.wait_ge(activated, n - 1)
                products = [(tap, wt, x) for tap in (1, 0, 2) for wt, x in ((w.taph, rows_h), (w.tapl, rows_h), (w.taph, rows_l))]
                for i, (tap, wt, x) in enumerate(products):
                    to = slice(max(0, 1 - tap), S - max(0, tap - 1))
                    of = slice(max(0, tap - 1), S - max(0, 1 - tap))
                    last = pe.matmul(conv[t % 2][:, :, to], wt[:, tap, t], x[:, u, :, of], start=i == 0, stop=i == len(products) - 1)
                last.then_inc(conved, 1)

            def to_rows(k, u, c):
                n = k * CH + c
                pe.wait_ge(silued, (k + 1) * M0)
                if not isinstance(k, int) or n >= 2:
                    pe.wait_ge(biased_in, n - 1)
                for t in range(M0):
                    last = pe.transpose(by_row[c % 2][:, t, :], silu[:, u, t, S * c:S * c + S], w.ident[:])
                last.then_inc(returned, 1)

            def to_channels(k, c):
                n = k * CH + c
                pe.wait_ge(biased_in, n + 1)
                if not isinstance(k, int) or n >= 2:
                    pe.wait_ge(ints_in, n - 1)
                for t in range(M0):
                    last = pe.transpose(by_channel[c % 2][:, t, :], biased[:, c % 2, 128 * t:128 * t + 128], w.ident[:])
                last.then_inc(turned_back, 1)

            def project(n, c):
                pe.wait_ge(ints_in, n + 1)
                if not isinstance(n, int) or n >= 1:
                    pe.wait_ge(added, n)
                for t in range(M0):
                    last = pe.matmul(out_p, ints[:, c % 2, t], w.w2t[:, t], start=t == 0, stop=t == M0 - 1)
                last.then_inc(projected, 1)

            def body(k, u):
                for c in range(CH):
                    more, *tile = next_tile(k, u, c)
                    if c < CH - 1:
                        to_rows(k, u, c + 1)
                    if more:
                        convolve(*tile)
                    if c == CH - 1 and within(k, 1):
                        to_rows(k + 1, 1 - u, 0)
                    to_channels(k, c)
                    if not (isinstance(k, int) and k == 0 and c == 0):
                        project(k * CH + (c - 1), (c + CH - 1) % CH)
                    if c == 1 and within(k, 2):
                        turn(k + 2, u)

            turn(0, 0)
            for t in range(M0):
                convolve(0, 0, t)
            turn(1, 1)
            convolve(1, 1, 0)
            to_rows(0, 0, 0)
            chunks(pe, body)
            project(B - 1, CH - 1)

        @block.scalar
        def _(act):
            def rows_high(k, u):
                act.wait_ge(turned, k + 1)
                if not isinstance(k, int) or k >= 2:
                    act.wait_ge(conved, (k - 1) * M0)
                act.activation(rows_h[:, u], rows_t, ACT.Copy).then_inc(rows_hi, 1)

            def activate(k, t):
                n = k * M0 + t
                act.wait_ge(conved, n + 1)
                if not isinstance(k, int) or n >= 2:
                    act.wait_ge(silued, n - 1)
                src = bank[1 + t % 2][:, :]
                act.activation(tanh[:, t % 2], src, ACT.Tanh, bias=w.conv_b_half[:, t:t + 1], scale=0.5 / WS)
                act.activation(pre[:, t % 2], src, ACT.Identity, bias=w.conv_b[:, t:t + 1], scale=1.0 / WS).then_inc(activated, 1)

            def quantise(k, c):
                n = k * CH + c
                act.wait_ge(returned, n + 1)
                act.wait_ge(scale_in, n + 1)
                if not isinstance(k, int) or n >= 2:
                    act.wait_ge(turned_back, n - 1)
                act.activation(biased[:, c % 2], bank[3 + c % 2][:, :], ACT.Copy, bias=ROUND,
                               scale=scale2[:, c % 2:c % 2 + 1]).then_inc(biased_in, 1)

            def body(k, u):
                for c in range(CH):
                    quantise(k, c)
                    more, chunk, _, t = next_tile(k, u, c)
                    if more:
                        activate(chunk, t)
                    if c == 1 and within(k, 2):
                        rows_high(k + 2, u)

            rows_high(0, 0)
            for t in range(M0):
                activate(0, t)
            rows_high(1, 1)
            activate(1, 0)
            chunks(act, body)

        @block.vector
        def _(dve):
            LINKS = 2
            OUT_LINKS = 2

            def normalise(k, u, half):
                if half == 0 and late(k, 2):
                    dve.wait_ge(turned, k - 1)
                for c in range(2 * half, 2 * half + 2):
                    one = bass.ds(k * CH + c, 1)
                    last = dve.tensor_scalar(normed[:, u, c:c + 1], w.X[:, one, :], w.mv[:, one, 0:1], w.rstd[:, one],
                                             ALU.subtract, ALU.mult)
                last.then_inc(normed_in, 1)

            def scales_of(k, u):
                dve.wait_ge(normed_in, 2 * k + 2)
                dve.tensor_reduce(amax[:, u], normed[:, u], AX.X, ALU.max, apply_absolute_value=True).then_inc(chain, 1)
                dve.wait_ge(chain, k * LINKS + 1)
                if late(k, 2):
                    dve.wait_ge(quant, k - 1)
                dve.tensor_scalar(step_of[:, u], amax[:, u], 1e-5, 1.0 / 127.0, ALU.max, ALU.mult).then_inc(chain, 1)
                dve.wait_ge(chain, k * LINKS + 2)
                dve.reciprocal(scale[:, u], step_of[:, u]).then_inc(scales, 1)

            def rows_low(k, u):
                dve.wait_ge(rows_hi, k + 1)
                dve.tensor_tensor(rows_l[:, u], rows_t, rows_h[:, u], ALU.subtract).then_inc(rows_lo, 1)

            def multiply(k, u, t):
                dve.wait_ge(activated, k * M0 + (t + 1))
                dve.scalar_tensor_tensor(silu[:, u, t], tanh[:, t % 2], 1.0, pre[:, t % 2], ALU.add, ALU.mult).then_inc(silued, 1)

            def scale_of(k, c):
                n = k * CH + c
                dve.wait_ge(returned, n + 1)
                if not isinstance(k, int) or n >= 2:
                    dve.wait_ge(biased_in, n - 1)
                dve.tensor_reduce(amax2[:], bank[3 + c % 2][:, :], AX.X, ALU.max, apply_absolute_value=True).then_inc(achain, 1)
                dve.wait_ge(achain, n * OUT_LINKS + 1)
                dve.tensor_scalar(step2[:], amax2[:], 2e-5, 1.0 / 127.0, ALU.max, ALU.mult).then_inc(achain, 1)
                dve.wait_ge(achain, n * OUT_LINKS + 2)
                dve.reciprocal(scale2[:, c % 2:c % 2 + 1], step2[:]).then_inc(scale_in, 1)
                dve.tensor_tensor(out_of[:, c:c + 1], step2[:], w.ffn_out[:], ALU.mult).then_inc(out_scale_in, 1)

            def integers(k, c):
                n = k * CH + c
                dve.wait_ge(turned_back, n + 1)
                if not isinstance(k, int) or n >= 2:
                    dve.wait_ge(projected, n - 1)
                dve.tensor_scalar(ints[:, c % 2], by_channel[c % 2], ROUND, None, ALU.subtract).then_inc(ints_in, 1)

            def residual(n, c):
                row = w.X[:, bass.ds(n, 1), :]
                dve.wait_ge(projected, n + 1)
                dve.wait_ge(out_scale_in, n + 1)
                dve.sem_inc(waited, 1)
                dve.scalar_tensor_tensor(row, out_p.unsqueeze(1), out_of[:, c:c + 1], row, ALU.mult, ALU.add).then_inc(added, 1)

            def body(k, u):
                for c in range(CH):
                    if c == 2 and within(k, 2):
                        rows_low(k + 2, u)
                    if c < CH - 1:
                        scale_of(k, c + 1)
                    if c == CH - 1 and within(k, 1):
                        scale_of(k + 1, 0)
                    more, *tile = next_tile(k, u, c)
                    if more:
                        multiply(*tile)
                    integers(k, c)
                    if not (isinstance(k, int) and k == 0 and c == 0):
                        residual(k * CH + (c - 1), (c + CH - 1) % CH)
                    if c < 2 and within(k, 3):
                        normalise(k + 3, 1 - u, c)
                    if c == 2 and within(k, 3):
                        scales_of(k + 3, 1 - u)

            link = linker(dve, rsqrt_done)
            row_statistics(dve, link, w, bn)
            rsqrt(dve, link, w.rstd[:], w.mv[:, :, 1], t1[:], t2[:])
            for k in range(3):
                for half in range(2):
                    normalise(k, k % 2, half)
                scales_of(k, k % 2)
            rows_low(0, 0)
            for t in range(M0):
                multiply(0, 0, t)
            rows_low(1, 1)
            multiply(1, 1, 0)
            scale_of(0, 0)
            chunks(dve, body)
            residual(B - 1, CH - 1)


def mask_keys(nc, w, kv):
    with Memory(nc, "mask_keys") as m:
        diff = m.sb("diff", [D, 2, B // 2, C], FP16)
        chain, copied = m.sem("chain"), m.sem("copied")
        block = m.block()

        @block.scalar
        def _(act):
            with act.Fori(0, NCH) as i:
                chunk = bass.ds(i * CH, CH)
                act.activation(kv[:, chunk, 2, 0:S], kv[:, chunk, 0, 0:S], ACT.Copy).then_inc(copied, 1)
            act.wait_ge(copied, NCH)

        @block.vector
        def _(dve):
            halves = [slice(0, B // 2), slice(B // 2, B)]
            latent0 = [kv[:, x, 0, 0:1].broadcast_to([D, B // 2, C]) for x in halves]
            for i, x in enumerate(halves):
                dve.tensor_tensor(diff[:, i], kv[:, x, 0, S:KV], latent0[i], ALU.subtract).then_inc(chain, 1)
            for i, x in enumerate(halves):
                dve.wait_ge(chain, i + 1)
                dve.tensor_tensor(diff[:, i], diff[:, i], w.mask01[:, x, :], ALU.mult).then_inc(chain, 1)
            for i, x in enumerate(halves):
                dve.wait_ge(chain, i + 3)
                dve.tensor_tensor(kv[:, x, 2, S:KV], diff[:, i], latent0[i], ALU.add)


def latent_scale(w):
    def memory(m):
        t1, t2, r, v = (m.sb(n, [S, B]) for n in ("t1", "t2", "r", "v"))
        bn = m.sb("bn", [S, B, 6])

        def work(dve, link):
            row_statistics(dve, link, w, bn)
            rsqrt(dve, link, r[:], w.mv[:, :, 1], t1[:], t2[:])
            link(dve.tensor_tensor(v[:], r[:], r[:], ALU.mult))
            link(dve.tensor_tensor(v[:], v[:], w.mv[:, :, 1], ALU.mult))
            rsqrt(dve, link, w.rstd[:], v[:], t1[:], t2[:])
            link(dve.tensor_tensor(w.rstd[:], w.rstd[:], r[:], ALU.mult))
        return work
    return memory


def row_scale(w):
    def memory(m):
        t1, t2, bn = m.sb("t1", [S, B]), m.sb("t2", [S, B]), m.sb("bn", [S, B, 6])

        def work(dve, link):
            row_statistics(dve, link, w, bn)
            rsqrt(dve, link, w.rstd[:], w.mv[:, :, 1], t1[:], t2[:])
        return work
    return memory


def attention1(nc, w, bank, kv):
    with Memory(nc, "attention1") as m:
        HI, LO, MAX = 0, 1, 2
        keys = m.sb("keys", [D, 2, 3, KV], FP16)
        th, tl = m.sb("th", [D, G, HG, S], FP16), m.sb("tl", [D, G, HG, S], FP16)
        negmax = m.sb("negmax", [S, G, HG], FP16)
        probs_l, probs_c = m.sb("probs_l", [S, 2, HG, S]), m.sb("probs_c", [C, 2, HG, S])
        ph_l, ph_c = m.sb("ph_l", [S, 2, HG, S], FP16), m.sb("ph_c", [C, 2, HG, S], FP16)
        pl_l, pl_c = m.sb("pl_l", [S, 2, HG, S], FP16), m.sb("pl_c", [C, 2, HG, S], FP16)
        vh_l, vh_c = m.sb("vh_l", [S, 2, H, DK1 + 1], FP16), m.sb("vh_c", [C, 2, H, DK1 + 1], FP16)
        vl_l, vl_c = m.sb("vl_l", [S, 2, H, DK1 + 1], FP16), m.sb("vl_c", [C, 2, H, DK1 + 1], FP16)
        recip = m.sb("recip", [S, HG])
        heads_out = m.sb("heads_out", [S, 2, H, DK1])
        turned_h, turned_l = m.sb("turned_h", [D, H // 2, S], FP16), m.sb("turned_l", [D, H // 2, S], FP16)
        out, zn, bn, mv, rstd = m.sb("out", [S, D]), m.sb("zn", [S, D]), m.sb("bn", [S, 6]), m.sb("mv", [S, 1, 2]), m.sb("rstd", [S, 1])
        t1, t2 = m.sb("t1", [S, 1]), m.sb("t2", [S, 1])
        (ones_in, staged, t_done, t_hi, t_lo, scored, maxed, shifted, exped_l, exped_c, p_split, v_done, v_hi, v_out, mixed, normed, turned, ot_hi,
         ot_lo, projected, out_copied, out_normed, scaled, summed, biased, nchain, chain, waited, pool_waited, act_waited) = (
            m.sem(n) for n in ("ones_in", "staged", "t_done", "t_hi", "t_lo", "scored", "maxed", "shifted", "exped_l", "exped_c",
                               "p_split", "v_done", "v_hi", "v_out", "mixed", "normed", "turned", "ot_hi", "ot_lo", "projected",
                               "out_copied", "out_normed", "scaled", "summed", "biased", "nchain", "chain", "waited", "pool_waited", "act_waited"))
        block = m.block()
        t_bank = bank[0][:, :].rearrange("p (h s) -> p h s", s=S)
        score = [bank[1 + i][:, 0:2 * KV].rearrange("p (h k) -> p h k", k=KV) for i in range(2)]
        by_key_l = bank[3][:, :].rearrange("p (h s) -> p h s", s=S)
        by_key_c = bank[4][0:C, :].rearrange("p (h s) -> p h s", s=S)
        mix = bank[5][:, 0:HG * (DK1 + 1)].rearrange("p (h k) -> p h k", k=DK1 + 1)
        VW = HG * DK1
        v_l, v_c = bank[6][:, 0:VW], bank[6][0:C, VW:2 * VW]
        out_t = bank[7][:, :].rearrange("p (t s) -> p t s", s=S)
        out_p = bank[7][:, 0:D]
        LAT, CTX = slice(0, S), slice(S, KV)
        VALUES_AHEAD = 3

        def after(b, g, u, n):
            return (b, g + n, u) if g + n < G else (b + 1, g + n - G, 1 - u)

        def before(b, g, u):
            return (b, g - 1, u) if g > 0 else (b - 1, G - 1, 1 - u)

        def sequences(eng, body):
            body(0, 0, True, False)
            with eng.Fori(0, (B - 2) // 2) as i:
                body(i * 2 + 1, 1, False, False)
                body(i * 2 + 2, 0, False, False)
            body(B - 1, (B - 1) % 2, False, True)

        @block.gpsimd
        def _(pool):
            def probs_low(b, g):
                if late(b * G + g, 2):
                    pool.wait_ge(mixed, b * G + (g - 1))
                for exped, low, whole, high in ((exped_l, pl_l, probs_l, ph_l), (exped_c, pl_c, probs_c, ph_c)):
                    pool.wait_ge(exped, b * G + (g + 1))
                    last = pool.tensor_tensor(low[:, g % 2], whole[:, g % 2], high[:, g % 2], ALU.subtract)
                last.then_inc(p_split, 1)

            def add_bias(b):
                row = w.X[:, bass.ds(b, 1), :]
                pool.tensor_tensor(row, row, w.bias1[:].unsqueeze(1), ALU.add).then_inc(biased, 1)

            def residual(t):
                pool.wait_ge(out_normed, t + 1)
                pool.tensor_tensor(zn[:], zn[:], w.gain1[:], ALU.mult).then_inc(scaled, 1)
                pool.wait_ge(scaled, t + 1)
                pool.wait_ge(biased, t + 1)
                pool.sem_inc(pool_waited, 1)
                row = w.X[:, bass.ds(t, 1), :]
                pool.tensor_tensor(row, row, zn[:].unsqueeze(1), ALU.add).then_inc(summed, 1)

            def body(b, u, first, last):
                for g in range(G):
                    probs_low(b, g)
                    if g == 3 and not first:
                        residual(b - 1)
                    if g == 0:
                        add_bias(b)

            sequences(pool, body)
            residual(B - 1)

        @block.tensor
        def _(pe):
            def three(dst, pairs):
                for i, (x, y) in enumerate(pairs):
                    last = pe.matmul(dst, x, y, start=i == 0, stop=i == 2)
                return last

            def make_t(b, g, u):
                pe.wait_ge(staged, b + 1)
                if late(b * G + g):
                    pe.wait_ge(t_lo, b * G + g)
                for h in range(HG):
                    ah, al = w.ah[:, HG * g + h], w.al[:, HG * g + h]
                    last = three(t_bank[:, h], ((ah, keys[:, u, HI, LAT]), (al, keys[:, u, HI, LAT]), (ah, keys[:, u, LO, LAT])))
                last.then_inc(t_done, 1)

            def scores(b, g, u):
                pe.wait_ge(t_hi, b * G + (g + 1))
                if late(b * G + g):
                    pe.wait_ge(maxed, b * G + g)
                for h in range(HG):
                    last = pe.matmul(score[h // 2][:, h % 2], th[:, g, h], keys[:, u, MAX], start=True, stop=True)
                last.then_inc(scored, 1)

            def scores_by_key(b, g, u, turns):
                pe.wait_ge(t_lo, b * G + (g + 1))
                pe.wait_ge(maxed, b * G + (g + 1))
                for dst, part, width, exped in ((by_key_l, LAT, S, exped_l), (by_key_c, CTX, C, exped_c)):
                    if late(b * G + g):
                        pe.wait_ge(exped, b * G + g)
                    kh, kl = keys[:, u, HI, part], keys[:, u, LO, part]
                    pe.matmul(dst, kh, th[:, g], start=True, stop=False)
                    pe.matmul(dst, kl, th[:, g], start=False, stop=False)
                    pe.matmul(dst, kh, tl[:, g], start=False, stop=False)
                    for h in range(HG):
                        last = pe.matmul(dst[:, h], negmax[:, g, h:h + 1].broadcast_to([S, width]), w.identh[:],
                                         start=False, stop=h == HG - 1)
                    last.then_inc(shifted, 1)
                    if part is LAT and turns:
                        turn(b - 1, g, 1 - u)

            def mix_values(b, g, u):
                pe.wait_ge(p_split, b * G + (g + 1))
                pe.wait_ge(v_out, b * G + (g + 1))
                if late(b * G + g):
                    pe.wait_ge(normed, b * G + g)
                for h in range(HG):
                    v = HG * g + h
                    products = [(ph_l[:, g % 2, h], vh_l[:, u, v]), (ph_l[:, g % 2, h], vl_l[:, u, v]), (pl_l[:, g % 2, h], vh_l[:, u, v]),
                                (ph_c[:, g % 2, h], vh_c[:, u, v]), (ph_c[:, g % 2, h], vl_c[:, u, v]), (pl_c[:, g % 2, h], vh_c[:, u, v])]
                    for i, (x, y) in enumerate(products):
                        last = pe.matmul(mix[:, h], x, y, start=i == 0, stop=i == len(products) - 1)
                last.then_inc(mixed, 1)

            def values(b, g, u):
                pe.wait_ge(staged, b + 1)
                if late(b * G + g):
                    pe.wait_ge(v_out, b * G + g)
                cols = slice(VW * g, VW * g + VW)
                for dst, part in ((v_l, LAT), (v_c, CTX)):
                    kh, kl = keys[:, u, HI, part], keys[:, u, LO, part]
                    last = three(dst, ((kh, w.v1h[:, cols]), (kh, w.v1l[:, cols]), (kl, w.v1h[:, cols])))
                last.then_inc(v_done, 1)

            def turn(t, half, u):
                pe.wait_ge(normed, t * G + (2 + 2 * half))
                if half == 1:
                    pe.wait_ge(ot_lo, t * 2 + 1)
                elif late(t):
                    pe.wait_ge(out_copied, t)
                for i in range(4):
                    h = 2 * (4 * half + i)
                    last = pe.transpose(out_t[:, i], heads_out[:, u, h:h + 2].rearrange("p h k -> p (h k)"), w.ident[:])
                last.then_inc(turned, 1)

            def project(t):
                pe.wait_ge(ot_lo, t * 2 + 2)
                for i in range(H // 2):
                    for j, (x, wt) in enumerate(((turned_h, w.o1h), (turned_h, w.o1l), (turned_l, w.o1h))):
                        last = pe.matmul(out_p, x[:, i], wt[:, i], start=i == 0 and j == 0, stop=i == H // 2 - 1 and j == 2)
                last.then_inc(projected, 1)

            def body(b, u, first, last):
                for g in range(G):
                    scores_by_key(b, g, u, turns=g < 2 and not first)
                    if not (last and g + 2 >= G):
                        make_t(*after(b, g, u, 2))
                    if not (last and g + 1 >= G):
                        scores(*after(b, g, u, 1))
                    if not (first and g == 0):
                        mix_values(*before(b, g, u))
                    if not (last and g > 0):
                        values(*after(b, g, u, VALUES_AHEAD))
                    if not first and g == 1:
                        project(b - 1)


            make_t(0, 0, 0)
            make_t(0, 1, 0)
            scores(0, 0, 0)
            pe.wait_ge(ones_in, 4)
            for g in range(VALUES_AHEAD):
                values(0, g, 0)
            sequences(pe, body)
            end = (B - 1) % 2
            mix_values(B - 1, G - 1, end)
            turn(B - 1, 0, end)
            turn(B - 1, 1, end)
            project(B - 1)

        @block.scalar
        def _(act):
            def t_high(b, g, u):
                act.wait_ge(t_done, b * G + (g + 1))
                act.activation(th[:, g], t_bank, ACT.Copy, scale=1.0 / AS).then_inc(t_hi, 1)

            def exp(b, g, u, outs):
                act.wait_ge(shifted, 2 * (b * G) + (2 * g + 1))
                if late(b * G + g, 2):
                    act.wait_ge(mixed, b * G + (g - 1))
                if late(b * G + g, 2):
                    act.wait_ge(p_split, b * G + (g - 1))
                for dst in (probs_l, ph_l):
                    last = act.activation(dst[:, g % 2], by_key_l, ACT.Exp)
                last.then_inc(exped_l, 1)
                if outs:
                    out_high(b - 1, g)
                act.wait_ge(shifted, 2 * (b * G) + (2 * g + 2))
                act.sem_inc(act_waited, 1)
                for dst in (probs_c, ph_c):
                    last = act.activation(dst[:, g % 2], by_key_c, ACT.Exp, bias=w.mask_bias[:, 0, bass.ds(b, 1)])
                last.then_inc(exped_c, 1)

            def values_out(b, g, u):
                act.wait_ge(v_done, b * G + (g + 1))
                if late(b, 2) and g == 0:
                    act.wait_ge(mixed, (b - 1) * G)
                for dst, src in ((vh_l, v_l), (vh_c, v_c)):
                    last = act.activation(dst[:, u, HG * g:HG * g + HG, 0:DK1], src.rearrange("p (h k) -> p h k", k=DK1),
                                          ACT.Copy, scale=1.0 / WS)
                last.then_inc(v_hi, 1)

            def out_high(t, half):
                act.wait_ge(turned, t * 2 + (half + 1))
                if late(t) and half == 0:
                    act.wait_ge(projected, t)
                act.activation(turned_h[:, 4 * half:4 * half + 4], out_t, ACT.Copy).then_inc(ot_hi, 1)

            def copy_out(t):
                act.wait_ge(projected, t + 1)
                if late(t):
                    act.wait_ge(out_normed, t)
                act.activation(out[:], out_p, ACT.Copy).then_inc(out_copied, 1)

            def body(b, u, first, last):
                for g in range(G):
                    if g == 2 and not first:
                        copy_out(b - 1)
                    exp(b, g, u, outs=g < 2 and not first)
                    if not (last and g + 2 >= G):
                        t_high(*after(b, g, u, 2))
                    if not (last and g > 0):
                        values_out(*after(b, g, u, VALUES_AHEAD))


            t_high(0, 0, 0)
            t_high(0, 1, 0)
            for g in range(VALUES_AHEAD):
                values_out(0, g, 0)
            sequences(act, body)
            out_high(B - 1, 0)
            out_high(B - 1, 1)
            copy_out(B - 1)

        @block.vector
        def _(dve):
            def t_low(b, g, u):
                dve.wait_ge(t_hi, b * G + (g + 1))
                dve.scalar_tensor_tensor(tl[:, g].rearrange("p h s -> p (h s)"), bank[0][:, :], 1.0 / AS,
                                         th[:, g].rearrange("p h s -> p (h s)"), ALU.mult, ALU.subtract).then_inc(t_lo, 1)

            def maximum(b, g, u):
                dve.wait_ge(scored, b * G + (g + 1))
                for i in range(2):
                    last = dve.tensor_reduce(negmax[:, g, 2 * i:2 * i + 2], score[i], AX.X, ALU.max, negate=True)
                last.then_inc(maxed, 1)

            def values_low(b, g, u):
                dve.wait_ge(v_hi, b * G + (g + 1))
                for dst, high, src in ((vl_l, vh_l, v_l), (vl_c, vh_c, v_c)):
                    cols = slice(HG * g, HG * g + HG)
                    last = dve.scalar_tensor_tensor(dst[:, u, cols, 0:DK1], src.rearrange("p (h k) -> p h k", k=DK1), 1.0 / WS,
                                                    high[:, u, cols, 0:DK1], ALU.mult, ALU.subtract)
                last.then_inc(v_out, 1)

            def normalise(b, g, u):
                dve.wait_ge(mixed, b * G + (g + 1))
                dve.reciprocal(recip[:], mix[:, :, DK1]).then_inc(nchain, 1)
                dve.wait_ge(nchain, b * G + (g + 1))
                if late(b, 2) and g == 0:
                    dve.wait_ge(turned, (b - 1) * 2)
                dve.tensor_tensor(heads_out[:, u, HG * g:HG * g + HG], mix[:, :, 0:DK1],
                                  recip[:].unsqueeze(2).broadcast_to([S, HG, DK1]), ALU.mult).then_inc(normed, 1)

            def out_low(t, half):
                dve.wait_ge(ot_hi, t * 2 + (half + 1))
                dve.tensor_tensor(turned_l[:, 4 * half:4 * half + 4], out_t, turned_h[:, 4 * half:4 * half + 4],
                                  ALU.subtract).then_inc(ot_lo, 1)

            def stage(b, u):
                if late(b, 2):
                    dve.wait_ge(shifted, 2 * G * (b - 1))
                dve.sem_inc(waited, 1)
                dve.tensor_copy(keys[:, u].rearrange("p v k -> p (v k)"),
                                kv[:, bass.ds(b, 1), :, :].rearrange("p o v k -> p (o v k)")).then_inc(staged, 1)

            LINKS = 11

            def statistics(t):
                link = linker(dve, chain, t * LINKS)
                dve.wait_ge(out_copied, t + 1)
                link(dve.bn_stats(bn[:], out[:]))
                dve.sem_inc(waited, 1)
                link(dve.bn_aggr(mv[:, 0], bn[:]))
                link(dve.tensor_scalar(t1[:], mv[:, 0, 1:2], 0.5 / (WS * WS), 0.5 * EPS, ALU.mult, ALU.add))
                link(dve.tensor_single_scalar(t2[:].bitcast(INT32), t1[:].bitcast(INT32), 1, ALU.arith_shift_right))
                link(dve.tensor_scalar(rstd[:].bitcast(INT32), t2[:].bitcast(INT32), -1.0,
                                       float(0x5F3759DF - 0x400000 - 0x80000000), ALU.mult, ALU.add))

            def newton(t, i):
                link = linker(dve, chain, t * LINKS + 5 + 2 * i)
                link(dve.scalar_tensor_tensor(t2[:], rstd[:], t1[:], rstd[:], ALU.mult, ALU.mult))
                link(dve.scalar_tensor_tensor(rstd[:], t2[:], 1.5, rstd[:], ALU.subtract, ALU.mult))

            def out_norm(t):
                if late(t):
                    dve.wait_ge(summed, t)
                dve.tensor_scalar(zn[:], out[:], mv[:, 0, 0:1], rstd[:], ALU.subtract, ALU.mult).then_inc(out_normed, 1)

            def body(b, u, first, last):
                for g in range(G):
                    if g < 2 and not first:
                        out_low(b - 1, g)
                    if not (last and g + 1 >= G):
                        maximum(*after(b, g, u, 1))
                    if g == 0 and not first:
                        normalise(b - 1, G - 1, 1 - u)
                    if g == 0 and not last:
                        stage(b + 1, 1 - u)
                    if g == 2 and not first:
                        statistics(b - 1)
                    if not (last and g + 2 >= G):
                        t_low(*after(b, g, u, 2))
                    if g > 0:
                        normalise(b, g - 1, u)
                    if g == 2 and not first:
                        newton(b - 1, 0)
                    if not (last and g > 0):
                        values_low(*after(b, g, u, VALUES_AHEAD))
                    if g == 2 and not first:
                        newton(b - 1, 1)
                    if g == 3 and not first:
                        newton(b - 1, 2)
                        out_norm(b - 1)

            for x, value in ((vh_l, 1.0), (vh_c, 1.0), (vl_l, 0.0), (vl_c, 0.0)):
                dve.memset(x[:, :, :, DK1:DK1 + 1], value).then_inc(ones_in, 1)
            stage(0, 0)
            t_low(0, 0, 0)
            t_low(0, 1, 0)
            maximum(0, 0, 0)
            for g in range(VALUES_AHEAD):
                values_low(0, g, 0)
            sequences(dve, body)
            end = (B - 1) % 2
            normalise(B - 1, G - 1, end)
            out_low(B - 1, 0)
            out_low(B - 1, 1)
            statistics(B - 1)
            for i in range(3):
                newton(B - 1, i)
            out_norm(B - 1)


def mixture(nc, a, w, bank, xh, xl):
    with Memory(nc, "mixture") as m:
        xs = m.sb("xs", [D, 2, 2, N], FP16)
        tanh, half = m.sb("tanh", [128, MH, N]), m.sb("half", [128, MH, N])
        hidden = m.sb("hidden", [128, 2, MH, N])
        part = m.sb("part", [S, 2, CH, D])
        gate2, gate = m.sb("gate2", [S, CH, 2, E]), m.sb("gate", [S, CH, E])
        top, index = m.sb("top", [S, CH, 8]), m.sb("index", [S, CH, 8], UINT32)
        chosen = m.sb("chosen", [S, CH, 2])
        diff, expd, p1, p2 = (m.sb(n, [S, CH]) for n in ("diff", "expd", "p1", "p2"))
        is1, is2 = m.sb("is1", [S, CH, E]), m.sb("is2", [S, CH, E])
        weight = m.sb("weight", [S, 2, CH, E])
        staged, gated, diffed, gexped, weighed, h_done, tanhed, halved, hid_in, y_done, combined, added, chain, stored, waited, pool_waited = (
            m.sem(n) for n in ("staged", "gated", "diffed", "gexped", "weighed", "h_done", "tanhed", "halved", "hid_in",
                               "y_done", "combined", "added", "chain", "stored", "waited", "pool_waited"))
        block = m.block()
        h1, h2 = [bank[i][:, :] for i in (0, 1)], [bank[i][:, :] for i in (2, 3)]
        y = [bank[4 + i][:, :].rearrange("p (c d) -> p c d", d=D) for i in range(2)]
        gates = bank[6][:, 0:CH * 2 * E]

        def chunks(eng, body):
            body(0, 0)
            with eng.Fori(0, (NCH - 2) // 2) as i:
                body(i * 2 + 1, 1)
                body(i * 2 + 2, 0)
            body(NCH - 1, (NCH - 1) % 2)

        def within(k):
            return not isinstance(k, int) or k + 1 < NCH

        @block.gpsimd
        def _(pool):
            def stage(k, u):
                chunk = bass.ds(k * CH, CH)
                for i, x in enumerate((xh, xl)):
                    last = pool.tensor_copy(xs[:, u, i].rearrange("p (c s) -> p c s", s=S), x[:, chunk, :])
                last.then_inc(staged, 1)

            def add(k, e):
                n = k * E + e
                rows = w.X[:, bass.ds(k * CH, CH), :]
                pool.wait_ge(combined, n + 1)
                if late(n):
                    pool.wait_ge(added, n)
                pool.sem_inc(pool_waited, 1)
                pool.tensor_tensor(rows, rows, part[:, e % 2], ALU.add).then_inc(added, 1)

            def body(k, u):
                for e in range(E):
                    if e > 0:
                        add(k, e - 1)
                    elif late(k):
                        add(k - 1, E - 1)
                    if e == 0 and within(k):
                        if late(k):
                            pool.wait_ge(h_done, k * (E * MH))
                        stage(k + 1, 1 - u)

            stage(0, 0)
            chunks(pool, body)
            add(NCH - 1, E - 1)

        @block.sync
        def _(sp):
            with sp.Fori(0, NCH) as i:
                chunk = bass.ds(i * CH, CH)
                sp.wait_ge(added, i * E + E)
                sp.dma_start(a["out"].rearrange("b s d -> s b d")[:, chunk, :], w.X[:, chunk, :]).then_inc(stored, 16)
            sp.wait_ge(stored, 16 * NCH)

        @block.tensor
        def _(pe):
            def choose(k, u):
                pe.wait_ge(staged, k + 1)
                for c in range(CH):
                    dst = gates[:, 2 * E * c:2 * E * c + 2 * E]
                    for i in range(2):
                        last = pe.matmul(dst, xs[:, u, i, S * c:S * c + S], w.wgt[:].rearrange("p i e -> p (i e)"),
                                         start=i == 0, stop=i == 1)
                last.then_inc(gated, 1)

            def rise(k, u, e, j):
                n = k * (E * MH) + (MH * e + j)
                if e == 0 and j == 0:
                    pe.wait_ge(staged, k + 1)
                if late(n, 2):
                    pe.wait_ge(hid_in, n - 1)
                for dst, i in ((h1[j], 0), (h2[j], 1)):
                    wh, wl = w.moeh[:, i, MH * e + j], w.moel[:, i, MH * e + j]
                    pe.matmul(dst, wh, xs[:, u, 0], start=True, stop=False)
                    pe.matmul(dst, wl, xs[:, u, 0], start=False, stop=False)
                    last = pe.matmul(dst, wh, xs[:, u, 1], start=False, stop=True)
                last.then_inc(h_done, 1)

            def fall(k, e):
                n = k * E + e
                pe.wait_ge(hid_in, n * MH + MH)
                if late(n, 2):
                    pe.wait_ge(combined, n - 1)
                for c in range(CH):
                    for j in range(MH):
                        last = pe.matmul(y[e % 2][:, c], hidden[:, e % 2, j, S * c:S * c + S], w.w3t[:, MH * e + j],
                                         start=j == 0, stop=j == MH - 1)
                last.then_inc(y_done, 1)

            def body(k, u):
                for e in range(E):
                    for j in range(MH):
                        rise(k, u, e, j)
                    if e > 0:
                        fall(k, e - 1)
                    elif late(k):
                        fall(k - 1, E - 1)
                    if e == 4 and within(k):
                        choose(k + 1, 1 - u)

            choose(0, 0)
            chunks(pe, body)
            fall(NCH - 1, E - 1)

        @block.scalar
        def _(act):
            def gate_exp(k):
                act.wait_ge(diffed, k + 1)
                act.activation(expd[:], diff[:], ACT.Exp).then_inc(gexped, 1)

            def body(k, u):
                for e in range(E):
                    for j in range(MH):
                        n = k * (E * MH) + (MH * e + j)
                        act.wait_ge(h_done, n + 1)
                        if late(n, 2):
                            act.wait_ge(halved, n - 1)
                        act.activation(tanh[:, j], h1[j], ACT.Tanh, scale=0.5 / WS).then_inc(tanhed, 1)
                    if e == 5 and within(k):
                        gate_exp(k + 1)

            gate_exp(0)
            chunks(act, body)

        @block.vector
        def _(dve):
            GATE_LINKS = 13

            def gates_in(k):
                link = linker(dve, chain, k * GATE_LINKS)
                dve.wait_ge(gated, k + 1)
                link(dve.tensor_scalar(gate2[:].rearrange("p c i e -> p (c i e)"), gates, 1.0 / WS, None, ALU.mult))
                link(dve.tensor_tensor(gate[:], gate2[:, :, 0], gate2[:, :, 1], ALU.add))
                dve.sem_inc(waited, 1)
                for c in range(CH):
                    last = dve.max(top[:, c], gate[:, c])
                link(last)
                dve.sem_inc(waited, 1)
                for c in range(CH):
                    last = dve.max_index(index[:, c], top[:, c], gate[:, c])
                link(last)
                link(dve.tensor_copy(chosen[:], index[:, :, 0:2]))
                dve.tensor_tensor(diff[:], top[:, :, 1], top[:, :, 0], ALU.subtract).then_inc(diffed, 1)

            def weigh(k, u):
                link = linker(dve, chain, k * GATE_LINKS + 5)
                dve.wait_ge(gexped, k + 1)
                link(dve.tensor_scalar(p1[:], expd[:], 1.0, None, ALU.add))
                link(dve.reciprocal(p1[:], p1[:]))
                link(dve.tensor_scalar(p1[:], p1[:], w.moe_out[:], None, ALU.mult))
                link(dve.tensor_scalar(p2[:], p1[:], -1.0, w.moe_out[:], ALU.mult, ALU.add))
                for dst, i in ((is1, 0), (is2, 1)):
                    link(dve.tensor_tensor(dst[:], w.iota[:].unsqueeze(1).broadcast_to([S, CH, E]),
                                           chosen[:, :, i:i + 1].broadcast_to([S, CH, E]), ALU.is_equal))
                    link(dve.tensor_tensor(dst[:], dst[:], (p1, p2)[i][:].unsqueeze(2).broadcast_to([S, CH, E]), ALU.mult))
                dve.tensor_tensor(weight[:, u], is1[:], is2[:], ALU.add).then_inc(weighed, 1)
                dve.wait_ge(weighed, k + 1)

            def hide(k, e, j):
                n = k * (E * MH) + (MH * e + j)
                dve.wait_ge(tanhed, n + 1)
                dve.scalar_tensor_tensor(half[:, j], tanh[:, j], 1.0, h1[j], ALU.add, ALU.mult).then_inc(halved, 1)
                dve.wait_ge(halved, n + 1)
                if j == 0 and late(k * E + e, 2):
                    dve.wait_ge(y_done, k * E + (e - 1))
                dve.tensor_tensor(hidden[:, e % 2, j], half[:, j], h2[j], ALU.mult).then_inc(hid_in, 1)

            def combine(k, u, e):
                n = k * E + e
                dve.wait_ge(y_done, n + 1)
                if late(n, 2):
                    dve.wait_ge(added, n - 1)
                dve.tensor_tensor(part[:, e % 2], y[e % 2], weight[:, u, :, e:e + 1].broadcast_to([S, CH, D]),
                                  ALU.mult).then_inc(combined, 1)

            def body(k, u):
                for e in range(E):
                    for j in range(MH):
                        hide(k, e, j)
                    if e > 0:
                        combine(k, u, e - 1)
                    elif late(k):
                        combine(k - 1, 1 - u, E - 1)
                    if e == 5 and within(k):
                        gates_in(k + 1)
                    if e == 6 and within(k):
                        weigh(k + 1, 1 - u)

            gates_in(0)
            weigh(0, 0)
            chunks(dve, body)
            combine(NCH - 1, (NCH - 1) % 2, E - 1)


def flamingo(nc, a):
    with ExitStack() as stack:
        def sb(name, shape, dt=FP32):
            return stack.enter_context(nc.sbuf_tensor(name, shape, dt))

        w = Weights()
        bank = [stack.enter_context(nc.psum_tensor(f"bank{i}", [128, 512], FP32)) for i in range(8)]
        w.X = sb("X", [S, B, D])
        w.mv, w.rstd = sb("mv", [S, B, 2]), sb("rstd", [S, B])
        w.rstd_c, w.shift_c = sb("rstd_c", [C, B]), sb("shift_c", [C, B])
        w.ident, w.identh = sb("ident", [128, 128]), sb("identh", [128, 128], FP16)
        w.head_rows = sb("head_rows", [R0, HG], FP16)
        w.iota = sb("iota", [128, E])
        w.mask01, w.mask_bias = sb("mask01", [128, B, C], FP16), sb("mask_bias", [C, 1, B])
        w.q0h, w.q0l, w.k0h, w.k0l = (sb(n, [D, G, 3, 32], FP16) for n in ("q0h", "q0l", "k0h", "k0l"))
        w.v0h, w.v0l = sb("v0h", [D, D], FP16), sb("v0l", [D, D], FP16)
        w.o0h, w.o0l = sb("o0h", [D, 1, D], FP16), sb("o0l", [D, 1, D], FP16)
        w.bias0, w.tg0 = sb("bias0", [128, D]), sb("tg0", [128, 1])
        w.taph, w.tapl = sb("taph", [D, 3, M0, 128], FP16), sb("tapl", [D, 3, M0, 128], FP16)
        w.conv_b, w.conv_b_half = sb("conv_b", [128, M0]), sb("conv_b_half", [128, M0])
        w.w2t, w.ffn_out = sb("w2t", [128, M0, D], FP16), sb("ffn_out", [128, 1])
        w.gb = sb("gb", [D, 4])
        w.ah, w.al = sb("ah", [D, H, D], FP16), sb("al", [D, H, D], FP16)
        w.v1h, w.v1l = sb("v1h", [D, H * DK1], FP16), sb("v1l", [D, H * DK1], FP16)
        w.o1h, w.o1l = sb("o1h", [128, H // 2, D], FP16), sb("o1l", [128, H // 2, D], FP16)
        w.gain1, w.bias1 = sb("gain1", [128, D]), sb("bias1", [128, D])
        w.wgt = sb("wgt", [D, 2, E], FP16)
        w.moeh, w.moel = sb("moeh", [D, 2, E * MH, 128], FP16), sb("moel", [D, 2, E * MH, 128], FP16)
        w.w3t, w.moe_out = sb("w3t", [128, E * MH, D]), sb("moe_out", [128, 1])

        with ExitStack() as ctx_stack:
            w.ctx = ctx_stack.enter_context(nc.sbuf_tensor("ctx", [C, B, D], FP32))
            setup(nc, a, w, bank)
            with Memory(nc, "layer0") as m:
                xh, xl = m.sb("xh", [D, B, S], FP16), m.sb("xl", [D, B, S], FP16)
                ch, cl = m.sb("ch", [D, B, C], FP16), m.sb("cl", [D, B, C], FP16)
                qst, kst = m.sb("qst", [R0, G, B, S], FP16), m.sb("kst", [R0, G, B, C], FP16)
                vals = m.sb("vals", [C, B, 2, H, DK0 + 1], FP16)
                split_transposed(nc, w, bank, "split0", [
                    Split("ctx", C, w.ctx, lambda c: ch[:, c, :], lambda c: cl[:, c, :]),
                    Split("x", S, w.X, lambda c: xh[:, c, :], lambda c: xl[:, c, :], "vector", w.mv, w.rstd)])
                project0(nc, w, bank, xh, xl, ch, cl, qst, kst, vals)
                attention0(nc, w, bank, qst, kst, vals)
            feed_forward0(nc, w, bank)
            with Memory(nc, "layer1") as m:
                kv = m.sb("kv", [D, B, 3, KV], FP16)
                gain_l, bias_l, gain_x, bias_x = (w.gb[:, i:i + 1] for i in range(4))
                split_transposed(nc, w, bank, "split1", [
                    Split("ctx", C, w.ctx, lambda c: kv[:, c, 0, S:KV], lambda c: kv[:, c, 1, S:KV],
                          "gpsimd", rstd=w.rstd_c, shift=w.shift_c, gain=gain_x, bias=bias_x),
                    Split("x", S, w.X, lambda c: kv[:, c, 0, 0:S], lambda c: kv[:, c, 1, 0:S],
                          "vector", w.mv, w.rstd, gain=gain_l, bias=bias_l)], before=latent_scale(w))
                mask_keys(nc, w, kv)
                attention1(nc, w, bank, kv)
        with Memory(nc, "moe") as m:
            xh, xl = m.sb("xh", [D, B, S], FP16), m.sb("xl", [D, B, S], FP16)
            split_transposed(nc, w, bank, "split2", [
                Split("x", S, w.X, lambda c: xh[:, c, :], lambda c: xl[:, c, :], "vector", w.mv, w.rstd)], before=row_scale(w))
            mixture(nc, a, w, bank, xh, xl)


_INS = {'x': 'x', 'ctx': 'ctx_1024', 'mask': 'mask_BxS2_bf1', 'gx': 'g_xattn', 'gf': 'g_ffn',
        'q0': 'L0_xattn_W_q', 'k0': 'L0_xattn_W_k', 'v0': 'L0_xattn_W_v', 'o0': 'L0_xattn_W_o', 'bo0': 'L0_xattn_b_o',
        'fw1': 'L0_ffn_w1', 'cw': 'L0_ffn_conv_w', 'cb': 'L0_ffn_conv_b', 'fw2': 'L0_ffn_w2',
        'gx1': 'L1_xattn_g_x', 'bx1': 'L1_xattn_b_x', 'gl1': 'L1_xattn_g_l', 'bl1': 'L1_xattn_b_l',
        'q1': 'L1_xattn_Wq', 'kv1': 'L1_xattn_Wkv', 'o1': 'L1_xattn_Wout', 'go1': 'L1_xattn_g_o', 'bo1': 'L1_xattn_b_o',
        'wg': 'L1_ffn_Wg', 'w1': 'L1_ffn_W1', 'w2': 'L1_ffn_W2', 'w3': 'L1_ffn_W3'}


def kernel(**inputs):
    import numpy as _np
    import concourse.bacc as _bacc
    from concourse import mybir as _mybir
    from concourse.bass_utils import run_bass_kernel_spmd as _run

    nc = _bacc.Bacc("TRN2", target_bir_lowering=False, num_devices=1)
    arrays, aps = {}, {}
    for short, name in _INS.items():
        v = _np.ascontiguousarray(inputs[name])
        if v.dtype == _np.bool_:
            v = v.view(_np.uint8)
        arrays[f"in_{short}"] = v
        aps[short] = nc.dram_tensor(f"in_{short}", v.shape, _mybir.dt.from_np(v.dtype), kind="ExternalInput").ap()
    aps["out"] = nc.dram_tensor("out", (B, S, D), _mybir.dt.float32, kind="ExternalOutput").ap()
    flamingo(nc, aps)
    r = _run(nc, [arrays], core_ids=[0])
    return r.results[0]["out"]
```

```python
import concourse.bass as bass
from concourse import mybir
from contextlib import ExitStack

FP32 = mybir.dt.float32
FP16 = mybir.dt.float16
INT32 = mybir.dt.int32
UINT32 = mybir.dt.uint32
UINT8 = mybir.dt.uint8
ALU = mybir.AluOpType
ACT = mybir.ActivationFunctionType
AX = mybir.AxisListType

B, S, D = 32, 128, 128
C = 77
H = 16
DK0 = D // H
DK1 = 64
G = 4
HG = H // G
KV = S + C
HID = 512
M0 = HID // 128
E, MH = 8, 2
R0 = 3 * HG * DK0
CH = 4
NCH = B // CH
N = CH * S
EPS = 1e-5
ROUND = 1.5 * 2.0 ** 23
WS = 64.0
AS = 1024.0
MASKED = -30000.0


class Weights:
    pass


def late(x, least=1):
    return not isinstance(x, int) or x >= least


def rsqrt(dve, link, out, var, t1, t2):
    link(dve.tensor_scalar(t1, var, EPS, None, ALU.add))
    link(dve.tensor_single_scalar(t2.bitcast(INT32), t1.bitcast(INT32), 1, ALU.arith_shift_right))
    link(dve.tensor_scalar(out.bitcast(INT32), t2.bitcast(INT32), -1.0, float(0x5F3759DF), ALU.mult, ALU.add))
    for _ in range(3):
        link(dve.scalar_tensor_tensor(t2, out, -0.5, out, ALU.mult, ALU.mult))
        link(dve.tensor_tensor(t2, t2, t1, ALU.mult))
        link(dve.scalar_tensor_tensor(out, t2, 1.5, out, ALU.add, ALU.mult))


def row_statistics(dve, link, w, bn):
    for b in range(B):
        last = dve.bn_stats(bn[:, b], w.X[:, b])
    link(last)
    for b in range(B):
        last = dve.bn_aggr(w.mv[:, b], bn[:, b])
    link(last)


def linker(eng, sem, base=0):
    n = [0]

    def link(ins):
        n[0] += 1
        ins.then_inc(sem, 1)
        eng.wait_ge(sem, base + n[0])
    return link


class Memory:

    def __init__(self, nc, tag):
        self.nc, self.tag, self.stack = nc, tag, ExitStack()

    def __enter__(self):
        return self

    def __exit__(self, *e):
        return self.stack.__exit__(*e)

    def sb(self, name, shape, dt=FP32):
        return self.stack.enter_context(self.nc.sbuf_tensor(f"{self.tag}_{name}", shape, dt))

    def sem(self, name):
        return self.stack.enter_context(self.nc.semaphore(f"{self.tag}_{name}"))

    def block(self):
        return self.stack.enter_context(self.nc.Block())


def setup(nc, a, w, bank):
    with Memory(nc, "setup") as m:
        nat_q0, nat_k0, nat_v0 = (m.sb(n, [128, D]) for n in ("nat_q0", "nat_k0", "nat_v0"))
        nat_o0 = m.sb("nat_o0", [128, 1, D])
        nat_f = m.sb("nat_f", [128, 2, HID])
        conv_w, conv_b = m.sb("conv_w", [128, M0, 3]), w.conv_b
        nat_q1, nat_k1, nat_v1 = (m.sb(n, [128, H * DK1]) for n in ("nat_q1", "nat_k1", "nat_v1"))
        nat_o1 = m.sb("nat_o1", [128, H // 2, D])
        nat_moe = m.sb("nat_moe", [128, 2, E * MH, D])
        nat_w3 = m.sb("nat_w3", [128, E * MH, D])
        nat_g = m.sb("nat_g", [E, 1, D])
        mask_u8, mask_f = m.sb("mask_u8", [B, C], UINT8), m.sb("mask_f", [B, 1, C])
        mask_rows = m.sb("mask_rows", [128, B * C], UINT8)
        gates, tanhs = m.sb("gates", [128, 4]), m.sb("tanhs", [128, 4])
        rows = m.sb("rows", [128, 3, D])
        bn = m.sb("bn", [128, B, 6])
        absum, wmean, winv = m.sb("absum", [128, 2]), m.sb("wmean", [128, 2]), m.sb("winv", [128, 2])
        ones = m.sb("ones", [128, 128])
        cs = m.sb("cs", [128, M0, 3])
        tap_w = m.sb("tap_w", [128, 3, M0, D])
        q1t, k1t = m.sb("q1t", [128, H // 2, D]), m.sb("k1t", [128, H // 2, D])
        comp = m.sb("comp", [128, 4, D], FP16)
        t1, t2 = m.sb("t1", [128, B]), m.sb("t2", [128, B])
        iota_i = m.sb("iota_i", [128, E], INT32)

        x_in = [m.sem(f"x_in{i}") for i in range(4)]
        ctx_in, l0_in, ffn_in, l1_in, moe_in, small_in = (
            m.sem(n) for n in ("ctx_in", "l0_in", "ffn_in", "l1_in", "moe_in", "small_in"))
        made, tanh_done, summed, quant_done, chain, tiles_done, hi_done, lo_done, plain_hi, mask_done, pchain = (
            m.sem(n) for n in ("made", "tanh_done", "summed", "quant_done", "chain", "tiles_done", "hi_done",
                               "lo_done", "plain_hi", "mask_done", "pchain"))
        block = m.block()

        LD_L1, LD_MOE, LD_SMALL, QUANT, TAPS = range(5)
        tiles = []
        for t in range(3):
            tiles.append((tap_w[:, t], TAPS, w.taph[:, t], w.tapl[:, t], WS))
        tiles.append((nat_f[:, 1].rearrange("p (t n) -> p t n", n=128), QUANT, w.w2t[:], None, 1.0))
        tiles.append((nat_g[:], LD_SMALL, w.wgt[:, 0:1, :], w.wgt[:, 1:2, :], WS))
        tiles.append((mask_f[:], LD_SMALL, w.mask_bias[:], None, 1.0))
        FIRST_L1 = len(tiles)
        for i in range(2):
            tiles.append((nat_q1[:, 512 * i:512 * i + 512].rearrange("p (t n) -> p t n", n=128), LD_L1,
                          q1t[:, 4 * i:4 * i + 4, :], None, 1.0))
            tiles.append((nat_k1[:, 512 * i:512 * i + 512].rearrange("p (t n) -> p t n", n=128), LD_L1,
                          k1t[:, 4 * i:4 * i + 4, :], None, 1.0))
        tiles.append((nat_o0[:], LD_L1, w.o0h[:], w.o0l[:], WS))
        L1_TILES = len(tiles) - 1
        for s in range(2):
            for i in range(4):
                tiles.append((nat_moe[:, s, 4 * i:4 * i + 4], LD_MOE, w.moeh[:, s, 4 * i:4 * i + 4],
                              w.moel[:, s, 4 * i:4 * i + 4], WS))
        for i in range(4):
            tiles.append((nat_w3[:, 4 * i:4 * i + 4], LD_MOE, w.w3h[:, 4 * i:4 * i + 4], w.w3l[:, 4 * i:4 * i + 4], WS))
        NT = len(tiles)
        NB = 6

        def lows(k):
            return sum(lo is not None for _, _, _, lo, _ in tiles[:k])

        def tile_bank(k, src):
            p, t, n = src.shape
            return bank[k % NB][0:n, 0:t * p].rearrange("q (t p) -> q t p", p=p)

        def product_bank(g):
            return bank[(NT + g) % NB][:, :].rearrange("q (t p) -> q t p", p=128)

        def product_heads(g):
            first = 2 * HG * (g // 2) + g % 2
            return slice(first, first + 2 * HG - 1, 2)

        @block.sync
        def _(sp):
            xv = a["x"].rearrange("b s d -> s b d")
            for i in range(4):
                sp.dma_start(w.X[:, 8 * i:8 * i + 8, :], xv[:, 8 * i:8 * i + 8, :]).then_inc(x_in[i], 16)
            for i, src in enumerate((a["w1"], a["w2"])):
                sp.dma_start(nat_moe[:, i], src.rearrange("e (m p) d -> p (e m) d", p=128)).then_inc(moe_in, 16)
            sp.dma_start(nat_w3[:].rearrange("p (e m) d -> p e m d", m=MH),
                         a["w3"].rearrange("e d (m h) -> d e m h", h=128)).then_inc(moe_in, 16)
            sp.dma_start(w.ctx[:], a["ctx"].rearrange("b s d -> s b d")).then_inc(ctx_in, 16)
            for s in (*x_in, ctx_in):
                sp.wait_ge(s, 16)
            sp.wait_ge(moe_in, 48)

        @block.scalar
        def _(act):
            act.dma_start(gates[:, 0:2], a["gx"].rearrange("(o n) -> o n", o=1).broadcast_to([128, 2])).then_inc(small_in, 16)
            act.dma_start(gates[:, 2:4], a["gf"].rearrange("(o n) -> o n", o=1).broadcast_to([128, 2])).then_inc(small_in, 16)
            act.dma_start(nat_f[:, 0].rearrange("p (m d) -> p m d", d=D),
                          a["fw1"].rearrange("(m p) d -> p m d", p=128)).then_inc(ffn_in, 16)
            act.dma_start(nat_f[:, 1], a["fw2"]).then_inc(ffn_in, 16)
            act.dma_start(conv_w[:], a["cw"].rearrange("(m p) o t -> p m (o t)", p=128)).then_inc(ffn_in, 16)
            act.dma_start(conv_b[:], a["cb"].rearrange("(m p) -> p m", p=128),
                          allow_slow_non_contiguous=True).then_inc(ffn_in, 16)
            for dst, src in ((nat_q0, a["q0"]), (nat_k0, a["k0"]), (nat_v0, a["v0"])):
                act.dma_start(dst[:].rearrange("d (h k) -> d h k", k=DK0), src.rearrange("h d k -> d h k")).then_inc(l0_in, 16)
            act.dma_start(nat_g[:, 0], a["wg"]).then_inc(small_in, 16)
            act.dma_start(mask_u8[:], a["mask"]).then_inc(small_in, 16)
            act.dma_start(mask_rows[:], a["mask"].rearrange("(o b) c -> o (b c)", o=1).broadcast_to([128, B * C])).then_inc(small_in, 16)
            for i, src in enumerate((a["bo0"], a["go1"], a["bo1"])):
                act.dma_start(rows[:, i], src.rearrange("(o n) -> o n", o=1).broadcast_to([128, D])).then_inc(small_in, 16)
            for i, src in enumerate((a["gl1"], a["bl1"], a["gx1"], a["bx1"])):
                act.dma_start(w.gb[:, i:i + 1], src.rearrange("(n o) -> n o", o=1)).then_inc(small_in, 16)
            act.dma_start(nat_q1[:], a["q1"]).then_inc(l1_in, 16)
            act.dma_start(nat_k1[:], a["kv1"][:, 0:H * DK1]).then_inc(l1_in, 16)
            act.dma_start(nat_v1[:], a["kv1"][:, H * DK1:]).then_inc(l1_in, 16)
            act.dma_start(nat_o1[:], a["o1"].rearrange("(t p) d -> p t d", p=128)).then_inc(l1_in, 16)
            act.dma_start(nat_o0[:, 0], a["o0"]).then_inc(l1_in, 16)
            act.wait_ge(small_in, 12 * 16)
            act.activation(tanhs[:], gates[:], ACT.Tanh).then_inc(tanh_done, 1)
            act.wait_ge(l0_in, 48)
            act.activation(comp[:, 0], nat_q0[:], ACT.Copy, scale=WS).then_inc(plain_hi, 1)
            act.activation(comp[:, 2], nat_k0[:], ACT.Copy, scale=WS).then_inc(plain_hi, 1)
            act.activation(w.v0h[:], nat_v0[:], ACT.Copy, scale=WS).then_inc(plain_hi, 1)
            for k, (src, _, hi, _, scale) in enumerate(tiles):
                if k == FIRST_L1:
                    act.wait_ge(l1_in, 80)
                    act.activation(w.v1h[:], nat_v1[:], ACT.Copy, scale=WS).then_inc(plain_hi, 1)
                    act.activation(w.o1h[:], nat_o1[:], ACT.Copy, scale=WS).then_inc(plain_hi, 1)
                act.wait_ge(tiles_done, k + 1)
                act.activation(hi, tile_bank(k, src), ACT.Copy, scale=scale).then_inc(hi_done, 1)
            for g in range(G):
                act.wait_ge(tiles_done, NT + g + 1)
                act.activation(w.ah[:, product_heads(g)], product_bank(g), ACT.Copy,
                               scale=AS * DK1 ** -0.5).then_inc(hi_done, 1)

        @block.tensor
        def _(pe):
            pe.wait_ge(made, 2)
            pe.wait_ge(summed, 1)
            pe.matmul(bank[7][:, 0:2], ones[:], absum[:], start=True, stop=True).then_inc(summed, 1)
            for k, (src, stage, _, _, _) in enumerate(tiles):
                if stage == LD_L1:
                    pe.wait_ge(l1_in, 80)
                elif stage == LD_MOE:
                    pe.wait_ge(moe_in, 48)
                elif stage == LD_SMALL:
                    pe.wait_ge(small_in, 12 * 16)
                    pe.wait_ge(mask_done, 1)
                elif stage == TAPS:
                    pe.wait_ge(quant_done, 2)
                elif stage == QUANT:
                    pe.wait_ge(quant_done, 1)
                if k >= NB:
                    pe.wait_ge(hi_done, k - NB + 1)
                    if lows(k - NB + 1):
                        pe.wait_ge(lo_done, lows(k - NB + 1))
                p, t, n = src.shape
                dst = tile_bank(k, src)
                for i in range(t):
                    last = pe.transpose(dst[:, i, :], src[:, i, :], w.ident[0:p, 0:p])
                last.then_inc(tiles_done, 1)
            pe.wait_ge(hi_done, L1_TILES)
            for g in range(G):
                pe.wait_ge(hi_done, NT + g - NB + 1)
                pe.wait_ge(lo_done, lows(NT + g - NB + 1))
                for i in range(HG):
                    half, t = slice(DK1 * (g % 2), DK1 * (g % 2) + DK1), HG * (g // 2) + i
                    last = pe.matmul(product_bank(g)[:, i, :], q1t[half, t, :], k1t[half, t, :],
                                     start=True, stop=True)
                last.then_inc(tiles_done, 1)

        @block.gpsimd
        def _(pool):
            link = linker(pool, pchain)
            link(pool.memset(w.ident[:], 0.0))
            link(pool.memset(w.identh[:], 0.0))
            pool.affine_select(out=w.ident[:], in_=w.ident[:], compare_op=ALU.not_equal, fill=1.0, base=0,
                               pattern=[[-1, 128]], channel_multiplier=1).then_inc(made, 1)
            pool.memset(ones[:], 1.0).then_inc(made, 1)
            pool.affine_select(out=w.identh[:], in_=w.identh[:], compare_op=ALU.not_equal, fill=1.0, base=0,
                               pattern=[[-1, 128]], channel_multiplier=1).then_inc(made, 1)
            link(pool.memset(w.head_rows[:], 0.0))
            for r in range(3):
                blk = w.head_rows[32 * r:32 * r + 32, :]
                link(pool.memset(blk, 1.0))
                link(pool.affine_select(out=blk, in_=blk, compare_op=ALU.is_ge, fill=0.0, base=0,
                                        pattern=[[-DK0, HG]], channel_multiplier=1))
                link(pool.affine_select(out=blk, in_=blk, compare_op=ALU.is_ge, fill=0.0, base=DK0 - 1,
                                        pattern=[[DK0, HG]], channel_multiplier=-1))
            link(pool.iota(iota_i[:], pattern=[[1, E]], base=0, channel_multiplier=0))
            link(pool.tensor_copy(w.iota[:], iota_i[:]))
            pool.wait_ge(small_in, 12 * 16)
            link(pool.tensor_copy(mask_f[:, 0], mask_u8[:]))
            pool.tensor_scalar(mask_f[:, 0], mask_f[:, 0], -1.0, -MASKED, ALU.add, ALU.mult).then_inc(mask_done, 1)
            pool.tensor_copy(w.mask01[:].rearrange("p b c -> p (b c)"), mask_rows[:]).then_inc(mask_done, 1)

        @block.vector
        def _(dve):
            link = linker(dve, chain)
            for b in range(B):
                if b % 8 == 0:
                    dve.wait_ge(x_in[b // 8], 16)
                last = dve.bn_stats(bn[:, b], w.X[:, b])
            link(last)
            for b in range(B):
                last = dve.bn_aggr(w.mv[:, b], bn[:, b])
            link(last)
            rsqrt(dve, link, w.rstd[:], w.mv[:, :, 1], t1[:], t2[:])
            dve.wait_ge(ffn_in, 64)
            link(dve.tensor_reduce(absum[:], nat_f[:], AX.X, ALU.add, apply_absolute_value=True))
            dve.sem_inc(summed, 1)
            dve.wait_ge(summed, 2)
            link(dve.tensor_scalar(wmean[:], bank[7][:, 0:2], 1.0 / (HID * D), 1e-5, ALU.mult, ALU.max))
            link(dve.reciprocal(winv[:], wmean[:]))
            for i in (1, 0):
                link(dve.tensor_scalar(nat_f[:, i], nat_f[:, i], winv[:, i:i + 1], ROUND, ALU.mult, ALU.add))
                link(dve.tensor_scalar(nat_f[:, i], nat_f[:, i], ROUND, 1.0, ALU.subtract, ALU.min))
                ins = dve.tensor_scalar(nat_f[:, i], nat_f[:, i], -1.0, None, ALU.max)
                if i == 1:
                    ins.then_inc(quant_done, 1)
                else:
                    link(ins)
            link(dve.tensor_scalar(cs[:], conv_w[:], wmean[:, 0:1], None, ALU.mult))
            for t in range(3):
                for i in range(M0):
                    last = dve.tensor_scalar(tap_w[:, t, i], nat_f[:, 0, D * i:D * i + D], cs[:, i, t:t + 1], None, ALU.mult)
            link(last)
            dve.sem_inc(quant_done, 1)
            dve.tensor_scalar(w.conv_b_half[:], conv_b[:], 0.5, None, ALU.mult)
            dve.wait_ge(tanh_done, 1)
            dve.tensor_scalar(w.tg0[:], tanhs[:, 0:1], 1.0 / WS, None, ALU.mult)
            dve.tensor_scalar(w.bias0[:], rows[:, 0], tanhs[:, 0:1], None, ALU.mult)
            dve.tensor_scalar(w.gain1[:], rows[:, 1], tanhs[:, 1:2], 1.0 / WS, ALU.mult, ALU.mult)
            dve.tensor_scalar(w.bias1[:], rows[:, 2], tanhs[:, 1:2], None, ALU.mult)
            link(dve.tensor_scalar(w.ffn_out[:], wmean[:, 1:2], 0.5, None, ALU.mult))
            link(dve.tensor_tensor(w.ffn_out[:], w.ffn_out[:], tanhs[:, 2:3], ALU.mult))
            dve.tensor_scalar(w.moe_out[:], tanhs[:, 3:4], 0.5 / WS, None, ALU.mult)
            dve.wait_ge(plain_hi, 3)
            dve.wait_ge(l0_in, 48)
            link(dve.scalar_tensor_tensor(comp[:, 1], nat_q0[:], WS, comp[:, 0], ALU.mult, ALU.subtract))
            link(dve.scalar_tensor_tensor(comp[:, 3], nat_k0[:], WS, comp[:, 2], ALU.mult, ALU.subtract))
            dve.scalar_tensor_tensor(w.v0l[:], nat_v0[:], WS, w.v0h[:], ALU.mult, ALU.subtract)
            for i, dst in enumerate((w.q0h, w.q0l, w.k0h, w.k0l)):
                dve.tensor_copy(dst[:], comp[:, i].rearrange("p (g r) -> p g r", g=G).unsqueeze(2).broadcast_to([128, G, 3, 32]))
            for k, (src, _, hi, lo, scale) in enumerate(tiles):
                if k == FIRST_L1:
                    dve.wait_ge(plain_hi, 5)
                    dve.wait_ge(l1_in, 80)
                    dve.scalar_tensor_tensor(w.v1l[:], nat_v1[:], WS, w.v1h[:], ALU.mult, ALU.subtract)
                    dve.scalar_tensor_tensor(w.o1l[:].rearrange("p t d -> p (t d)"), nat_o1[:].rearrange("p t d -> p (t d)"), WS,
                                             w.o1h[:].rearrange("p t d -> p (t d)"), ALU.mult, ALU.subtract)
                if lo is not None:
                    dve.wait_ge(hi_done, k + 1)
                    dve.scalar_tensor_tensor(lo, tile_bank(k, src), scale, hi, ALU.mult, ALU.subtract).then_inc(lo_done, 1)
            for g in range(G):
                dve.wait_ge(hi_done, NT + g + 1)
                dve.scalar_tensor_tensor(w.al[:, product_heads(g)], product_bank(g), AS * DK1 ** -0.5,
                                         w.ah[:, product_heads(g)], ALU.mult, ALU.subtract).then_inc(lo_done, 1)


class Split:

    def __init__(self, name, rows, src, hi, lo, by=None, mean=None, rstd=None, shift=None, gain=None, bias=None):
        self.name, self.rows, self.src, self.hi, self.lo = name, rows, src, hi, lo
        self.by, self.mean, self.rstd, self.shift, self.gain, self.bias = by, mean, rstd, shift, gain, bias


def split_transposed(nc, w, bank, tag, jobs, before=None, after=None):
    with Memory(nc, tag) as m:
        for at, job in enumerate(jobs):
            n, rows = job.name, job.rows
            job.normed = m.sb(f"normed_{n}", [rows, 2, CH, D]) if job.by else None
            job.whole = m.sb(f"whole_{n}", [128, 2, CH, rows])
            job.ready, job.turned, job.high, job.split = (m.sem(f"{x}_{n}") for x in ("ready", "turned", "high", "split"))
            job.banks = [bank[2 * at + u][:, 0:CH * rows].rearrange("p (c r) -> p c r", r=rows) for u in range(2)]
        chain = m.sem("chain")
        pre, post = (work(m) if work is not None else None for work in (before, after))
        block = m.block()

        def chunks(eng, job, body):
            if job.by == "vector":
                with eng.Fori(0, NCH // 4) as i:
                    for n in range(4):
                        body(i * 4 + n, n % 2)
            else:
                for k in range(NCH):
                    body(k, k % 2)

        def normalise(eng, job, k, u):
            eng.wait_ge(job.turned, k + 1)
            for c in range(CH):
                one = slice(k * CH + c, k * CH + c + 1) if isinstance(k, int) else bass.ds(k * CH + c, 1)
                if job.by == "gpsimd":
                    how = (job.rstd[:, one], job.shift[:, one], ALU.mult, ALU.add)
                else:
                    how = (job.mean[:, one, 0:1], job.rstd[:, one], ALU.subtract, ALU.mult)
                last = eng.tensor_scalar(job.normed[:, u, c:c + 1], job.src[:, one, :], *how)
            last.then_inc(job.ready, 1)

        @block.vector
        def _(dve):
            if pre is not None:
                pre(dve, linker(dve, chain))
            for job in jobs:
                if job.by == "vector":
                    chunks(dve, job, lambda k, u: normalise(dve, job, k, u))
            if post is not None:
                post(dve, linker(dve, chain))

        @block.tensor
        def _(pe):
            for job in jobs:
                def turn(k, u):
                    if job.by:
                        pe.wait_ge(job.ready, k + 1)
                    pe.wait_ge(job.high, k + 1)
                    for c in range(CH):
                        rows = job.normed[:, u, c] if job.by else job.src[:, k * CH + c]
                        last = pe.transpose(job.banks[u][:, c, :], rows, w.ident[0:job.rows, 0:job.rows])
                    last.then_inc(job.turned, 1)

                pe.sem_inc(job.turned, 2)
                chunks(pe, job, turn)

        @block.scalar
        def _(act):
            for job in jobs:
                def copy(k, u):
                    chunk = bass.ds(k * CH, CH)
                    act.wait_ge(job.turned, k + 3)
                    act.wait_ge(job.split, k + 1)
                    for dst in (job.whole[:, u], job.hi(chunk)):
                        if job.gain is None:
                            last = act.activation(dst, job.banks[u], ACT.Copy)
                        else:
                            last = act.activation(dst, job.banks[u], ACT.Identity, bias=job.bias, scale=job.gain)
                    last.then_inc(job.high, 1)

                act.sem_inc(job.high, 2)
                chunks(act, job, copy)

        @block.gpsimd
        def _(pool):
            for job in jobs:
                def low(k, u):
                    chunk = bass.ds(k * CH, CH)
                    pool.wait_ge(job.high, k + 3)
                    pool.tensor_tensor(job.lo(chunk), job.whole[:, u], job.hi(chunk), ALU.subtract).then_inc(job.split, 1)
                    if job.by == "gpsimd" and k + 2 < NCH:
                        normalise(pool, job, k + 2, u)

                pool.sem_inc(job.split, 2)
                if job.by == "gpsimd":
                    normalise(pool, job, 0, 0)
                    normalise(pool, job, 1, 1)
                chunks(pool, job, low)


def project0(nc, w, bank, xh, xl, ch, cl, qst, kst, vals):
    with Memory(nc, "project0") as m:
        q_done, q_hi, q_lo, k_done, k_hi, k_lo, v_done, v_hi, v_out = (
            m.sem(n) for n in ("q_done", "q_hi", "q_lo", "k_done", "k_hi", "k_lo", "v_done", "v_hi", "v_out"))
        block = m.block()
        KC = CH * C
        q_bank = [bank[g][0:R0, :] for g in range(G)]
        k_bank = [bank[4 + g % 2][0:R0, 0:KC] for g in range(G)]
        v_bank = [bank[6 + u][0:C, :] for u in range(2)]
        SQ = DK0 ** -0.5 / WS

        @block.tensor
        def _(pe):
            pe.sem_inc(q_lo, G)
            pe.sem_inc(k_lo, 2)
            pe.sem_inc(v_out, 2)
            with pe.Fori(0, NCH // 2) as i:
                for u in range(2):
                    chunk = bass.ds(i * (2 * CH) + CH * u, CH)
                    for g in range(G):
                        n = G * u + g
                        pe.wait_ge(q_lo, i * (2 * G) + (n + 1))
                        for k, (wt, x) in enumerate(((w.q0h, xh), (w.q0l, xh), (w.q0h, xl))):
                            last = pe.matmul(q_bank[g], wt[:, g].rearrange("p a r -> p (a r)"), x[:, chunk, :],
                                             start=k == 0, stop=k == 2)
                        last.then_inc(q_done, 1)
                        pe.wait_ge(k_lo, i * (2 * G) + (n + 1))
                        for k, (wt, x) in enumerate(((w.k0h, ch), (w.k0l, ch), (w.k0h, cl))):
                            last = pe.matmul(k_bank[g], wt[:, g].rearrange("p a r -> p (a r)"), x[:, chunk, :],
                                             start=k == 0, stop=k == 2)
                        last.then_inc(k_done, 1)
                    pe.wait_ge(v_out, i * 2 + (u + 1))
                    for c in range(CH):
                        one = bass.ds(i * (2 * CH) + (CH * u + c), 1)
                        for k, (x, wt) in enumerate(((ch, w.v0h), (ch, w.v0l), (cl, w.v0h))):
                            last = pe.matmul(v_bank[u][:, D * c:D * c + D], x[:, one, :], wt[:], start=k == 0, stop=k == 2)
                    last.then_inc(v_done, 1)

        @block.scalar
        def _(act):
            with act.Fori(0, NCH // 2) as i:
                for u in range(2):
                    chunk = bass.ds(i * (2 * CH) + CH * u, CH)
                    for g in range(G):
                        n = G * u + g
                        act.wait_ge(q_done, i * (2 * G) + (n + 1))
                        act.activation(qst[:, g, chunk, :], q_bank[g].rearrange("p (c s) -> p c s", c=CH), ACT.Copy,
                                       scale=SQ).then_inc(q_hi, 1)
                        act.wait_ge(k_done, i * (2 * G) + (n + 1))
                        act.activation(kst[:, g, chunk, :], k_bank[g].rearrange("p (c s) -> p c s", c=CH), ACT.Copy,
                                       scale=1.0 / WS).then_inc(k_hi, 1)
                    act.wait_ge(v_done, i * 2 + (u + 1))
                    for c in range(CH):
                        one = bass.ds(i * (2 * CH) + (CH * u + c), 1)
                        head = v_bank[u][:, D * c:D * c + D].rearrange("p (o h k) -> p o h k", o=1, k=DK0)
                        last = act.activation(vals[:, one, :, 0, 0:DK0], head, ACT.Copy, scale=1.0 / WS)
                    last.then_inc(v_hi, 1)

        @block.vector
        def _(dve):
            for i, value in enumerate((1.0, 0.0)):
                dve.memset(vals[:, :, :, i, DK0:DK0 + 1], value)
            with dve.Fori(0, NCH // 2) as i:
                for u in range(2):
                    chunk = bass.ds(i * (2 * CH) + CH * u, CH)
                    for g in range(G):
                        n = G * u + g
                        low = slice(64, 96)
                        dve.wait_ge(q_hi, i * (2 * G) + (n + 1))
                        dve.scalar_tensor_tensor(qst[low, g, chunk, :], q_bank[g][low].rearrange("p (c s) -> p c s", c=CH), SQ,
                                                 qst[low, g, chunk, :], ALU.mult, ALU.subtract).then_inc(q_lo, 1)
                        low = slice(32, 64)
                        dve.wait_ge(k_hi, i * (2 * G) + (n + 1))
                        dve.scalar_tensor_tensor(kst[low, g, chunk, :], k_bank[g][low].rearrange("p (c s) -> p c s", c=CH),
                                                 1.0 / WS, kst[low, g, chunk, :], ALU.mult, ALU.subtract).then_inc(k_lo, 1)
                    dve.wait_ge(v_hi, i * 2 + (u + 1))
                    for c in range(CH):
                        one = bass.ds(i * (2 * CH) + (CH * u + c), 1)
                        head = v_bank[u][:, D * c:D * c + D].rearrange("p (o h k) -> p o h k", o=1, k=DK0)
                        last = dve.scalar_tensor_tensor(vals[:, one, :, 1, 0:DK0], head, 1.0 / WS, vals[:, one, :, 0, 0:DK0],
                                                        ALU.mult, ALU.subtract)
                    last.then_inc(v_out, 1)


def attention0(nc, w, bank, qst, kst, vals):
    with Memory(nc, "attention0") as m:
        LAG = 3
        keys = m.sb("keys", [R0, 2, G, HG, C], FP16)
        queries = m.sb("queries", [R0, 2, G, S], FP16)
        values = m.sb("values", [C, 2, H, 2, DK0 + 1], FP16)
        summed = m.sb("summed", [S, H, DK0 + 1])
        negmax = m.sb("negmax", [S, G, HG], FP16)
        probs, probs_h, probs_l = m.sb("probs", [C, 2, HG, S]), m.sb("probs_h", [C, G, HG, S], FP16), m.sb("probs_l", [C, G, HG, S], FP16)
        recip = m.sb("recip", [S, H])
        heads_out = m.sb("heads_out", [S, H, DK0])
        turned_h, turned_l = m.sb("turned_h", [D, S], FP16), m.sb("turned_l", [D, S], FP16)
        new, bn, mv = m.sb("new", [S, 1, D]), m.sb("bn", [S, 6]), m.sb("mv", [S, 1, 2])
        (k_staged, q_staged, v_staged, scored, maxed, shifted, exped, p_split, mixed, inverted, normed, turned, ot_hi, ot_lo,
         projected, added, biased, totalled, bn_done, copied, aggregated, mv_copied, waited) = (
            m.sem(n) for n in ("k_staged", "q_staged", "v_staged", "scored", "maxed", "shifted", "exped", "p_split", "mixed",
                               "inverted", "normed", "turned", "ot_hi", "ot_lo", "projected", "added", "biased",
                               "totalled", "bn_done", "copied", "aggregated", "mv_copied", "waited"))
        block = m.block()
        score = [bank[u][:, 0:HG * C].rearrange("p (h c) -> p h c", c=C) for u in range(2)]
        score_t = [bank[2 + u][0:C, :].rearrange("p (h s) -> p h s", s=S) for u in range(2)]
        mix = [bank[4 + u][:, 0:H * 2 * (DK0 + 1)].rearrange("p (h i k) -> p h i k", i=2, k=DK0 + 1) for u in range(2)]
        out_t = bank[6][:, 0:S]
        out_p = bank[7][:, 0:D]

        def sequences(eng, body):
            body(0, 0)
            body(1, 1)
            with eng.Fori(0, (B - 4) // 2) as i:
                body(i * 2 + 2, 0)
                body(i * 2 + 3, 1)
            body(B - 2, 0)
            body(B - 1, 1)

        def within(b):
            return not isinstance(b, int) or b < B

        @block.gpsimd
        def _(pool):
            def probs_low(b, g):
                n = b * G + g
                pool.wait_ge(exped, n + 1)
                if late(n, G):
                    pool.wait_ge(mixed, n - (G - 1))
                pool.tensor_tensor(probs_l[:, g], probs[:, g % 2], probs_h[:, g], ALU.subtract).then_inc(p_split, 1)

            def add_bias(b):
                row = w.X[:, bass.ds(b, 1), :]
                pool.tensor_tensor(row, row, w.bias0[:].unsqueeze(1), ALU.add).then_inc(biased, 1)

            def body(b, u):
                for g in range(G):
                    probs_low(b, g)
                add_bias(b)

            sequences(pool, body)

        @block.tensor
        def _(pe):
            def scores(b, g, u):
                n = b * G + g
                if g == 0:
                    pe.wait_ge(k_staged, b + 1)
                    pe.wait_ge(q_staged, b + 1)
                if late(n, 2):
                    pe.wait_ge(maxed, n - 1)
                pe.matmul(score[g % 2], queries[:, u, g], keys[:, u, g], start=True, stop=True).then_inc(scored, 1)

            def scores_by_key(b, g, u):
                n = b * G + g
                pe.wait_ge(maxed, n + 1)
                if late(n, 2):
                    pe.wait_ge(exped, n - 1)
                for h in range(HG):
                    dst = score_t[g % 2][:, h, :]
                    pe.matmul(dst, keys[:, u, g, h], queries[:, u, g], start=True, stop=False)
                    last = pe.matmul(dst, negmax[:, g, h:h + 1].broadcast_to([S, C]), w.identh[:], start=False, stop=True)
                last.then_inc(shifted, 1)

            def mix_values(b, g, u):
                pe.wait_ge(p_split, b * G + (g + 1))
                if g == 0:
                    pe.wait_ge(v_staged, b + 1)
                    if late(b, 2):
                        pe.wait_ge(normed, b - 1)
                for h in range(HG):
                    v = HG * g + h
                    pe.matmul(mix[u][:, v], probs_h[:, g, h], values[:, u, v], start=True, stop=False)
                    last = pe.matmul(mix[u][:, v, 0], probs_l[:, g, h], values[:, u, v, 0], start=False, stop=True)
                last.then_inc(mixed, 1)

            def turn(b):
                pe.wait_ge(normed, b + 1)
                if late(b):
                    pe.wait_ge(ot_lo, b)
                pe.transpose(out_t, heads_out[:].rearrange("p h k -> p (h k)"), w.ident[:]).then_inc(turned, 1)

            def project(b):
                pe.wait_ge(ot_lo, b + 1)
                if late(b):
                    pe.wait_ge(added, b)
                for k, (x, wt) in enumerate(((turned_h, w.o0h), (turned_h, w.o0l), (turned_l, w.o0h))):
                    last = pe.matmul(out_p, x[:], wt[:, 0, :], start=k == 0, stop=k == 2)
                last.then_inc(projected, 1)

            def body(b, u):
                for g in range(G):
                    if g + 1 < G:
                        scores(b, g + 1, u)
                    elif within(b + 1):
                        scores(b + 1, 0, 1 - u)
                    scores_by_key(b, g, u)
                    if g >= LAG:
                        mix_values(b, g - LAG, u)
                    elif late(b):
                        mix_values(b - 1, G + g - LAG, 1 - u)
                    if g == 3 and late(b):
                        turn(b - 1)
                    if g == 0 and late(b, 2):
                        project(b - 2)

            scores(0, 0, 0)
            sequences(pe, body)
            for g in range(G - LAG, G):
                mix_values(B - 1, g, (B - 1) % 2)
            project(B - 2)
            turn(B - 1)
            project(B - 1)

        @block.scalar
        def _(act):
            def exp(b, g):
                n = b * G + g
                act.wait_ge(shifted, n + 1)
                if late(n, 2):
                    act.wait_ge(p_split, n - 1)
                if late(n, G):
                    act.wait_ge(mixed, n - (G - 1))
                act.activation(probs[:, g % 2], score_t[g % 2], ACT.Exp)
                act.activation(probs_h[:, g], score_t[g % 2], ACT.Exp).then_inc(exped, 1)

            def stage_values(b, u):
                if late(b, 2):
                    act.wait_ge(mixed, (b - 1) * G)
                act.activation(values[:, u].rearrange("p h i k -> p (h i k)"),
                               vals[:, bass.ds(b, 1)].rearrange("p o h i k -> p (o h i k)"), ACT.Copy).then_inc(v_staged, 1)

            def out_high(b):
                act.wait_ge(turned, b + 1)
                if late(b):
                    act.wait_ge(projected, b)
                act.activation(turned_h[:], out_t, ACT.Copy).then_inc(ot_hi, 1)

            def body(b, u):
                for g in range(G):
                    exp(b, g)
                    if g == 2 and within(b + 1):
                        stage_values(b + 1, 1 - u)
                    if g == 3 and late(b):
                        out_high(b - 1)

            stage_values(0, 0)
            sequences(act, body)
            out_high(B - 1)

        @block.vector
        def _(dve):
            def stage(b, u):
                one = bass.ds(b, 1)
                if late(b, 2):
                    dve.wait_ge(shifted, (b - 1) * G)
                dve.sem_inc(waited, 1)
                dve.tensor_copy(queries[:, u], qst[:, :, one, :].rearrange("p g o s -> p g (o s)")).then_inc(q_staged, 1)
                for h in range(HG):
                    last = dve.tensor_scalar(keys[:, u, :, h], kst[:, :, one, :].rearrange("p g o c -> p g (o c)"),
                                             w.head_rows[:, h:h + 1], None, ALU.mult)
                last.then_inc(k_staged, 1)

            def maximum(b, g):
                dve.wait_ge(scored, b * G + (g + 1))
                dve.tensor_reduce(negmax[:, g], score[g % 2], AX.X, ALU.max, negate=True).then_inc(maxed, 1)

            def normalise(b, u):
                dve.wait_ge(mixed, (b + 1) * G)
                dve.tensor_reduce(summed[:], mix[u].rearrange("p h i k -> p h k i"), AX.X, ALU.add).then_inc(totalled, 1)
                dve.wait_ge(totalled, b + 1)
                dve.reciprocal(recip[:], summed[:, :, DK0]).then_inc(inverted, 1)
                dve.wait_ge(inverted, b + 1)
                if late(b):
                    dve.wait_ge(turned, b)
                dve.tensor_tensor(heads_out[:], summed[:, :, 0:DK0], recip[:].unsqueeze(2).broadcast_to([S, H, DK0]),
                                  ALU.mult).then_inc(normed, 1)

            def out_low(b):
                dve.wait_ge(ot_hi, b + 1)
                dve.tensor_tensor(turned_l[:], out_t, turned_h[:], ALU.subtract).then_inc(ot_lo, 1)

            def residual(b):
                dve.wait_ge(projected, b + 1)
                dve.wait_ge(biased, b + 1)
                if late(b):
                    dve.wait_ge(bn_done, b)
                    dve.wait_ge(copied, b)
                dve.sem_inc(waited, 1)
                dve.scalar_tensor_tensor(new[:], out_p.unsqueeze(1), w.tg0[:], w.X[:, bass.ds(b, 1), :], ALU.mult, ALU.add).then_inc(added, 1)

            def statistics(b):
                dve.wait_ge(added, b + 1)
                if late(b):
                    dve.wait_ge(aggregated, b)
                dve.bn_stats(bn[:], new[:, 0]).then_inc(bn_done, 1)
                dve.tensor_copy(w.X[:, bass.ds(b, 1), :], new[:]).then_inc(copied, 1)

            def aggregate(b):
                dve.wait_ge(bn_done, b + 1)
                if late(b):
                    dve.wait_ge(mv_copied, b)
                dve.sem_inc(waited, 1)
                dve.bn_aggr(mv[:, 0], bn[:]).then_inc(aggregated, 1)

            def put_away(b):
                dve.wait_ge(aggregated, b + 1)
                dve.sem_inc(waited, 1)
                dve.tensor_copy(w.mv[:, bass.ds(b, 1), :], mv[:]).then_inc(mv_copied, 1)

            def body(b, u):
                for g in range(G):
                    if g + 1 < G:
                        maximum(b, g + 1)
                    elif within(b + 1):
                        maximum(b + 1, 0)
                    if g == 0 and late(b, 2):
                        out_low(b - 2)
                    if g == 0 and within(b + 1):
                        stage(b + 1, 1 - u)
                    if g == 1 and late(b, 2):
                        residual(b - 2)
                    if g == 2 and late(b, 2):
                        statistics(b - 2)
                    if g == 2 and late(b):
                        normalise(b - 1, 1 - u)
                    if g == 2 and late(b, 2):
                        aggregate(b - 2)
                    if g == 3 and late(b, 2):
                        put_away(b - 2)

            def finish(b):
                residual(b)
                statistics(b)
                aggregate(b)
                put_away(b)

            stage(0, 0)
            maximum(0, 0)
            sequences(dve, body)
            out_low(B - 2)
            finish(B - 2)
            normalise(B - 1, (B - 1) % 2)
            out_low(B - 1)
            finish(B - 1)


def feed_forward0(nc, w, bank):
    with Memory(nc, "feed_forward0") as m:
        normed, rounded = m.sb("normed", [S, 2, CH, D]), m.sb("rounded", [S, 2, CH, D])
        amax, scale, step_of = m.sb("amax", [S, 2, CH]), m.sb("scale", [S, 2, CH]), m.sb("step_of", [S, 2, CH])
        rows_h, rows_l = m.sb("rows_h", [D, 2, CH, S], FP16), m.sb("rows_l", [D, 2, CH, S], FP16)
        pre, tanh = m.sb("pre", [128, 2, N]), m.sb("tanh", [128, 2, N])
        silu = m.sb("silu", [128, 2, M0, N])
        biased = m.sb("biased", [S, 2, HID])
        ints = m.sb("ints", [128, 2, M0, S], FP16)
        amax2, step2, scale2, out_of = m.sb("amax2", [S, 1]), m.sb("step2", [S, 1]), m.sb("scale2", [S, 2]), m.sb("out_of", [S, CH])
        waited, pool_waited = m.sem("waited"), m.sem("pool_waited")
        t1, t2 = m.sb("t1", [S, B]), m.sb("t2", [S, B])
        (rsqrt_done, normed_in, scales, rounded_in, quant, turned, rows_hi, rows_lo, conved, activated, silued, returned,
         scale_in, biased_in, turned_back, ints_in, projected, added, chain, achain, out_scale_in) = (
            m.sem(n) for n in ("rsqrt_done", "normed_in", "scales", "rounded_in", "quant", "turned", "rows_hi", "rows_lo",
                               "conved", "activated", "silued", "returned", "scale_in", "biased_in",
                               "turned_back", "ints_in", "projected", "added", "chain", "achain", "out_scale_in"))
        block = m.block()
        rows_t = bank[0][:, :].rearrange("p (c s) -> p c s", s=S)
        conv = [bank[1 + u][:, :].rearrange("p (c s) -> p c s", s=S) for u in range(2)]
        by_row = [bank[3 + u][:, :].rearrange("p (m c) -> p m c", c=128) for u in range(2)]
        by_channel = [bank[5 + u][:, :].rearrange("p (m s) -> p m s", s=S) for u in range(2)]
        out_p = bank[7][:, 0:D]
        LOOP = (1, 5)

        def chunks(eng, body):
            body(0, 0)
            with eng.Fori(0, (LOOP[1] - LOOP[0]) // 2) as i:
                body(i * 2 + 1, 1)
                body(i * 2 + 2, 0)
            for k in range(LOOP[1], NCH):
                body(k, k % 2)

        def within(k, ahead):
            return not isinstance(k, int) or k + ahead < NCH

        def next_tile(k, u, c):
            return (within(k, 1), k + 1, 1 - u, c + 1) if c < CH - 1 else (within(k, 2), k + 2, u, 0)

        @block.gpsimd
        def _(pool):
            def quantise(k, u):
                pool.wait_ge(scales, k + 1)
                pool.sem_inc(pool_waited, 1)
                for c in range(CH):
                    last = pool.tensor_scalar(rounded[:, u, c], normed[:, u, c], scale[:, u, c:c + 1], ROUND, ALU.mult, ALU.add)
                last.then_inc(rounded_in, 1)
                pool.wait_ge(rounded_in, k + 1)
                if not isinstance(k, int) or k >= 2:
                    pool.wait_ge(turned, k - 1)
                pool.sem_inc(pool_waited, 1)
                for c in range(CH):
                    last = pool.tensor_scalar(normed[:, u, c], rounded[:, u, c], -ROUND, step_of[:, u, c:c + 1],
                                              ALU.add, ALU.mult)
                last.then_inc(quant, 1)

            quantise(0, 0)
            quantise(1, 1)
            quantise(2, 0)
            chunks(pool, lambda k, u: quantise(k + 3, 1 - u) if within(k, 3) else None)

        @block.tensor
        def _(pe):
            def turn(k, u):
                pe.wait_ge(quant, k + 1)
                if not isinstance(k, int) or k > 0:
                    pe.wait_ge(rows_lo, k)
                for c in range(CH):
                    last = pe.transpose(rows_t[:, c, :], normed[:, u, c], w.ident[:])
                last.then_inc(turned, 1)

            def convolve(k, u, t):
                n = k * M0 + t
                pe.wait_ge(rows_lo, k + 1)
                if not isinstance(k, int) or n >= 2:
                    pe.wait_ge(activated, n - 1)
                products = [(tap, wt, x) for tap in (1, 0, 2) for wt, x in ((w.taph, rows_h), (w.tapl, rows_h), (w.taph, rows_l))]
                for i, (tap, wt, x) in enumerate(products):
                    to = slice(max(0, 1 - tap), S - max(0, tap - 1))
                    of = slice(max(0, tap - 1), S - max(0, 1 - tap))
                    last = pe.matmul(conv[t % 2][:, :, to], wt[:, tap, t], x[:, u, :, of], start=i == 0, stop=i == len(products) - 1)
                last.then_inc(conved, 1)

            def to_rows(k, u, c):
                n = k * CH + c
                pe.wait_ge(silued, (k + 1) * M0)
                if not isinstance(k, int) or n >= 2:
                    pe.wait_ge(biased_in, n - 1)
                for t in range(M0):
                    last = pe.transpose(by_row[c % 2][:, t, :], silu[:, u, t, S * c:S * c + S], w.ident[:])
                last.then_inc(returned, 1)

            def to_channels(k, c):
                n = k * CH + c
                pe.wait_ge(biased_in, n + 1)
                if not isinstance(k, int) or n >= 2:
                    pe.wait_ge(ints_in, n - 1)
                for t in range(M0):
                    last = pe.transpose(by_channel[c % 2][:, t, :], biased[:, c % 2, 128 * t:128 * t + 128], w.ident[:])
                last.then_inc(turned_back, 1)

            def project(n, c):
                pe.wait_ge(ints_in, n + 1)
                if not isinstance(n, int) or n >= 1:
                    pe.wait_ge(added, n)
                for t in range(M0):
                    last = pe.matmul(out_p, ints[:, c % 2, t], w.w2t[:, t], start=t == 0, stop=t == M0 - 1)
                last.then_inc(projected, 1)

            def body(k, u):
                for c in range(CH):
                    more, *tile = next_tile(k, u, c)
                    if c < CH - 1:
                        to_rows(k, u, c + 1)
                    if more:
                        convolve(*tile)
                    if c == CH - 1 and within(k, 1):
                        to_rows(k + 1, 1 - u, 0)
                    to_channels(k, c)
                    if not (isinstance(k, int) and k == 0 and c == 0):
                        project(k * CH + (c - 1), (c + CH - 1) % CH)
                    if c == 1 and within(k, 2):
                        turn(k + 2, u)

            turn(0, 0)
            turn(1, 1)
            for t in range(M0):
                convolve(0, 0, t)
            convolve(1, 1, 0)
            to_rows(0, 0, 0)
            chunks(pe, body)
            project(B - 1, CH - 1)

        @block.scalar
        def _(act):
            def rows_high(k, u):
                act.wait_ge(turned, k + 1)
                if not isinstance(k, int) or k >= 2:
                    act.wait_ge(conved, (k - 1) * M0)
                act.activation(rows_h[:, u], rows_t, ACT.Copy).then_inc(rows_hi, 1)

            def activate(k, t):
                n = k * M0 + t
                act.wait_ge(conved, n + 1)
                if not isinstance(k, int) or n >= 2:
                    act.wait_ge(silued, n - 1)
                src = bank[1 + t % 2][:, :]
                act.activation(tanh[:, t % 2], src, ACT.Tanh, bias=w.conv_b_half[:, t:t + 1], scale=0.5 / WS)
                act.activation(pre[:, t % 2], src, ACT.Identity, bias=w.conv_b[:, t:t + 1], scale=1.0 / WS).then_inc(activated, 1)

            def quantise(k, c):
                n = k * CH + c
                act.wait_ge(returned, n + 1)
                act.wait_ge(scale_in, n + 1)
                if not isinstance(k, int) or n >= 2:
                    act.wait_ge(turned_back, n - 1)
                act.activation(biased[:, c % 2], bank[3 + c % 2][:, :], ACT.Copy, bias=ROUND,
                               scale=scale2[:, c % 2:c % 2 + 1]).then_inc(biased_in, 1)

            def body(k, u):
                for c in range(CH):
                    quantise(k, c)
                    more, chunk, _, t = next_tile(k, u, c)
                    if more:
                        activate(chunk, t)
                    if c == 1 and within(k, 2):
                        rows_high(k + 2, u)

            rows_high(0, 0)
            rows_high(1, 1)
            for t in range(M0):
                activate(0, t)
            activate(1, 0)
            chunks(act, body)

        @block.vector
        def _(dve):
            LINKS = 2
            OUT_LINKS = 2

            def normalise(k, u, half):
                if half == 0 and late(k, 2):
                    dve.wait_ge(turned, k - 1)
                for c in range(2 * half, 2 * half + 2):
                    one = bass.ds(k * CH + c, 1)
                    last = dve.tensor_scalar(normed[:, u, c:c + 1], w.X[:, one, :], w.mv[:, one, 0:1], w.rstd[:, one],
                                             ALU.subtract, ALU.mult)
                last.then_inc(normed_in, 1)

            def scales_of(k, u):
                dve.wait_ge(normed_in, 2 * k + 2)
                dve.tensor_reduce(amax[:, u], normed[:, u], AX.X, ALU.max, apply_absolute_value=True).then_inc(chain, 1)
                dve.wait_ge(chain, k * LINKS + 1)
                if late(k, 2):
                    dve.wait_ge(quant, k - 1)
                dve.tensor_scalar(step_of[:, u], amax[:, u], 1e-5, 1.0 / 127.0, ALU.max, ALU.mult).then_inc(chain, 1)
                dve.wait_ge(chain, k * LINKS + 2)
                dve.reciprocal(scale[:, u], step_of[:, u]).then_inc(scales, 1)

            def rows_low(k, u):
                dve.wait_ge(rows_hi, k + 1)
                dve.tensor_tensor(rows_l[:, u], rows_t, rows_h[:, u], ALU.subtract).then_inc(rows_lo, 1)

            def multiply(k, u, t):
                dve.wait_ge(activated, k * M0 + (t + 1))
                dve.scalar_tensor_tensor(silu[:, u, t], tanh[:, t % 2], 1.0, pre[:, t % 2], ALU.add, ALU.mult).then_inc(silued, 1)

            def scale_of(k, c):
                n = k * CH + c
                dve.wait_ge(returned, n + 1)
                if not isinstance(k, int) or n >= 2:
                    dve.wait_ge(biased_in, n - 1)
                dve.tensor_reduce(amax2[:], bank[3 + c % 2][:, :], AX.X, ALU.max, apply_absolute_value=True).then_inc(achain, 1)
                dve.wait_ge(achain, n * OUT_LINKS + 1)
                dve.tensor_scalar(step2[:], amax2[:], 2e-5, 1.0 / 127.0, ALU.max, ALU.mult).then_inc(achain, 1)
                dve.wait_ge(achain, n * OUT_LINKS + 2)
                dve.reciprocal(scale2[:, c % 2:c % 2 + 1], step2[:]).then_inc(scale_in, 1)
                dve.tensor_tensor(out_of[:, c:c + 1], step2[:], w.ffn_out[:], ALU.mult).then_inc(out_scale_in, 1)

            def integers(k, c):
                n = k * CH + c
                dve.wait_ge(turned_back, n + 1)
                if not isinstance(k, int) or n >= 2:
                    dve.wait_ge(projected, n - 1)
                dve.tensor_scalar(ints[:, c % 2], by_channel[c % 2], ROUND, None, ALU.subtract).then_inc(ints_in, 1)

            def residual(n, c):
                row = w.X[:, bass.ds(n, 1), :]
                dve.wait_ge(projected, n + 1)
                dve.wait_ge(out_scale_in, n + 1)
                dve.sem_inc(waited, 1)
                dve.scalar_tensor_tensor(row, out_p.unsqueeze(1), out_of[:, c:c + 1], row, ALU.mult, ALU.add).then_inc(added, 1)

            def body(k, u):
                for c in range(CH):
                    if c == 2 and within(k, 2):
                        rows_low(k + 2, u)
                    if c < CH - 1:
                        scale_of(k, c + 1)
                    if c == CH - 1 and within(k, 1):
                        scale_of(k + 1, 0)
                    more, *tile = next_tile(k, u, c)
                    if more:
                        multiply(*tile)
                    integers(k, c)
                    if not (isinstance(k, int) and k == 0 and c == 0):
                        residual(k * CH + (c - 1), (c + CH - 1) % CH)
                    if c < 2 and within(k, 3):
                        normalise(k + 3, 1 - u, c)
                    if c == 2 and within(k, 3):
                        scales_of(k + 3, 1 - u)

            rsqrt(dve, linker(dve, rsqrt_done), w.rstd[:], w.mv[:, :, 1], t1[:], t2[:])
            for k in range(3):
                if k == 2:
                    rows_low(0, 0)
                    rows_low(1, 1)
                for half in range(2):
                    normalise(k, k % 2, half)
                scales_of(k, k % 2)
            for t in range(M0):
                multiply(0, 0, t)
            multiply(1, 1, 0)
            scale_of(0, 0)
            chunks(dve, body)
            residual(B - 1, CH - 1)


def mask_keys(w, kv, jobs):
    def memory(m):
        diff = m.sb("diff", [D, 2, B // 2, C], FP16)
        steps = m.sem("steps")

        def work(dve, link):
            for job in jobs:
                dve.wait_ge(job.high, NCH + 2)
            halves = [slice(0, B // 2), slice(B // 2, B)]
            latent0 = [kv[:, x, 0, 0:1].broadcast_to([D, B // 2, C]) for x in halves]
            for i, x in enumerate(halves):
                dve.tensor_tensor(diff[:, i], kv[:, x, 0, S:KV], latent0[i], ALU.subtract).then_inc(steps, 1)
            dve.tensor_copy(kv[:, halves[0], 2, 0:S], kv[:, halves[0], 0, 0:S])
            for i, x in enumerate(halves):
                dve.wait_ge(steps, i + 1)
                dve.tensor_tensor(diff[:, i], diff[:, i], w.mask01[:, x, :], ALU.mult).then_inc(steps, 1)
            dve.tensor_copy(kv[:, halves[1], 2, 0:S], kv[:, halves[1], 0, 0:S])
            for i, x in enumerate(halves):
                dve.wait_ge(steps, i + 3)
                dve.tensor_tensor(kv[:, x, 2, S:KV], diff[:, i], latent0[i], ALU.add)
        return work
    return memory


def latent_scale(w):
    def memory(m):
        t1, t2, r, v = (m.sb(n, [S, B]) for n in ("t1", "t2", "r", "v"))
        bn = m.sb("bn", [S, B, 6])

        def work(dve, link):
            row_statistics(dve, link, w, bn)
            rsqrt(dve, link, r[:], w.mv[:, :, 1], t1[:], t2[:])
            link(dve.tensor_tensor(v[:], r[:], r[:], ALU.mult))
            link(dve.tensor_tensor(v[:], v[:], w.mv[:, :, 1], ALU.mult))
            rsqrt(dve, link, w.rstd[:], v[:], t1[:], t2[:])
            link(dve.tensor_tensor(w.rstd[:], w.rstd[:], r[:], ALU.mult))
        return work
    return memory


def context_scale(w):
    def memory(m):
        t1, t2, bn, mv = m.sb("t1", [C, B]), m.sb("t2", [C, B]), m.sb("bn", [C, B, 6]), m.sb("mv", [C, B, 2])

        def work(dve, link):
            for b in range(B):
                last = dve.bn_stats(bn[:, b], w.ctx[:, b])
            link(last)
            for b in range(B):
                last = dve.bn_aggr(mv[:, b], bn[:, b])
            link(last)
            rsqrt(dve, link, w.rstd_c[:], mv[:, :, 1], t1[:], t2[:])
            dve.scalar_tensor_tensor(w.shift_c[:], mv[:, :, 0], -1.0, w.rstd_c[:], ALU.mult, ALU.mult)
        return work
    return memory


def row_scale(w):
    def memory(m):
        t1, t2 = m.sb("t1", [S, B]), m.sb("t2", [S, B])
        return lambda dve, link: rsqrt(dve, link, w.rstd[:], w.mv[:, :, 1], t1[:], t2[:])
    return memory


def attention1(nc, w, bank, kv):
    with Memory(nc, "attention1") as m:
        HI, LO, MAX = 0, 1, 2
        keys = m.sb("keys", [D, 2, 3, KV], FP16)
        th, tl = m.sb("th", [D, G, HG, S], FP16), m.sb("tl", [D, G, HG, S], FP16)
        negmax = m.sb("negmax", [S, G, HG], FP16)
        probs_l, probs_c = m.sb("probs_l", [S, 2, HG, S]), m.sb("probs_c", [C, 2, HG, S])
        ph_l, ph_c = m.sb("ph_l", [S, 2, HG, S], FP16), m.sb("ph_c", [C, 2, HG, S], FP16)
        pl_l, pl_c = m.sb("pl_l", [S, 2, HG, S], FP16), m.sb("pl_c", [C, 2, HG, S], FP16)
        vh_l, vh_c = m.sb("vh_l", [S, 2, H, DK1 + 1], FP16), m.sb("vh_c", [C, 2, H, DK1 + 1], FP16)
        vl_l, vl_c = m.sb("vl_l", [S, 2, H, DK1 + 1], FP16), m.sb("vl_c", [C, 2, H, DK1 + 1], FP16)
        recip = m.sb("recip", [S, HG])
        heads_out = m.sb("heads_out", [S, 2, H, DK1])
        turned_h, turned_l = m.sb("turned_h", [D, H // 2, S], FP16), m.sb("turned_l", [D, H // 2, S], FP16)
        out, zn, bn, mv, rstd = m.sb("out", [S, D]), m.sb("zn", [S, D]), m.sb("bn", [S, 6]), m.sb("mv", [S, 1, 2]), m.sb("rstd", [S, 1])
        t1, t2 = m.sb("t1", [S, 1]), m.sb("t2", [S, 1])
        new, bn_x, mv_x = m.sb("new", [S, 1, D]), m.sb("bn_x", [S, 6]), m.sb("mv_x", [S, 1, 2])
        (ones_in, staged, t_done, t_hi, t_lo, scored, maxed, shifted, exped_l, exped_c, p_split, v_done, v_hi, v_out, mixed, normed, turned, ot_hi,
         ot_lo, projected, out_copied, out_normed, scaled, summed, copied, new_read, aggregated, mv_copied, biased, nchain, chain, waited, pool_waited, act_waited) = (
            m.sem(n) for n in ("ones_in", "staged", "t_done", "t_hi", "t_lo", "scored", "maxed", "shifted", "exped_l", "exped_c",
                               "p_split", "v_done", "v_hi", "v_out", "mixed", "normed", "turned", "ot_hi", "ot_lo", "projected",
                               "out_copied", "out_normed", "scaled", "summed", "copied",
                               "new_read", "aggregated", "mv_copied", "biased", "nchain", "chain", "waited", "pool_waited", "act_waited"))
        block = m.block()
        t_bank = bank[0][:, :].rearrange("p (h s) -> p h s", s=S)
        score = [bank[1 + i][:, 0:2 * KV].rearrange("p (h k) -> p h k", k=KV) for i in range(2)]
        by_key_l = bank[3][:, :].rearrange("p (h s) -> p h s", s=S)
        by_key_c = bank[4][0:C, :].rearrange("p (h s) -> p h s", s=S)
        mix = bank[5][:, 0:HG * (DK1 + 1)].rearrange("p (h k) -> p h k", k=DK1 + 1)
        VW = HG * DK1
        v_l, v_c = bank[6][:, 0:VW], bank[6][0:C, VW:2 * VW]
        out_t = bank[7][:, :].rearrange("p (t s) -> p t s", s=S)
        out_p = bank[7][:, 0:D]
        LAT, CTX = slice(0, S), slice(S, KV)
        VALUES_AHEAD = 3

        def after(b, g, u, n):
            return (b, g + n, u) if g + n < G else (b + 1, g + n - G, 1 - u)

        def before(b, g, u):
            return (b, g - 1, u) if g > 0 else (b - 1, G - 1, 1 - u)

        def sequences(eng, body):
            body(0, 0, True, False)
            with eng.Fori(0, (B - 2) // 2) as i:
                body(i * 2 + 1, 1, False, False)
                body(i * 2 + 2, 0, False, False)
            body(B - 1, (B - 1) % 2, False, True)

        @block.gpsimd
        def _(pool):
            def probs_low(b, g):
                if late(b * G + g, 2):
                    pool.wait_ge(mixed, b * G + (g - 1))
                for exped, low, whole, high in ((exped_l, pl_l, probs_l, ph_l), (exped_c, pl_c, probs_c, ph_c)):
                    pool.wait_ge(exped, b * G + (g + 1))
                    last = pool.tensor_tensor(low[:, g % 2], whole[:, g % 2], high[:, g % 2], ALU.subtract)
                last.then_inc(p_split, 1)

            def add_bias(b):
                row = w.X[:, bass.ds(b, 1), :]
                pool.tensor_tensor(row, row, w.bias1[:].unsqueeze(1), ALU.add).then_inc(biased, 1)

            def residual(t):
                pool.wait_ge(out_normed, t + 1)
                pool.tensor_tensor(zn[:], zn[:], w.gain1[:], ALU.mult).then_inc(scaled, 1)
                pool.wait_ge(scaled, t + 1)
                pool.wait_ge(biased, t + 1)
                if late(t):
                    pool.wait_ge(copied, t)
                    pool.wait_ge(new_read, t)
                pool.sem_inc(pool_waited, 1)
                pool.tensor_tensor(new[:], zn[:].unsqueeze(1), w.X[:, bass.ds(t, 1), :], ALU.add).then_inc(summed, 1)

            def body(b, u, first, last):
                for g in range(G):
                    if g == 3 and not first:
                        residual(b - 1)
                    probs_low(b, g)
                    if g == 0:
                        add_bias(b)

            sequences(pool, body)
            residual(B - 1)

        @block.tensor
        def _(pe):
            def three(dst, pairs):
                for i, (x, y) in enumerate(pairs):
                    last = pe.matmul(dst, x, y, start=i == 0, stop=i == 2)
                return last

            def make_t(b, g, u):
                pe.wait_ge(staged, b + 1)
                if late(b * G + g):
                    pe.wait_ge(t_lo, b * G + g)
                for h in range(HG):
                    ah, al = w.ah[:, HG * g + h], w.al[:, HG * g + h]
                    last = three(t_bank[:, h], ((ah, keys[:, u, HI, LAT]), (al, keys[:, u, HI, LAT]), (ah, keys[:, u, LO, LAT])))
                last.then_inc(t_done, 1)

            def scores(b, g, u):
                pe.wait_ge(t_hi, b * G + (g + 1))
                if late(b * G + g):
                    pe.wait_ge(maxed, b * G + g)
                for h in range(HG):
                    last = pe.matmul(score[h // 2][:, h % 2], th[:, g, h], keys[:, u, MAX], start=True, stop=True)
                last.then_inc(scored, 1)

            def scores_by_key(b, g, u, turns):
                pe.wait_ge(t_lo, b * G + (g + 1))
                pe.wait_ge(maxed, b * G + (g + 1))
                for dst, part, width, exped in ((by_key_l, LAT, S, exped_l), (by_key_c, CTX, C, exped_c)):
                    if late(b * G + g):
                        pe.wait_ge(exped, b * G + g)
                    kh, kl = keys[:, u, HI, part], keys[:, u, LO, part]
                    pe.matmul(dst, kh, th[:, g], start=True, stop=False)
                    pe.matmul(dst, kl, th[:, g], start=False, stop=False)
                    pe.matmul(dst, kh, tl[:, g], start=False, stop=False)
                    for h in range(HG):
                        last = pe.matmul(dst[:, h], negmax[:, g, h:h + 1].broadcast_to([S, width]), w.identh[:],
                                         start=False, stop=h == HG - 1)
                    last.then_inc(shifted, 1)
                    if part is LAT and turns:
                        turn(b - 1, g, 1 - u)

            def mix_values(b, g, u):
                pe.wait_ge(p_split, b * G + (g + 1))
                pe.wait_ge(v_out, b * G + (g + 1))
                if late(b * G + g):
                    pe.wait_ge(normed, b * G + g)
                for h in range(HG):
                    v = HG * g + h
                    products = [(ph_l[:, g % 2, h], vh_l[:, u, v]), (ph_l[:, g % 2, h], vl_l[:, u, v]), (pl_l[:, g % 2, h], vh_l[:, u, v]),
                                (ph_c[:, g % 2, h], vh_c[:, u, v]), (ph_c[:, g % 2, h], vl_c[:, u, v]), (pl_c[:, g % 2, h], vh_c[:, u, v])]
                    for i, (x, y) in enumerate(products):
                        last = pe.matmul(mix[:, h], x, y, start=i == 0, stop=i == len(products) - 1)
                last.then_inc(mixed, 1)

            def values(b, g, u):
                pe.wait_ge(staged, b + 1)
                if late(b * G + g):
                    pe.wait_ge(v_out, b * G + g)
                cols = slice(VW * g, VW * g + VW)
                for dst, part in ((v_l, LAT), (v_c, CTX)):
                    kh, kl = keys[:, u, HI, part], keys[:, u, LO, part]
                    last = three(dst, ((kh, w.v1h[:, cols]), (kh, w.v1l[:, cols]), (kl, w.v1h[:, cols])))
                last.then_inc(v_done, 1)

            def turn(t, half, u):
                pe.wait_ge(normed, t * G + (2 + 2 * half))
                if half == 1:
                    pe.wait_ge(ot_lo, t * 2 + 1)
                elif late(t):
                    pe.wait_ge(out_copied, t)
                for i in range(4):
                    h = 2 * (4 * half + i)
                    last = pe.transpose(out_t[:, i], heads_out[:, u, h:h + 2].rearrange("p h k -> p (h k)"), w.ident[:])
                last.then_inc(turned, 1)

            def project(t):
                pe.wait_ge(ot_lo, t * 2 + 2)
                for i in range(H // 2):
                    for j, (x, wt) in enumerate(((turned_h, w.o1h), (turned_h, w.o1l), (turned_l, w.o1h))):
                        last = pe.matmul(out_p, x[:, i], wt[:, i], start=i == 0 and j == 0, stop=i == H // 2 - 1 and j == 2)
                last.then_inc(projected, 1)

            def body(b, u, first, last):
                for g in range(G):
                    scores_by_key(b, g, u, turns=g < 2 and not first)
                    if not (last and g + 2 >= G):
                        make_t(*after(b, g, u, 2))
                    if not (last and g + 1 >= G):
                        scores(*after(b, g, u, 1))
                    if not (first and g == 0):
                        mix_values(*before(b, g, u))
                    if not (last and g > 0):
                        values(*after(b, g, u, VALUES_AHEAD))
                    if not first and g == 1:
                        project(b - 1)


            for g in range(2):
                make_t(0, g, 0)
                values(0, g, 0)
            scores(0, 0, 0)
            pe.wait_ge(ones_in, 4)
            for g in range(2, VALUES_AHEAD):
                values(0, g, 0)
            sequences(pe, body)
            end = (B - 1) % 2
            mix_values(B - 1, G - 1, end)
            turn(B - 1, 0, end)
            turn(B - 1, 1, end)
            project(B - 1)

        @block.scalar
        def _(act):
            def t_high(b, g, u):
                act.wait_ge(t_done, b * G + (g + 1))
                act.activation(th[:, g], t_bank, ACT.Copy, scale=1.0 / AS).then_inc(t_hi, 1)

            def exp(b, g, u, outs):
                act.wait_ge(shifted, 2 * (b * G) + (2 * g + 1))
                if late(b * G + g, 2):
                    act.wait_ge(mixed, b * G + (g - 1))
                if late(b * G + g, 2):
                    act.wait_ge(p_split, b * G + (g - 1))
                for dst in (probs_l, ph_l):
                    last = act.activation(dst[:, g % 2], by_key_l, ACT.Exp)
                last.then_inc(exped_l, 1)
                if outs:
                    out_high(b - 1, g)
                act.wait_ge(shifted, 2 * (b * G) + (2 * g + 2))
                act.sem_inc(act_waited, 1)
                for dst in (probs_c, ph_c):
                    last = act.activation(dst[:, g % 2], by_key_c, ACT.Exp, bias=w.mask_bias[:, 0, bass.ds(b, 1)])
                last.then_inc(exped_c, 1)

            def values_out(b, g, u):
                act.wait_ge(v_done, b * G + (g + 1))
                if late(b, 2) and g == 0:
                    act.wait_ge(mixed, (b - 1) * G)
                for dst, src in ((vh_l, v_l), (vh_c, v_c)):
                    last = act.activation(dst[:, u, HG * g:HG * g + HG, 0:DK1], src.rearrange("p (h k) -> p h k", k=DK1),
                                          ACT.Copy, scale=1.0 / WS)
                last.then_inc(v_hi, 1)

            def out_high(t, half):
                act.wait_ge(turned, t * 2 + (half + 1))
                if late(t) and half == 0:
                    act.wait_ge(projected, t)
                act.activation(turned_h[:, 4 * half:4 * half + 4], out_t, ACT.Copy).then_inc(ot_hi, 1)

            def copy_out(t):
                act.wait_ge(projected, t + 1)
                if late(t):
                    act.wait_ge(out_normed, t)
                act.activation(out[:], out_p, ACT.Copy).then_inc(out_copied, 1)

            def body(b, u, first, last):
                for g in range(G):
                    if g == 2 and not first:
                        copy_out(b - 1)
                    exp(b, g, u, outs=g < 2 and not first)
                    if not (last and g + 2 >= G):
                        t_high(*after(b, g, u, 2))
                    if not (last and g > 0):
                        values_out(*after(b, g, u, VALUES_AHEAD))


            for g in range(2):
                t_high(0, g, 0)
                values_out(0, g, 0)
            for g in range(2, VALUES_AHEAD):
                values_out(0, g, 0)
            sequences(act, body)
            out_high(B - 1, 0)
            out_high(B - 1, 1)
            copy_out(B - 1)

        @block.vector
        def _(dve):
            def t_low(b, g, u):
                dve.wait_ge(t_hi, b * G + (g + 1))
                dve.scalar_tensor_tensor(tl[:, g].rearrange("p h s -> p (h s)"), bank[0][:, :], 1.0 / AS,
                                         th[:, g].rearrange("p h s -> p (h s)"), ALU.mult, ALU.subtract).then_inc(t_lo, 1)

            def maximum(b, g, u):
                dve.wait_ge(scored, b * G + (g + 1))
                for i in range(2):
                    last = dve.tensor_reduce(negmax[:, g, 2 * i:2 * i + 2], score[i], AX.X, ALU.max, negate=True)
                last.then_inc(maxed, 1)

            def values_low(b, g, u):
                dve.wait_ge(v_hi, b * G + (g + 1))
                for dst, high, src in ((vl_l, vh_l, v_l), (vl_c, vh_c, v_c)):
                    cols = slice(HG * g, HG * g + HG)
                    last = dve.scalar_tensor_tensor(dst[:, u, cols, 0:DK1], src.rearrange("p (h k) -> p h k", k=DK1), 1.0 / WS,
                                                    high[:, u, cols, 0:DK1], ALU.mult, ALU.subtract)
                last.then_inc(v_out, 1)

            def normalise(b, g, u):
                dve.wait_ge(mixed, b * G + (g + 1))
                dve.reciprocal(recip[:], mix[:, :, DK1]).then_inc(nchain, 1)
                dve.wait_ge(nchain, b * G + (g + 1))
                if late(b, 2) and g == 0:
                    dve.wait_ge(turned, (b - 1) * 2)
                dve.tensor_tensor(heads_out[:, u, HG * g:HG * g + HG], mix[:, :, 0:DK1],
                                  recip[:].unsqueeze(2).broadcast_to([S, HG, DK1]), ALU.mult).then_inc(normed, 1)

            def out_low(t, half):
                dve.wait_ge(ot_hi, t * 2 + (half + 1))
                dve.tensor_tensor(turned_l[:, 4 * half:4 * half + 4], out_t, turned_h[:, 4 * half:4 * half + 4],
                                  ALU.subtract).then_inc(ot_lo, 1)

            def stage(b, u):
                if late(b, 2):
                    dve.wait_ge(shifted, 2 * G * (b - 1))
                dve.sem_inc(waited, 1)
                dve.tensor_copy(keys[:, u].rearrange("p v k -> p (v k)"),
                                kv[:, bass.ds(b, 1), :, :].rearrange("p o v k -> p (o v k)")).then_inc(staged, 1)

            LINKS = 11

            def statistics(t):
                link = linker(dve, chain, t * LINKS)
                dve.wait_ge(out_copied, t + 1)
                link(dve.bn_stats(bn[:], out[:]))
                dve.sem_inc(waited, 1)
                link(dve.bn_aggr(mv[:, 0], bn[:]))
                link(dve.tensor_scalar(t1[:], mv[:, 0, 1:2], 0.5 / (WS * WS), 0.5 * EPS, ALU.mult, ALU.add))
                link(dve.tensor_single_scalar(t2[:].bitcast(INT32), t1[:].bitcast(INT32), 1, ALU.arith_shift_right))
                link(dve.tensor_scalar(rstd[:].bitcast(INT32), t2[:].bitcast(INT32), -1.0,
                                       float(0x5F3759DF - 0x400000 - 0x80000000), ALU.mult, ALU.add))

            def newton(t, i):
                link = linker(dve, chain, t * LINKS + 5 + 2 * i)
                link(dve.scalar_tensor_tensor(t2[:], rstd[:], t1[:], rstd[:], ALU.mult, ALU.mult))
                link(dve.scalar_tensor_tensor(rstd[:], t2[:], 1.5, rstd[:], ALU.subtract, ALU.mult))

            def out_norm(t):
                if late(t):
                    dve.wait_ge(summed, t)
                dve.tensor_scalar(zn[:], out[:], mv[:, 0, 0:1], rstd[:], ALU.subtract, ALU.mult).then_inc(out_normed, 1)

            def statistics_x(t):
                dve.wait_ge(summed, t + 1)
                if late(t):
                    dve.wait_ge(aggregated, t)
                dve.bn_stats(bn_x[:], new[:, 0]).then_inc(new_read, 1)
                dve.tensor_copy(w.X[:, bass.ds(t, 1), :], new[:]).then_inc(copied, 1)

            def aggregate_x(t):
                dve.wait_ge(new_read, t + 1)
                dve.sem_inc(waited, 1)
                dve.bn_aggr(mv_x[:, 0], bn_x[:]).then_inc(aggregated, 1)

            def put_away_x(t):
                dve.wait_ge(aggregated, t + 1)
                dve.sem_inc(waited, 1)
                dve.tensor_copy(w.mv[:, bass.ds(t, 1), :], mv_x[:]).then_inc(mv_copied, 1)
                dve.wait_ge(mv_copied, t + 1)

            def body(b, u, first, last):
                for g in range(G):
                    if g < 2 and not first:
                        out_low(b - 1, g)
                    if not (last and g + 1 >= G):
                        maximum(*after(b, g, u, 1))
                    if g == 0 and not first:
                        normalise(b - 1, G - 1, 1 - u)
                    if g == 0 and not last:
                        stage(b + 1, 1 - u)
                    if not (last and g + 2 >= G):
                        t_low(*after(b, g, u, 2))
                    if g == 3 and not first:
                        statistics_x(b - 1)
                    if g > 0:
                        normalise(b, g - 1, u)
                    if g == 3 and not first:
                        aggregate_x(b - 1)
                    if not (last and g > 0):
                        values_low(*after(b, g, u, VALUES_AHEAD))
                    if g == 1 and not first:
                        statistics(b - 1)
                        newton(b - 1, 0)
                        newton(b - 1, 1)
                    if g == 2 and not first:
                        newton(b - 1, 2)
                        out_norm(b - 1)
                    if g == 3 and not first:
                        put_away_x(b - 1)

            for x, value in ((vh_l, 1.0), (vh_c, 1.0), (vl_l, 0.0), (vl_c, 0.0)):
                dve.memset(x[:, :, :, DK1:DK1 + 1], value).then_inc(ones_in, 1)
            stage(0, 0)
            for g in range(2):
                t_low(0, g, 0)
                values_low(0, g, 0)
            maximum(0, 0, 0)
            for g in range(2, VALUES_AHEAD):
                values_low(0, g, 0)
            sequences(dve, body)
            end = (B - 1) % 2
            normalise(B - 1, G - 1, end)
            out_low(B - 1, 0)
            out_low(B - 1, 1)
            statistics(B - 1)
            for i in range(3):
                newton(B - 1, i)
            out_norm(B - 1)
            statistics_x(B - 1)
            aggregate_x(B - 1)
            put_away_x(B - 1)


def mixture(nc, a, w, bank, xh, xl):
    with Memory(nc, "mixture") as m:
        xs = m.sb("xs", [D, 2, 2, N], FP16)
        tanh, half = m.sb("tanh", [128, MH, N]), m.sb("half", [128, MH, N])
        LAG = 2
        hidden = m.sb("hidden", [128, 2, MH, N])
        hidden_h, hidden_l = m.sb("hidden_h", [128, 4, MH, N], FP16), m.sb("hidden_l", [128, 4, MH, N], FP16)
        part = m.sb("part", [S, 2, CH, D])
        gate2, gate = m.sb("gate2", [S, CH, 2, E]), m.sb("gate", [S, CH, E])
        top, index = m.sb("top", [S, CH, 8]), m.sb("index", [S, CH, 8], UINT32)
        chosen = m.sb("chosen", [S, CH, 2])
        diff, expd, p1, p2 = (m.sb(n, [S, CH]) for n in ("diff", "expd", "p1", "p2"))
        is1, is2 = m.sb("is1", [S, CH, E]), m.sb("is2", [S, CH, E])
        weight = m.sb("weight", [S, 2, CH, E])
        staged, gated, diffed, gexped, weighed, h_done, tanhed, halved, hid_in, hid_hi, hid_lo, y_done, combined, added, chain, stored, waited, pool_waited = (
            m.sem(n) for n in ("staged", "gated", "diffed", "gexped", "weighed", "h_done", "tanhed", "halved", "hid_in", "hid_hi", "hid_lo",
                               "y_done", "combined", "added", "chain", "stored", "waited", "pool_waited"))
        block = m.block()
        h1, h2 = [bank[i][:, :] for i in (0, 1)], [bank[i][:, :] for i in (2, 3)]
        y = [bank[4 + i][:, :].rearrange("p (c d) -> p c d", d=D) for i in range(2)]
        gates = bank[6][:, 0:CH * 2 * E]

        def chunks(eng, body):
            body(0, 0)
            with eng.Fori(0, (NCH - 2) // 2) as i:
                body(i * 2 + 1, 1)
                body(i * 2 + 2, 0)
            body(NCH - 1, (NCH - 1) % 2)

        def within(k):
            return not isinstance(k, int) or k + 1 < NCH

        def lagged(k, u, e, lag):
            return (True, k, u, e - lag) if e >= lag else (late(k), k - 1, 1 - u, E + e - lag)

        @block.gpsimd
        def _(pool):
            def add(k, e):
                n = k * E + e
                rows = w.X[:, bass.ds(k * CH, CH), :]
                pool.wait_ge(combined, n + 1)
                if late(n):
                    pool.wait_ge(added, n)
                pool.sem_inc(pool_waited, 1)
                pool.tensor_tensor(rows, rows, part[:, e % 2], ALU.add).then_inc(added, 1)

            def hidden_low(k, e, j):
                n = k * (E * MH) + (MH * e + j)
                pool.wait_ge(hid_hi, n + 1)
                pool.tensor_tensor(hidden_l[:, e % 4, j], hidden[:, e % 2, j], hidden_h[:, e % 4, j], ALU.subtract).then_inc(hid_lo, 1)

            def body(k, u):
                for e in range(E):
                    there, before, _, expert = lagged(k, u, e, 1)
                    if there:
                        hidden_low(before, expert, 1)
                    there, before, _, expert = lagged(k, u, e, LAG + 2)
                    if there:
                        add(before, expert)
                    hidden_low(k, e, 0)

            chunks(pool, body)
            hidden_low(NCH - 1, E - 1, 1)
            for e in range(E - LAG - 2, E):
                add(NCH - 1, e)

        @block.sync
        def _(sp):
            with sp.Fori(0, NCH) as i:
                chunk = bass.ds(i * CH, CH)
                sp.wait_ge(added, i * E + E)
                sp.dma_start(a["out"].rearrange("b s d -> s b d")[:, chunk, :], w.X[:, chunk, :]).then_inc(stored, 16)
            sp.wait_ge(stored, 16 * NCH)

        @block.tensor
        def _(pe):
            def choose(k, u):
                pe.wait_ge(staged, k + 1)
                for c in range(CH):
                    dst = gates[:, 2 * E * c:2 * E * c + 2 * E]
                    for i in range(2):
                        last = pe.matmul(dst, xs[:, u, i, S * c:S * c + S], w.wgt[:].rearrange("p i e -> p (i e)"),
                                         start=i == 0, stop=i == 1)
                last.then_inc(gated, 1)

            def rise(k, u, e, j):
                n = k * (E * MH) + (MH * e + j)
                if e == 0 and j == 0:
                    pe.wait_ge(staged, k + 1)
                if late(n, 2):
                    pe.wait_ge(hid_in, n - 1)
                for dst, i in ((h1[j], 0), (h2[j], 1)):
                    wh, wl = w.moeh[:, i, MH * e + j], w.moel[:, i, MH * e + j]
                    pe.matmul(dst, wh, xs[:, u, 0], start=True, stop=False)
                    pe.matmul(dst, wl, xs[:, u, 0], start=False, stop=False)
                    last = pe.matmul(dst, wh, xs[:, u, 1], start=False, stop=True)
                last.then_inc(h_done, 1)

            def fall(k, e):
                n = k * E + e
                pe.wait_ge(hid_lo, n * MH + MH)
                if late(n, 2):
                    pe.wait_ge(combined, n - 1)
                for c in range(CH):
                    products = [(x[:, e % 4, j, S * c:S * c + S], wt[:, MH * e + j]) for j in range(MH)
                                for x, wt in ((hidden_h, w.w3h), (hidden_h, w.w3l), (hidden_l, w.w3h))]
                    for i, (x, wt) in enumerate(products):
                        last = pe.matmul(y[e % 2][:, c], x, wt, start=i == 0, stop=i == len(products) - 1)
                last.then_inc(y_done, 1)

            def body(k, u):
                for e in range(E):
                    for j in range(MH):
                        rise(k, u, e, j)
                    there, before, _, expert = lagged(k, u, e, LAG)
                    if there:
                        fall(before, expert)
                    if e == 2 and within(k):
                        choose(k + 1, 1 - u)

            choose(0, 0)
            chunks(pe, body)
            for e in range(E - LAG, E):
                fall(NCH - 1, e)

        @block.scalar
        def _(act):
            def gate_exp(k):
                act.wait_ge(diffed, k + 1)
                act.activation(expd[:], diff[:], ACT.Exp).then_inc(gexped, 1)

            def hidden_high(k, e, j):
                act.wait_ge(hid_in, k * (E * MH) + (MH * e + j + 1))
                if j == 0 and late(k * E + e, 4):
                    act.wait_ge(y_done, k * E + (e - 3))
                act.activation(hidden_h[:, e % 4, j], hidden[:, e % 2, j], ACT.Copy).then_inc(hid_hi, 1)

            def body(k, u):
                for e in range(E):
                    for j in range(MH):
                        n = k * (E * MH) + (MH * e + j)
                        act.wait_ge(h_done, n + 1)
                        if late(n, 2):
                            act.wait_ge(halved, n - 1)
                        act.activation(tanh[:, j], h1[j], ACT.Tanh, scale=0.5 / WS).then_inc(tanhed, 1)
                        there, before, _, expert = lagged(k, u, e, 1) if j == 0 else (True, k, u, e)
                        if there:
                            hidden_high(before, expert, 1 - j)
                    if e == 5 and within(k):
                        gate_exp(k + 1)

            gate_exp(0)
            chunks(act, body)
            hidden_high(NCH - 1, E - 1, 1)

        @block.vector
        def _(dve):
            GATE_LINKS = 13

            def stage(k, u):
                chunk = bass.ds(k * CH, CH)
                if late(k, 2):
                    dve.wait_ge(h_done, (k - 1) * (E * MH))
                dve.sem_inc(waited, 1)
                for i, x in enumerate((xh, xl)):
                    last = dve.tensor_copy(xs[:, u, i].rearrange("p (c s) -> p c s", s=S), x[:, chunk, :])
                last.then_inc(staged, 1)

            def sum_gates(k):
                link = linker(dve, chain, k * GATE_LINKS)
                dve.wait_ge(gated, k + 1)
                link(dve.tensor_scalar(gate2[:].rearrange("p c i e -> p (c i e)"), gates, 1.0 / WS, None, ALU.mult))
                link(dve.tensor_tensor(gate[:], gate2[:, :, 0], gate2[:, :, 1], ALU.add))

            def largest(k):
                link = linker(dve, chain, k * GATE_LINKS + 2)
                dve.sem_inc(waited, 1)
                for c in range(CH):
                    last = dve.max(top[:, c], gate[:, c])
                link(last)

            def which(k):
                link = linker(dve, chain, k * GATE_LINKS + 3)
                dve.sem_inc(waited, 1)
                for c in range(CH):
                    last = dve.max_index(index[:, c], top[:, c], gate[:, c])
                link(last)
                link(dve.tensor_copy(chosen[:], index[:, :, 0:2]))
                dve.tensor_tensor(diff[:], top[:, :, 1], top[:, :, 0], ALU.subtract).then_inc(diffed, 1)

            def factors(k):
                link = linker(dve, chain, k * GATE_LINKS + 5)
                dve.wait_ge(gexped, k + 1)
                link(dve.tensor_scalar(p1[:], expd[:], 1.0, None, ALU.add))
                link(dve.reciprocal(p1[:], p1[:]))
                link(dve.tensor_scalar(p1[:], p1[:], w.moe_out[:], None, ALU.mult))
                link(dve.tensor_scalar(p2[:], p1[:], -1.0, w.moe_out[:], ALU.mult, ALU.add))

            def spread(k, i):
                link = linker(dve, chain, k * GATE_LINKS + 9 + 2 * i)
                dst = (is1, is2)[i]
                link(dve.tensor_tensor(dst[:], w.iota[:].unsqueeze(1).broadcast_to([S, CH, E]),
                                       chosen[:, :, i:i + 1].broadcast_to([S, CH, E]), ALU.is_equal))
                link(dve.tensor_tensor(dst[:], dst[:], (p1, p2)[i][:].unsqueeze(2).broadcast_to([S, CH, E]), ALU.mult))

            def weigh(k, u):
                spread(k, 1)
                dve.tensor_tensor(weight[:, u], is1[:], is2[:], ALU.add).then_inc(weighed, 1)

            def halve(k, e, j):
                n = k * (E * MH) + (MH * e + j)
                dve.wait_ge(tanhed, n + 1)
                if late(n, 2):
                    dve.wait_ge(hid_in, n - 1)
                dve.scalar_tensor_tensor(half[:, j], tanh[:, j], 1.0, h1[j], ALU.add, ALU.mult).then_inc(halved, 1)

            def hide(k, e, j):
                n = k * (E * MH) + (MH * e + j)
                dve.wait_ge(halved, n + 1)
                if late(n, 2 * MH):
                    dve.wait_ge(hid_lo, n - (2 * MH - 1))
                dve.scalar_tensor_tensor(hidden[:, e % 2, j], half[:, j], 1.0 / (WS * WS), h2[j], ALU.mult,
                                         ALU.mult).then_inc(hid_in, 1)

            def combine(k, u, e):
                n = k * E + e
                dve.wait_ge(y_done, n + 1)
                if e == 0:
                    dve.wait_ge(weighed, k + 1)
                if late(n, 2):
                    dve.wait_ge(added, n - 1)
                dve.tensor_tensor(part[:, e % 2], y[e % 2], weight[:, u, :, e:e + 1].broadcast_to([S, CH, D]),
                                  ALU.mult).then_inc(combined, 1)

            def body(k, u):
                between = {3: lambda: sum_gates(k + 1), 4: lambda: largest(k + 1), 5: lambda: which(k + 1),
                           6: lambda: factors(k + 1), 7: lambda: spread(k + 1, 0)}
                for e in range(E):
                    there, *expert = lagged(k, u, e, LAG + 1)
                    if there:
                        combine(*expert)
                    if e == 1 and within(k):
                        stage(k + 1, 1 - u)
                    halve(k, e, 0)
                    hide(k, e, 0)
                    halve(k, e, 1)
                    if e in between and within(k):
                        between[e]()
                    hide(k, e, 1)
                    if e == 7 and within(k):
                        weigh(k + 1, 1 - u)

            stage(0, 0)
            sum_gates(0)
            largest(0)
            which(0)
            factors(0)
            spread(0, 0)
            weigh(0, 0)
            chunks(dve, body)
            for e in range(E - LAG - 1, E):
                combine(NCH - 1, (NCH - 1) % 2, e)


def flamingo(nc, a):
    with ExitStack() as stack:
        def sb(name, shape, dt=FP32):
            return stack.enter_context(nc.sbuf_tensor(name, shape, dt))

        w = Weights()
        bank = [stack.enter_context(nc.psum_tensor(f"bank{i}", [128, 512], FP32)) for i in range(8)]
        w.X = sb("X", [S, B, D])
        w.mv, w.rstd = sb("mv", [S, B, 2]), sb("rstd", [S, B])
        w.rstd_c, w.shift_c = sb("rstd_c", [C, B]), sb("shift_c", [C, B])
        w.ident, w.identh = sb("ident", [128, 128]), sb("identh", [128, 128], FP16)
        w.head_rows = sb("head_rows", [R0, HG])
        w.iota = sb("iota", [128, E])
        w.mask01, w.mask_bias = sb("mask01", [128, B, C], FP16), sb("mask_bias", [C, 1, B])
        w.q0h, w.q0l, w.k0h, w.k0l = (sb(n, [D, G, 3, 32], FP16) for n in ("q0h", "q0l", "k0h", "k0l"))
        w.v0h, w.v0l = sb("v0h", [D, D], FP16), sb("v0l", [D, D], FP16)
        w.o0h, w.o0l = sb("o0h", [D, 1, D], FP16), sb("o0l", [D, 1, D], FP16)
        w.bias0, w.tg0 = sb("bias0", [128, D]), sb("tg0", [128, 1])
        w.taph, w.tapl = sb("taph", [D, 3, M0, 128], FP16), sb("tapl", [D, 3, M0, 128], FP16)
        w.conv_b, w.conv_b_half = sb("conv_b", [128, M0]), sb("conv_b_half", [128, M0])
        w.w2t, w.ffn_out = sb("w2t", [128, M0, D], FP16), sb("ffn_out", [128, 1])
        w.gb = sb("gb", [D, 4])
        w.ah, w.al = sb("ah", [D, H, D], FP16), sb("al", [D, H, D], FP16)
        w.v1h, w.v1l = sb("v1h", [D, H * DK1], FP16), sb("v1l", [D, H * DK1], FP16)
        w.o1h, w.o1l = sb("o1h", [128, H // 2, D], FP16), sb("o1l", [128, H // 2, D], FP16)
        w.gain1, w.bias1 = sb("gain1", [128, D]), sb("bias1", [128, D])
        w.wgt = sb("wgt", [D, 2, E], FP16)
        w.moeh, w.moel = sb("moeh", [D, 2, E * MH, 128], FP16), sb("moel", [D, 2, E * MH, 128], FP16)
        w.w3h, w.w3l = sb("w3h", [128, E * MH, D], FP16), sb("w3l", [128, E * MH, D], FP16)
        w.moe_out = sb("moe_out", [128, 1])

        with ExitStack() as ctx_stack:
            w.ctx = ctx_stack.enter_context(nc.sbuf_tensor("ctx", [C, B, D], FP32))
            setup(nc, a, w, bank)
            with Memory(nc, "layer0") as m:
                qst, kst = m.sb("qst", [R0, G, B, S], FP16), m.sb("kst", [R0, G, B, C], FP16)
                vals = m.sb("vals", [C, B, H, 2, DK0 + 1], FP16)
                with Memory(nc, "rows0") as rows:
                    xh, xl = rows.sb("xh", [D, B, S], FP16), rows.sb("xl", [D, B, S], FP16)
                    ch, cl = rows.sb("ch", [D, B, C], FP16), rows.sb("cl", [D, B, C], FP16)
                    split_transposed(nc, w, bank, "split0", [
                        Split("x", S, w.X, lambda c: xh[:, c, :], lambda c: xl[:, c, :], "vector", w.mv, w.rstd),
                        Split("ctx", C, w.ctx, lambda c: ch[:, c, :], lambda c: cl[:, c, :])], after=context_scale(w))
                    project0(nc, w, bank, xh, xl, ch, cl, qst, kst, vals)
                attention0(nc, w, bank, qst, kst, vals)
            feed_forward0(nc, w, bank)
            with Memory(nc, "layer1") as m:
                kv = m.sb("kv", [D, B, 3, KV], FP16)
                gain_l, bias_l, gain_x, bias_x = (w.gb[:, i:i + 1] for i in range(4))
                jobs = [Split("ctx", C, w.ctx, lambda c: kv[:, c, 0, S:KV], lambda c: kv[:, c, 1, S:KV],
                              "gpsimd", rstd=w.rstd_c, shift=w.shift_c, gain=gain_x, bias=bias_x),
                        Split("x", S, w.X, lambda c: kv[:, c, 0, 0:S], lambda c: kv[:, c, 1, 0:S],
                              "vector", w.mv, w.rstd, gain=gain_l, bias=bias_l)]
                split_transposed(nc, w, bank, "split1", jobs, before=latent_scale(w), after=mask_keys(w, kv, jobs))
                attention1(nc, w, bank, kv)
        with Memory(nc, "moe") as m:
            xh, xl = m.sb("xh", [D, B, S], FP16), m.sb("xl", [D, B, S], FP16)
            split_transposed(nc, w, bank, "split2", [
                Split("x", S, w.X, lambda c: xh[:, c, :], lambda c: xl[:, c, :], "vector", w.mv, w.rstd)], before=row_scale(w))
            mixture(nc, a, w, bank, xh, xl)


_INS = {'x': 'x', 'ctx': 'ctx_1024', 'mask': 'mask_BxS2_bf1', 'gx': 'g_xattn', 'gf': 'g_ffn',
        'q0': 'L0_xattn_W_q', 'k0': 'L0_xattn_W_k', 'v0': 'L0_xattn_W_v', 'o0': 'L0_xattn_W_o', 'bo0': 'L0_xattn_b_o',
        'fw1': 'L0_ffn_w1', 'cw': 'L0_ffn_conv_w', 'cb': 'L0_ffn_conv_b', 'fw2': 'L0_ffn_w2',
        'gx1': 'L1_xattn_g_x', 'bx1': 'L1_xattn_b_x', 'gl1': 'L1_xattn_g_l', 'bl1': 'L1_xattn_b_l',
        'q1': 'L1_xattn_Wq', 'kv1': 'L1_xattn_Wkv', 'o1': 'L1_xattn_Wout', 'go1': 'L1_xattn_g_o', 'bo1': 'L1_xattn_b_o',
        'wg': 'L1_ffn_Wg', 'w1': 'L1_ffn_W1', 'w2': 'L1_ffn_W2', 'w3': 'L1_ffn_W3'}


def kernel(**inputs):
    import numpy as _np
    import concourse.bacc as _bacc
    from concourse import mybir as _mybir
    from concourse.bass_utils import run_bass_kernel_spmd as _run

    nc = _bacc.Bacc("TRN2", target_bir_lowering=False, num_devices=1)
    arrays, aps = {}, {}
    for short, name in _INS.items():
        v = _np.ascontiguousarray(inputs[name])
        if v.dtype == _np.bool_:
            v = v.view(_np.uint8)
        arrays[f"in_{short}"] = v
        aps[short] = nc.dram_tensor(f"in_{short}", v.shape, _mybir.dt.from_np(v.dtype), kind="ExternalInput").ap()
    aps["out"] = nc.dram_tensor("out", (B, S, D), _mybir.dt.float32, kind="ExternalOutput").ap()
    flamingo(nc, aps)
    r = _run(nc, [arrays], core_ids=[0])
    return r.results[0]["out"]
```
